# Optimizing a Trainium2 kernel written in Bass

```python
import numpy as np
import jax
import jax.numpy as jnp

def _softmax(x, axis=-1):
    return jax.nn.softmax(x, axis=axis)

def _gelu(x):
    return jax.nn.gelu(x, approximate=True)

def _silu(x):
    return jax.nn.silu(x)

def _sigmoid(x):
    return jax.nn.sigmoid(x)

def _layernorm(x, axis=-1, eps=1e-05):
    m = jnp.mean(x, axis=axis, keepdims=True)
    v = jnp.var(x, axis=axis, keepdims=True)
    return (x - m) / jnp.sqrt(v + eps)

def _scatter_add(tgt, idx, src, axis=0):
    return tgt.at[idx].add(src)

def _segment_sum(src, seg, n):
    return jax.ops.segment_sum(src, seg, n)
kernel_name = 'mk_decoder_postln_d1_seqx_r4_18d0d2'

def setup_inputs(seed: int=0):
    np.random.seed(seed)
    _w = jnp.asarray

    def _rec_inputs():
        import jax
        import jax.numpy as jnp
        _rk = jax.random.key(seed)
        x = -0.000125 + 0.9999 * jax.random.normal(jax.random.fold_in(_rk, 1), (8, 512, 512), jnp.float32)
        _lenS = 512 - jax.random.randint(jax.random.fold_in(_rk, 7), (8,), 0, max(1, 512 // 4) + 1, jnp.int32)
        _lenS2 = 64 - jax.random.randint(jax.random.fold_in(_rk, 8), (8,), 0, max(1, 64 // 4) + 1, jnp.int32)
        _ctx_2048P = jax.random.normal(jax.random.fold_in(_rk, 11), (8, 16, 512), jnp.float32)
        _ctx_2048c = jax.random.dirichlet(jax.random.fold_in(_rk, 511), 0.3 * jnp.ones((16,), jnp.float32), (8, 64))
        _ctx_2048t = jnp.einsum('bsk,bkd->bsd', _ctx_2048c, _ctx_2048P)
        _ctx_2048t = _ctx_2048t * jax.lax.rsqrt(jnp.mean(jnp.square(_ctx_2048t)) + 1e-12) * 0.953939
        ctx_2048 = -0.000514642 + 1.00011 * (_ctx_2048t + 0.3 * jax.random.normal(jax.random.fold_in(_rk, 611), (8, 64, 512), jnp.float32))
        _validS = jnp.arange(512)[None, :] < _lenS[:, None]
        _validS2 = jnp.arange(64)[None, :] < _lenS2[:, None]
        _causal = jnp.tril(jnp.ones((512, 512), dtype=bool))
        mask_BxS2_bk0 = jnp.logical_not(jnp.broadcast_to(_validS2[:, :], (8, 64)))
        return (x, ctx_2048, mask_BxS2_bk0)
    x, ctx_2048, mask_BxS2_bk0 = _rec_inputs()

    def _L0_attn_setup():
        import jax, jax.numpy as jnp
        import numpy as np
        HIDDEN = 512
        HEAD_DIM = 64
        N_HEADS = HIDDEN // HEAD_DIM
        ROT_DIM = HEAD_DIM // 2
        THETA = 10000.0
        SCALE_BASE = 512.0
        EPS = 1e-05
        B, S = (1, 512)

        def _rotate_half(t):
            x1 = t[..., 0::2]
            x2 = t[..., 1::2]
            return jnp.stack([-x2, x1], axis=-1).reshape(t.shape)

        def _xpos_rotary(q, k, seqlen):
            dim = ROT_DIM
            inv_freq = 1.0 / THETA ** (jnp.arange(0, dim, 2, dtype=jnp.float32) / dim)
            t = jnp.arange(seqlen, dtype=jnp.float32)
            freqs = t[:, None] * inv_freq[None, :]
            freqs = jnp.repeat(freqs, 2, axis=-1)
            base_scale = (jnp.arange(0, dim, 2, dtype=jnp.float32) + 0.4 * dim) / (1.4 * dim)
            power = (t - seqlen // 2) / SCALE_BASE
            scale = base_scale[None, :] ** power[:, None]
            scale = jnp.concatenate([scale, scale], axis=-1)
            cos, sin = (jnp.cos(freqs), jnp.sin(freqs))

            def apply(x, sc):
                xr, xp = (x[..., :dim], x[..., dim:])
                xr = xr * cos * sc + _rotate_half(xr) * sin * sc
                return jnp.concatenate([xr, xp], axis=-1)
            return (apply(q, scale), apply(k, 1.0 / scale))

        def _msr_forward(x, wqkv, wg, wo, gn_weight, gn_bias):
            b, s, _ = x.shape
            qkv = x @ wqkv.T
            qkv = qkv.reshape(b, s, N_HEADS, 3 * HEAD_DIM).transpose(0, 2, 1, 3)
            q, k, v = jnp.split(qkv, 3, axis=-1)
            q, k = _xpos_rotary(q, k, s)
            gamma = 1.0 - 2.0 ** (-5.0 - jnp.arange(N_HEADS, dtype=jnp.float32))
            idx = jnp.arange(s)
            nm = idx[:, None] - idx[None, :]
            decay = jnp.where(nm >= 0, gamma[:, None, None] ** jnp.maximum(nm, 0).astype(jnp.float32), 0.0)
            scores = jnp.einsum('bhid,bhjd->bhij', q, k) * decay
            ret = jnp.einsum('bhij,bhjd->bhid', scores, v)
            mean = ret.mean(axis=(2, 3), keepdims=True)
            var = ret.var(axis=(2, 3), keepdims=True)
            ret = (ret - mean) / jnp.sqrt(var + EPS)
            ret = ret * gn_weight[None, :, None, None] + gn_bias[None, :, None, None]
            y = ret.transpose(0, 2, 1, 3).reshape(b, s, HIDDEN)
            g = x @ wg.T
            mish = g * jnp.tanh(jax.nn.softplus(g))
            return mish * y @ wo.T
        key = jax.random.key(seed)
        ks = jax.random.split(key, 4)
        std = HIDDEN ** (-0.5)
        x = jax.random.normal(ks[0], (B, S, HIDDEN), jnp.float32)
        wqkv = jax.random.normal(ks[1], (3 * HIDDEN, HIDDEN), jnp.float32) * std
        wg = jax.random.normal(ks[2], (HIDDEN, HIDDEN), jnp.float32) * std
        wo = jax.random.normal(ks[3], (HIDDEN, HIDDEN), jnp.float32) * std
        gn_weight = jnp.ones((N_HEADS,), jnp.float32)
        gn_bias = jnp.zeros((N_HEADS,), jnp.float32)
        return {'x': x, 'wqkv': wqkv, 'wg': wg, 'wo': wo, 'gn_weight': gn_weight, 'gn_bias': gn_bias}
    _L0_attn_all = _L0_attn_setup()
    _L0_attn_in = {k: v for k, v in _L0_attn_all.items() if k in ('wqkv', 'wg', 'wo', 'gn_weight', 'gn_bias')}
    del _L0_attn_all

    def _L0_xattn_setup():
        import jax, jax.numpy as jnp
        import numpy as np
        key = jax.random.key(seed)
        k1, k2, k3 = jax.random.split(key, 3)
        B, S, D, M = (8, 512, 512, 128)
        hidden_states = jax.random.normal(k1, (B, S, D), dtype=jnp.float32)
        memory_tokens = jax.random.normal(k2, (B, M, D), dtype=jnp.float32)
        memory_mask = jax.random.randint(k3, (B, M), 0, 2).astype(jnp.bool_)
        return {'hidden_states': hidden_states, 'memory_tokens': memory_tokens, 'memory_mask': memory_mask}
    _L0_xattn_all = _L0_xattn_setup()
    _L0_xattn_in = {k: v for k, v in _L0_xattn_all.items() if k in ()}
    del _L0_xattn_all

    def _L0_ffn_setup():
        import jax, jax.numpy as jnp
        import numpy as np
        BLOCK = 64

        def dequant4bit(q, scale):
            return (q.astype(jnp.float32) - 7.5) * jnp.repeat(scale, BLOCK, axis=1)
        key = jax.random.key(seed)
        ks = jax.random.split(key, 11)
        B, S, D, H, R = (4, 512, 512, 2048, 16)
        return {'x1': jax.random.normal(ks[0], (B, S, D), jnp.float32), 'w_up_q': jax.random.randint(ks[1], (H, D), 0, 16, dtype=jnp.int32), 'w_up_scale': jax.random.uniform(ks[2], (H, D // BLOCK), jnp.float32) * 0.02, 'b_up': jax.random.normal(ks[3], (H,), jnp.float32) * 0.01, 'w_up_lora_a': jax.random.normal(ks[4], (D, R), jnp.float32) * 0.02, 'w_up_lora_b': jax.random.normal(ks[5], (R, H), jnp.float32) * 0.02, 'w_down_q': jax.random.randint(ks[6], (D, H), 0, 16, dtype=jnp.int32), 'w_down_scale': jax.random.uniform(ks[7], (D, H // BLOCK), jnp.float32) * 0.02, 'b_down': jax.random.normal(ks[8], (D,), jnp.float32) * 0.01, 'w_down_lora_a': jax.random.normal(ks[9], (H, R), jnp.float32) * 0.02, 'w_down_lora_b': jax.random.normal(ks[10], (R, D), jnp.float32) * 0.02}
    _L0_ffn_all = _L0_ffn_setup()
    _L0_ffn_in = {k: v for k, v in _L0_ffn_all.items() if k in ('w_up_q', 'w_up_scale', 'b_up', 'w_up_lora_a', 'w_up_lora_b', 'w_down_q', 'w_down_scale', 'b_down', 'w_down_lora_a', 'w_down_lora_b')}
    del _L0_ffn_all
    return {'x': x, 'ctx_2048': ctx_2048, 'mask_BxS2_bk0': mask_BxS2_bk0, 'L0_attn_wqkv': _L0_attn_in['wqkv'], 'L0_attn_wg': _L0_attn_in['wg'], 'L0_attn_wo': _L0_attn_in['wo'], 'L0_attn_gn_weight': _L0_attn_in['gn_weight'], 'L0_attn_gn_bias': _L0_attn_in['gn_bias'], 'L0_ffn_w_up_q': _L0_ffn_in['w_up_q'], 'L0_ffn_w_up_scale': _L0_ffn_in['w_up_scale'], 'L0_ffn_b_up': _L0_ffn_in['b_up'], 'L0_ffn_w_up_lora_a': _L0_ffn_in['w_up_lora_a'], 'L0_ffn_w_up_lora_b': _L0_ffn_in['w_up_lora_b'], 'L0_ffn_w_down_q': _L0_ffn_in['w_down_q'], 'L0_ffn_w_down_scale': _L0_ffn_in['w_down_scale'], 'L0_ffn_b_down': _L0_ffn_in['b_down'], 'L0_ffn_w_down_lora_a': _L0_ffn_in['w_down_lora_a'], 'L0_ffn_w_down_lora_b': _L0_ffn_in['w_down_lora_b']}

def reference(x, ctx_2048, mask_BxS2_bk0, L0_attn_wqkv, L0_attn_wg, L0_attn_wo, L0_attn_gn_weight, L0_attn_gn_bias, L0_ffn_w_up_q, L0_ffn_w_up_scale, L0_ffn_b_up, L0_ffn_w_up_lora_a, L0_ffn_w_up_lora_b, L0_ffn_w_down_q, L0_ffn_w_down_scale, L0_ffn_b_down, L0_ffn_w_down_lora_a, L0_ffn_w_down_lora_b):
    import jax
    import jax.numpy as jnp

    def _L0_attn_ref(x, wqkv, wg, wo, gn_weight, gn_bias):
        import jax, jax.numpy as jnp
        import numpy as np
        HIDDEN = 512
        HEAD_DIM = 64
        N_HEADS = HIDDEN // HEAD_DIM
        ROT_DIM = HEAD_DIM // 2
        THETA = 10000.0
        SCALE_BASE = 512.0
        EPS = 1e-05
        B, S = (1, 512)

        def _rotate_half(t):
            x1 = t[..., 0::2]
            x2 = t[..., 1::2]
            return jnp.stack([-x2, x1], axis=-1).reshape(t.shape)

        def _xpos_rotary(q, k, seqlen):
            dim = ROT_DIM
            inv_freq = 1.0 / THETA ** (jnp.arange(0, dim, 2, dtype=jnp.float32) / dim)
            t = jnp.arange(seqlen, dtype=jnp.float32)
            freqs = t[:, None] * inv_freq[None, :]
            freqs = jnp.repeat(freqs, 2, axis=-1)
            base_scale = (jnp.arange(0, dim, 2, dtype=jnp.float32) + 0.4 * dim) / (1.4 * dim)
            power = (t - seqlen // 2) / SCALE_BASE
            scale = base_scale[None, :] ** power[:, None]
            scale = jnp.concatenate([scale, scale], axis=-1)
            cos, sin = (jnp.cos(freqs), jnp.sin(freqs))

            def apply(x, sc):
                xr, xp = (x[..., :dim], x[..., dim:])
                xr = xr * cos * sc + _rotate_half(xr) * sin * sc
                return jnp.concatenate([xr, xp], axis=-1)
            return (apply(q, scale), apply(k, 1.0 / scale))

        def _msr_forward(x, wqkv, wg, wo, gn_weight, gn_bias):
            b, s, _ = x.shape
            qkv = x @ wqkv.T
            qkv = qkv.reshape(b, s, N_HEADS, 3 * HEAD_DIM).transpose(0, 2, 1, 3)
            q, k, v = jnp.split(qkv, 3, axis=-1)
            q, k = _xpos_rotary(q, k, s)
            gamma = 1.0 - 2.0 ** (-5.0 - jnp.arange(N_HEADS, dtype=jnp.float32))
            idx = jnp.arange(s)
            nm = idx[:, None] - idx[None, :]
            decay = jnp.where(nm >= 0, gamma[:, None, None] ** jnp.maximum(nm, 0).astype(jnp.float32), 0.0)
            scores = jnp.einsum('bhid,bhjd->bhij', q, k) * decay
            ret = jnp.einsum('bhij,bhjd->bhid', scores, v)
            mean = ret.mean(axis=(2, 3), keepdims=True)
            var = ret.var(axis=(2, 3), keepdims=True)
            ret = (ret - mean) / jnp.sqrt(var + EPS)
            ret = ret * gn_weight[None, :, None, None] + gn_bias[None, :, None, None]
            y = ret.transpose(0, 2, 1, 3).reshape(b, s, HIDDEN)
            g = x @ wg.T
            mish = g * jnp.tanh(jax.nn.softplus(g))
            return mish * y @ wo.T
        return _msr_forward(x, wqkv, wg, wo, gn_weight, gn_bias)

    def _L0_xattn_ref(hidden_states, memory_tokens, memory_mask):
        import jax, jax.numpy as jnp
        import numpy as np
        B, S, D = hidden_states.shape
        scale = 1.0 / jnp.sqrt(jnp.asarray(D, hidden_states.dtype))
        scores = jnp.einsum('bsd,bmd->bsm', hidden_states, memory_tokens) * scale
        neg_inf = jnp.asarray(-1e+30, scores.dtype)
        scores = jnp.where(memory_mask[:, None, :], scores, neg_inf)
        attn = jax.nn.softmax(scores, axis=-1)
        readout = jnp.einsum('bsm,bmd->bsd', attn, memory_tokens)
        valid_b = jnp.any(memory_mask, axis=-1)
        out = jnp.where(valid_b[:, None, None], readout, jnp.zeros_like(readout))
        return out

    def _L0_ffn_ref(x1, w_up_q, w_up_scale, b_up, w_up_lora_a, w_up_lora_b, w_down_q, w_down_scale, b_down, w_down_lora_a, w_down_lora_b):
        import jax, jax.numpy as jnp
        import numpy as np
        BLOCK = 64

        def dequant4bit(q, scale):
            return (q.astype(jnp.float32) - 7.5) * jnp.repeat(scale, BLOCK, axis=1)
        w_up = dequant4bit(w_up_q, w_up_scale).T
        y1 = x1 @ w_up + b_up + x1 @ w_up_lora_a @ w_up_lora_b
        x2 = jax.nn.relu(y1)
        w_down = dequant4bit(w_down_q, w_down_scale).T
        y2 = x2 @ w_down + b_down + x2 @ w_down_lora_a @ w_down_lora_b
        return y2
    x = _layernorm(x + _L0_attn_ref(x, L0_attn_wqkv, L0_attn_wg, L0_attn_wo, L0_attn_gn_weight, L0_attn_gn_bias), axis=-1)
    x = _layernorm(x + _L0_xattn_ref(x, ctx_2048, mask_BxS2_bk0), axis=-1)
    x = _layernorm(x + _L0_ffn_ref(x, L0_ffn_w_up_q, L0_ffn_w_up_scale, L0_ffn_b_up, L0_ffn_w_up_lora_a, L0_ffn_w_up_lora_b, L0_ffn_w_down_q, L0_ffn_w_down_scale, L0_ffn_b_down, L0_ffn_w_down_lora_a, L0_ffn_w_down_lora_b), axis=-1)
    return x

_drawn_inputs = setup_inputs


def setup_inputs(seed=0):
    import zlib

    import numpy as np

    out = dict(_drawn_inputs(seed))
    spreads = {'L0_attn_gn_weight': (1.0, 0.2), 'L0_attn_gn_bias': (0.0, 0.1)}
    factors = {'L0_ffn_b_up': 7.663, 'L0_ffn_b_down': 8.0}
    for name, (base, spread) in spreads.items():
        noise = np.random.default_rng([zlib.crc32(name.encode()), seed]).standard_normal(out[name].shape)
        drawn = base * np.exp(spread * noise) if base else spread * noise
        out[name] = jnp.asarray(drawn.astype(out[name].dtype))
    for name, factor in factors.items():
        out[name] = (out[name] * factor).astype(out[name].dtype)
    return out
```

```python
import numpy as np
import concourse.bass as bass
from concourse import mybir
from contextlib import ExitStack

F32 = mybir.dt.float32
F32R = mybir.dt.float32r
I32 = mybir.dt.int32
U8 = mybir.dt.uint8
ALU = mybir.AluOpType
ACT = mybir.ActivationFunctionType
AX = mybir.AxisListType

B, S, D = 8, 512, 512
P = 128
NH, HD, ROT = 8, 64, 32
NC = S // P
NK = D // P
NP = NH // 2
M = 64
FF = 2048
NF = FF // P
QB = 64
R = 16
EPS = 1e-5
NEG = 1e30

PASS_PROJ = [("V", 0), ("Tq", 0), ("V", 1), ("Tk", 0), ("V", 2), ("Tq", 1), ("V", 3), ("Tk", 1),
             ("G", 0), ("Tq", 2), ("G", 1), ("Tk", 2), ("G", 2), ("Tq", 3), ("G", 3), ("Tk", 3)]
PASS_BOTH = ([("ST", 0), ("ST", 1), ("ST", 2), ("V", 0), ("ST", 3)] + PASS_PROJ[1:])
PASS_RET = [("ST", p) for p in range(NP)]


def pass_order(ret, proj):
    return PASS_BOTH if ret and proj else PASS_PROJ if proj else PASS_RET


def pass_base(b):
    return 0 if isinstance(b, int) and b < 0 else b * len(PASS_BOTH) + len(PASS_PROJ)


def tables():
    f = np.float32
    inv = (f(1.0) / (f(10000.0) ** (np.arange(0, ROT, 2, dtype=f) / f(ROT)))).astype(f)
    t = np.arange(S, dtype=f)
    ang = (t[:, None] * inv[None, :]).astype(f)
    ang = np.repeat(ang, 2, axis=-1).astype(np.float64)
    base = ((np.arange(0, ROT, 2, dtype=f) + f(0.4 * ROT)) / f(1.4 * ROT)).astype(np.float64)
    power = ((t - S // 2) / f(512.0)).astype(np.float64)
    sc = base[None, :] ** power[:, None]
    sc = np.concatenate([sc, sc], axis=-1)
    sign = np.tile([-1.0, 1.0], ROT // 2)
    rot = np.zeros((S, 2, 2, ROT))
    for n, s_ in enumerate((sc, 1.0 / sc)):
        rot[:, 0, n] = np.cos(ang) * s_
        rot[:, 1, n] = np.sin(ang) * s_ * sign
    gamma = 1.0 - 2.0 ** (-5.0 - np.arange(NH))
    dist = np.arange(S) - S // 2
    dec = np.stack([gamma[None] ** dist[:, None], gamma[None] ** -dist[:, None]], axis=1)
    tab = np.concatenate([rot.reshape(S, -1), dec.reshape(S, -1)], axis=1)
    tab = tab.reshape(NC, P, -1).transpose(1, 0, 2)
    j, i = np.arange(P)[:, None], np.arange(P)[None, :]
    causal = (j <= i).astype(f)
    heads = np.where((j // HD) == (i // HD), 1.0 / HD, 0.0).astype(f)
    sel_up = np.zeros((2 * NK, NK, P), f)
    for k in range(NK):
        for q in range(P):
            sel_up[2 * k + q // QB, k, q] = 1.0
    sel_dn = np.zeros((2 * NF, NF, P), f)
    for k in range(NF):
        for q in range(P):
            sel_dn[2 * k + q // QB, k, q] = 1.0
    return (np.ascontiguousarray(tab.astype(f)), np.concatenate([causal, heads, np.eye(P, dtype=f)], axis=1),
            sel_up, sel_dn)


def wait(eng, sem, value):
    if isinstance(value, int) and value <= 0:
        return
    eng.wait_ge(sem, value)


class Links:

    def __init__(self, eng, sem, base):
        self.eng, self.sem, self.base, self.n = eng, sem, base, 0

    def __call__(self, ins):
        ins.then_inc(self.sem, 1)
        self.n += 1
        self.eng.wait_ge(self.sem, self.base + self.n)


def decoder_kernel(nc, xT, x, ctxT, ctx_in, mask, wqkT, wvgT, woT, gnw, gnb, qup, sup, bup, aup, bupl,
                   qdn, sdn, bdn, adn, bdnl, tab, consts, selup, seldn, out, x1s):
    retention_phase(nc, xT, x, wqkT, wvgT, woT, gnw, gnb, tab, consts, x1s)
    ffn_phase(nc, ctxT, ctx_in, mask, qup, sup, bup, aup, bupl, qdn, sdn, bdn, adn, bdnl, consts,
              selup, seldn, x1s, out)


def retention_phase(nc, xT, x, wqkT, wvgT, woT, gnw, gnb, tab, consts, x1s):
    with ExitStack() as stack:
        def sb(name, shape, dt=F32):
            return stack.enter_context(nc.sbuf_tensor(name, shape, dt))

        def pb(name, shape):
            return stack.enter_context(nc.psum_tensor(name, shape, F32))

        def sem(name):
            return stack.enter_context(nc.semaphore(name))

        wqk_h, wqk_l = sb("wqk_h", [P, NK, 2 * D], F32R), sb("wqk_l", [P, NK, 2 * D], F32R)
        wvg_h, wvg_l = sb("wvg_h", [P, NK, 2 * D], F32R), sb("wvg_l", [P, NK, 2 * D], F32R)
        wo_h, wo_l = sb("wo_h", [P, NK, D], F32R), sb("wo_l", [P, NK, D], F32R)
        x_raw = sb("x_raw", [P, NK, S])
        x_h, x_l = sb("x_h", [P, NK, S], F32R), sb("x_l", [P, NK, S], F32R)
        x_tok = sb("x_tok", [P, NC, D])
        qk_tok = sb("qk_tok", [P, NC, 2, NH, HD])
        v_tok = sb("v_tok", [P, NC, D])
        q_T, k_T = sb("q_T", [P, NP, S]), sb("k_T", [P, NP, S])
        sc_T = sb("sc_T", [P, 4, NC, P])
        state = sb("state", [P, NC - 1, NP, P])
        gate = sb("gate", [P, NP, S])
        y_h, y_l = sb("y_h", [P, NP, S], F32R), sb("y_l", [P, NP, S], F32R)
        y_t = sb("y_t", [P, 2, S])
        gate_t = sb("gate_t", [P, S])
        rot_a, rot_b = sb("rot_a", [P, 2, NH, ROT]), sb("rot_b", [P, 2, NH, ROT])
        tab_s = sb("tab_s", [P, NC, 4 * ROT + 2 * NH])
        cst = sb("cst", [P, 3 * P])
        gn_s = sb("gn_s", [P, 2, NP])
        half = sb("half", [P, NC])
        pad = sb("pad", [P, 1])
        bn6 = sb("bn6", [P, NC, 6])
        mv = sb("mv", [P, 2])
        hm = sb("hm", [P, 2])
        ab = sb("ab", [P, 4])
        ab_b = sb("ab_b", [P, 1])
        ln_mv, ln_ve, ln_rs = sb("ln_mv", [P, NC, 2]), sb("ln_ve", [P, NC]), sb("ln_rs", [P, NC])

        causal, heads, ident = cst[:, 0:P], cst[:, P:2 * P], cst[:, 2 * P:3 * P]
        acc = pb("acc", [P, 2, 512])
        pas = [pb(f"pas{i}", [P, 512]) for i in range(2)]
        psc = [pb(f"psc{i}", [P, NC, P]) for i in range(2)]
        pret = [pb(f"pret{i}", [P, 512]) for i in range(2)]

        wqk_in, wvg_in, wo_in = sem("wqk_in"), sem("wvg_in"), sem("wo_in")
        const_in, x_in, xtok_in, x1_out = sem("const_in"), sem("x_in"), sem("xtok_in"), sem("x1_out")
        w_hi, w_lo = sem("w_hi"), sem("w_lo")
        xs_hi, xs_lo = sem("xs_hi"), sem("xs_lo")
        init = sem("init")
        qk_done, v_done, g_done, t_done, s_done = map(sem, ("qk_done", "v_done", "g_done", "t_done", "s_done"))
        sc_done, r_done, st_done, o_done = map(sem, ("sc_done", "r_done", "st_done", "o_done"))
        qk_read, rot_done, pas_read, s_read, sc_read = map(sem, ("qk_read", "rot_done", "pas_read", "s_read", "sc_read"))
        sq_done, gate_done = sem("sq_done"), sem("gate_done")
        bn_done, ve_done, rs_done, ab_done, aff_done, y_done = map(
            sem, ("bn_done", "ve_done", "rs_done", "ab_done", "aff_done", "y_done"))
        o_read, lnve_done, lnrs_done, x1_done = map(sem, ("o_read", "lnve_done", "lnrs_done", "x1_done"))
        act_link, dve_link, pool_link = sem("act_link"), sem("dve_link"), sem("pool_link")

        def run(eng, part):
            part(-1, False, True, True)
            with eng.Fori(0, B - 2) as b:
                part(b, True, True, True)
            part(B - 2, True, True, False)
            part(B - 1, True, False, False)

        block = stack.enter_context(nc.Block())

        @block.sync
        def _(sp):
            sp.dma_start(qk_tok[:, :, :, :, :].rearrange("p c a h d -> p c (a h d)"),
                         wqkT.rearrange("(k p) n -> p k n", p=P)).then_inc(wqk_in, 16)
            sp.dma_start(x_raw[:, :, :], xT[0].rearrange("(k p) t -> p k t", p=P)).then_inc(x_in, 16)
            sp.dma_start(tab_s[:, :, :], tab).then_inc(const_in, 16)
            sp.dma_start(cst[:, :], consts).then_inc(const_in, 16)
            for e in range(2):
                for n, g in enumerate((gnw, gnb)):
                    src = g[e:e + 1, :].to_broadcast([HD, NP])
                    sp.dma_start(gn_s[e * HD:(e + 1) * HD, n, :], src).then_inc(const_in, 16)
            sp.dma_start(gate[:, :, :], wvgT.rearrange("(k p) n -> p k n", p=P)[:, :, 0:D]).then_inc(wvg_in, 16)
            sp.dma_start(v_tok[:, :, :], wvgT.rearrange("(k p) n -> p k n", p=P)[:, :, D:2 * D]).then_inc(wvg_in, 16)
            sp.dma_start(sc_T[:, :, :, :].rearrange("p a c q -> p a (c q)"),
                         woT.rearrange("(k p) n -> p k n", p=P)).then_inc(wo_in, 16)

            def part(b, ret, proj, more):
                if more:
                    sp.wait_ge(xs_hi, b + 2)
                    sp.wait_ge(xs_lo, b + 2)
                    sp.dma_start(x_raw[:, :, :], xT[b + 2].rearrange("(k p) t -> p k t", p=P)).then_inc(x_in, 16)
                if ret:
                    sp.wait_ge(x1_done, b + 1)
                    sp.dma_start(x1s[b].rearrange("(c p) n -> p c n", p=P), x_tok[:, :, :]).then_inc(x1_out, 16)
                    sp.wait_ge(x1_out, 16 * (b + 1))
                if proj:
                    sp.dma_start(x_tok[:, :, :], x[b + 1].rearrange("(c p) n -> p c n", p=P)).then_inc(xtok_in, 16)
            run(sp, part)

        @block.tensor
        def _(pe):
            def split3(dst, lh, ll, rh, rl, first, last):
                nc.tensor.matmul(dst, lh, rh, start=first, stop=False)
                nc.tensor.matmul(dst, ll, rh, start=False, stop=False)
                return nc.tensor.matmul(dst, lh, rl, start=False, stop=last)

            def project_qk(b, c):
                if c == 0:
                    pe.wait_ge(xs_hi, b + 1)
                    pe.wait_ge(xs_lo, b + 1)
                    wait(pe, s_read, (NC - 1) * b)
                    if isinstance(b, int) and b == 0:
                        pe.wait_ge(w_hi, 1)
                        pe.wait_ge(w_lo, 1)
                else:
                    pe.wait_ge(qk_read, NC * b + c)
                ts = slice(c * P, (c + 1) * P)
                for n in range(2):
                    for k in range(NK):
                        cols = slice(n * D, (n + 1) * D)
                        last = split3(acc[:, n, :], x_h[:, k, ts], x_l[:, k, ts], wqk_h[:, k, cols],
                                      wqk_l[:, k, cols], k == 0, k == NK - 1)
                last.then_inc(qk_done, 1)

            def pass_bank(b, ret, proj, item):
                n = pass_order(ret, proj).index(item)
                wait(pe, pas_read, pass_base(b) + n - 1)
                return pas[n % 2]

            def project_v(b, c, bank):
                if isinstance(b, int) and b == 0 and c == 0:
                    pe.wait_ge(w_hi, 2)
                    pe.wait_ge(w_lo, 2)
                ts = slice(c * P, (c + 1) * P)
                for k in range(NK):
                    last = split3(bank[:, :], x_h[:, k, ts], x_l[:, k, ts], wvg_h[:, k, 0:D],
                                  wvg_l[:, k, 0:D], k == 0, k == NK - 1)
                last.then_inc(v_done, 1)

            def project_gate(b, p, bank):
                cols = slice(D + p * P, D + (p + 1) * P)
                for k in range(NK):
                    last = split3(bank[:, :], wvg_h[:, k, cols], wvg_l[:, k, cols], x_h[:, k, :],
                                  x_l[:, k, :], k == 0, k == NK - 1)
                last.then_inc(g_done, 1)

            def transpose_qk(b, p, which, bank):
                if p == 0 and which == 0:
                    pe.wait_ge(rot_done, NC * (b + 1))
                    pe.wait_ge(qk_read, NC * (b + 1))
                    if isinstance(b, int) and b == 0:
                        pe.wait_ge(const_in, 16 * 6)
                for c in range(NC):
                    src = qk_tok[:, c, which, 2 * p:2 * p + 2, :].rearrange("p h d -> p (h d)")
                    last = nc.tensor.transpose(bank[:, c * P:(c + 1) * P], src, ident)
                last.then_inc(t_done, 1)

            def chunk_state(b, c, ret, v3):
                if c == 0:
                    pe.wait_ge(pas_read, v3)
                if c == 1:
                    pe.wait_ge(s_read, (NC - 1) * b + 1)
                if c == 2 and ret:
                    pe.wait_ge(o_read, NC * (b - 1) + 3)
                dst = acc[:, (1, 1, 0)[c], :]
                for p in range(NP):
                    cols = slice(p * P, (p + 1) * P)
                    last = nc.tensor.matmul(dst[:, cols],
                                            qk_tok[:, c, 1, 2 * p:2 * p + 2, :].rearrange("p h d -> p (h d)"),
                                            v_tok[:, c, cols], start=True, stop=True)
                last.then_inc(s_done, 1)

            def scores(b, h):
                p, e = h // 2, h % 2
                if h == 0:
                    pe.wait_ge(pas_read, pass_base(b))
                if h >= 2:
                    pe.wait_ge(sc_read, NH * b + h - 1)
                rows = slice(e * HD, (e + 1) * HD)
                for c in range(NC):
                    ts = slice(c * P, (c + 1) * P)
                    last = nc.tensor.matmul(psc[e][:, c, :], k_T[rows, p, ts], q_T[rows, p, ts],
                                            start=True, stop=True)
                last.then_inc(sc_done, 1)

            def retention(b, p):
                pe.wait_ge(sc_read, NH * b + 2 * p + 2)
                if p == 0:
                    pe.wait_ge(s_read, (NC - 1) * (b + 1))
                if p >= 2:
                    pe.wait_ge(aff_done, NP * b + p - 1)
                bank = pret[p % 2]
                for c in range(NC):
                    ts = slice(c * P, (c + 1) * P)
                    if c:
                        nc.tensor.matmul(bank[:, ts], state[:, c - 1, p, :], q_T[:, p, ts],
                                         start=True, stop=False, skip_group_check=True)
                    for e in range(2):
                        rows = slice(e * HD, (e + 1) * HD)
                        h = 2 * p + e
                        last = nc.tensor.matmul(bank[rows, ts], v_tok[:, c, h * HD:(h + 1) * HD],
                                                sc_T[:, h % 4, c, :], start=(c == 0), stop=True,
                                                skip_group_check=True)
                last.then_inc(r_done, 1)

            def head_stats(b, p, bank):
                pe.wait_ge(bn_done, NP * b + p + 1)
                nc.tensor.matmul(bank[:, 0:2], heads, mv[:, :], start=True, stop=True).then_inc(st_done, 1)

            def project_out(b, c, proj):
                if c == 0:
                    pe.wait_ge(y_done, NP * (b + 1))
                    if isinstance(b, int) and b < 0:
                        pass
                    pe.wait_ge(w_lo, 3)
                    pe.wait_ge(w_hi, 3)
                    if proj:
                        pe.wait_ge(qk_read, NC * (b + 2))
                elif c < 3:
                    pe.wait_ge(o_read, NC * b + c)
                elif proj:
                    pe.wait_ge(s_read, (NC - 1) * (b + 1) + 2)
                else:
                    pe.wait_ge(o_read, NC * b + 2)
                ts = slice(c * P, (c + 1) * P)
                dst = acc[:, (0, 0, 0, 1)[c], :]
                for p in range(NP):
                    last = split3(dst, y_h[:, p, ts], y_l[:, p, ts], wo_h[:, p, :], wo_l[:, p, :],
                                  p == 0, p == NP - 1)
                last.then_inc(o_done, 1)

            def part(b, ret, proj, more):
                for p in range(NP):
                    if ret:
                        scores(b, 2 * p)
                        scores(b, 2 * p + 1)
                        if p:
                            head_stats(b, p - 1, pass_bank(b, ret, proj, ("ST", p - 1)))
                    if proj:
                        project_qk(b + 1, p)
                    if ret:
                        retention(b, p)
                for item in pass_order(ret, proj)[NP - 1 if ret else 0:]:
                    bank = pass_bank(b, ret, proj, item)
                    what, n = item
                    if what == "ST":
                        head_stats(b, n, bank)
                    elif what == "V":
                        project_v(b + 1, n, bank)
                    elif what == "G":
                        project_gate(b + 1, n, bank)
                    else:
                        transpose_qk(b + 1, n, int(what == "Tk"), bank)
                v3 = pass_base(b) + pass_order(ret, proj).index(("V", 3)) + 1 if proj else 0
                for c, s in ((0, 0), (1, 1), (2, None), (3, 2)):
                    if ret:
                        project_out(b, c, proj)
                    if proj and s is not None:
                        chunk_state(b + 1, s, ret, v3)
            run(pe, part)

        @block.scalar
        def _(act):
            act.wait_ge(wqk_in, 16)
            nc.scalar.activation(wqk_h[:, :, :].rearrange("p k n -> p (k n)"),
                                 qk_tok[:, :, :, :, :].rearrange("p c a h d -> p (c a h d)"), ACT.Copy).then_inc(w_hi, 1)
            act.wait_ge(x_in, 16)
            nc.scalar.activation(x_h[:, :, :], x_raw[:, :, :], ACT.Copy).then_inc(xs_hi, 1)
            act.wait_ge(wvg_in, 32)
            nc.scalar.activation(wvg_h[:, :, 0:D], gate[:, :, :], ACT.Copy)
            nc.scalar.activation(wvg_h[:, :, D:2 * D], v_tok[:, :, :], ACT.Copy).then_inc(w_hi, 1)
            act.wait_ge(wo_in, 16)
            nc.scalar.activation(wo_h[:, :, :], sc_T[:, :, :, :].rearrange("p a c q -> p a (c q)"),
                                 ACT.Copy).then_inc(w_hi, 1)
            act.wait_ge(w_lo, 3)

            def norm_pair(b, p):
                act.wait_ge(ab_done, NP * b + p + 1)
                if p >= 2:
                    act.wait_ge(y_done, NP * b + p - 1)
                nc.scalar.activation(y_t[:, p % 2, :], pret[p % 2][:, :], ACT.Identity, bias=ab_b[:, 0:1],
                                     scale=ab[:, 2:3]).then_inc(aff_done, 1)

            def read_stats(b, p, bank):
                act.wait_ge(st_done, NP * b + p + 1)
                nc.scalar.activation(hm[:, :], bank[:, 0:2], ACT.Copy).then_inc(pas_read, 1)

            def part(b, ret, proj, more):
                order = pass_order(ret, proj)
                if ret:
                    for p in range(NP - 1):
                        read_stats(b, p, pas[order.index(("ST", p)) % 2])
                        norm_pair(b, p)
                for n, (what, i) in enumerate(order):
                    bank = pas[n % 2]
                    if n < NP - 1 and ret:
                        continue
                    if what == "ST":
                        read_stats(b, i, bank)
                    elif what == "V":
                        act.wait_ge(v_done, NC * (b + 1) + i + 1)
                        nc.scalar.activation(v_tok[:, i, :], bank[:, :], ACT.Copy).then_inc(pas_read, 1)
                    elif what == "G":
                        act.wait_ge(g_done, NP * (b + 1) + i + 1)
                        wait(act, gate_done, NP * (b + 1) + i)
                        nc.scalar.activation(gate_t[:, :], bank[:, :], ACT.Tanh, scale=0.5).then_inc(act_link, 1)
                        nc.scalar.activation(gate[:, i, :], bank[:, :], ACT.Copy).then_inc(pas_read, 1)
                        act.wait_ge(act_link, NP * (b + 1) + i + 1)
                        nc.scalar.activation(gate_t[:, :], gate_t[:, :], ACT.Square, bias=1.0,
                                             scale=-1.0).then_inc(sq_done, 1)
                    else:
                        dst = q_T if what == "Tq" else k_T
                        act.wait_ge(t_done, 2 * NP * (b + 1) + 2 * i + int(what == "Tk") + 1)
                        nc.scalar.activation(dst[:, i, :], bank[:, :], ACT.Copy).then_inc(pas_read, 1)
                    if ret and (what, i) == (("V", 2) if proj else ("ST", 3)):
                        norm_pair(b, NP - 1)
                if more:
                    act.wait_ge(x_in, 16 * (b + 3))
                    act.wait_ge(g_done, NP * (b + 2))
                    nc.scalar.activation(x_h[:, :, :], x_raw[:, :, :], ACT.Copy).then_inc(xs_hi, 1)
            run(act, part)

        @block.vector
        def _(dve):
            def sub(dst, a, hi):
                return nc.vector.tensor_tensor(dst, a, hi.bitcast(F32), ALU.subtract)

            nc.vector.memset(half[:, :], -0.5).then_inc(init, 1)
            nc.vector.memset(state[:, :, :, :], 0.0).then_inc(dve_link, 1)
            dve.wait_ge(w_hi, 1)
            sub(wqk_l[:, :, :].rearrange("p k n -> p (k n)"),
                qk_tok[:, :, :, :, :].rearrange("p c a h d -> p (c a h d)"),
                wqk_h[:, :, :].rearrange("p k n -> p (k n)")).then_inc(w_lo, 1)
            dve.wait_ge(xs_hi, 1)
            sub(x_l[:, :, :], x_raw[:, :, :], x_h[:, :, :]).then_inc(xs_lo, 1)
            dve.wait_ge(w_hi, 2)
            sub(wvg_l[:, :, 0:D], gate[:, :, :], wvg_h[:, :, 0:D])
            sub(wvg_l[:, :, D:2 * D], v_tok[:, :, :], wvg_h[:, :, D:2 * D]).then_inc(w_lo, 1)
            dve.wait_ge(w_hi, 3)
            sub(wo_l[:, :, :], sc_T[:, :, :, :].rearrange("p a c q -> p a (c q)"), wo_h[:, :, :]).then_inc(w_lo, 1)
            dve.wait_ge(const_in, 16 * 6)
            dve.wait_ge(dve_link, 1)

            cos, sin = tab_s[:, :, 0:2 * ROT], tab_s[:, :, 2 * ROT:4 * ROT]
            dec = tab_s[:, :, 4 * ROT:4 * ROT + 2 * NH]
            base = [1]

            def mask_scores(b, h):
                dve.wait_ge(sc_done, NH * b + h + 1)
                if h >= 4:
                    dve.wait_ge(r_done, NP * b + (h - 4) // 2 + 1)
                nc.vector.tensor_tensor(sc_T[:, h % 4, :, :], psc[h % 2][:, :, :],
                                        causal.unsqueeze(1).to_broadcast([P, NC, P]), ALU.mult).then_inc(sc_read, 1)

            def rotate(b, c):
                dve.wait_ge(qk_done, NC * b + c + 1)
                wait(dve, rot_done, NC * b + c)
                ps = acc[:, :, :].rearrange("p a (h d) -> p a h d", h=NH)
                cs = cos[:, c, :].rearrange("p (a d) -> p a d", a=2).unsqueeze(2).to_broadcast([P, 2, NH, ROT])
                sn = sin[:, c, :].rearrange("p (a d) -> p a d", a=2).unsqueeze(2).to_broadcast([P, 2, NH, ROT])
                nc.vector.tensor_tensor(rot_a[:, :, :, :], ps[:, :, :, 0:ROT], cs, ALU.mult)
                nc.vector.tensor_tensor(rot_b[:, :, :, 0:ROT:2], ps[:, :, :, 1:ROT:2], sn[:, :, :, 0:ROT:2], ALU.mult)
                nc.vector.tensor_tensor(rot_b[:, :, :, 1:ROT:2], ps[:, :, :, 0:ROT:2], sn[:, :, :, 1:ROT:2], ALU.mult)
                dc = dec[:, c, :].rearrange("p (a h) -> p a h", a=2).unsqueeze(3).to_broadcast([P, 2, NH, HD - ROT])
                nc.vector.tensor_tensor(qk_tok[:, c, :, :, ROT:HD], ps[:, :, :, ROT:HD], dc, ALU.mult).then_inc(qk_read, 1)

            def pair_moments(b, p, link):
                dve.wait_ge(r_done, NP * b + p + 1)
                link(nc.vector.bn_stats(bn6[:, 0, :], pret[p % 2][:, :]))
                nc.vector.memset(pad[:, :], 0.0)
                link(nc.vector.bn_aggr(mv[:, :], bn6[:, 0, :]))
                nc.vector.scalar_tensor_tensor(mv[:, 1:2], mv[:, 0:1], mv[:, 0:1], mv[:, 1:2],
                                               ALU.mult, ALU.add).then_inc(bn_done, 1)

            def pair_variance(b, p, link, st):
                dve.wait_ge(pas_read, st)
                link(nc.vector.scalar_tensor_tensor(ab[:, 0:1], hm[:, 0:1], hm[:, 0:1], hm[:, 1:2],
                                                    ALU.mult, ALU.subtract))
                nc.vector.tensor_scalar(ab[:, 0:1], ab[:, 0:1], -1.0, EPS, ALU.mult, ALU.add).then_inc(ve_done, 1)

            def pair_affine(b, p, link):
                dve.wait_ge(rs_done, NP * b + p + 1)
                link(nc.vector.scalar_tensor_tensor(ab[:, 2:3], ab[:, 1:2], 8.0, gn_s[:, 0, p:p + 1], ALU.mult, ALU.mult))
                link(nc.vector.tensor_tensor(ab[:, 3:4], ab[:, 2:3], hm[:, 0:1], ALU.mult))
                nc.vector.scalar_tensor_tensor(ab_b[:, :], gn_s[:, 1, p:p + 1], 8.0, ab[:, 3:4],
                                               ALU.mult, ALU.subtract).then_inc(ab_done, 1)

            def gated(b, p, link):
                dve.wait_ge(aff_done, NP * b + p + 1)
                if p == 0:
                    dve.wait_ge(gate_done, NP * (b + 1))
                y = y_t[:, p % 2, :]
                link(nc.vector.tensor_tensor(y, y, gate[:, p, :], ALU.mult))
                link(nc.vector.tensor_copy(y_h[:, p, :], y))
                sub(y_l[:, p, :], y, y_h[:, p, :]).then_inc(y_done, 1)

            def finish_gate(b, p, link):
                dve.wait_ge(sq_done, NP * b + p + 1)
                link(nc.vector.tensor_scalar(gate_t[:, :], gate_t[:, :], 4.0, None, ALU.add))
                link(nc.vector.reciprocal(gate_t[:, :], gate_t[:, :]))
                nc.vector.scalar_tensor_tensor(gate[:, p, :], gate_t[:, :], -0.125, gate[:, p, :],
                                               ALU.add, ALU.mult).then_inc(gate_done, 1)

            def add_state(b, c):
                dve.wait_ge(s_done, (NC - 1) * b + c + 1)
                if c:
                    dve.wait_ge(s_read, (NC - 1) * b + c)
                ps = acc[:, (1, 1, 0)[c], :].rearrange("p (q n) -> p q n", q=NP)
                for e in range(2):
                    half_ = slice(e * HD, (e + 1) * HD)
                    if c == 0:
                        last = nc.vector.tensor_copy(state[half_, 0, :, half_], ps[half_, :, half_])
                    else:
                        last = nc.vector.tensor_tensor(state[half_, c, :, half_], ps[half_, :, half_],
                                                       state[half_, c - 1, :, half_], ALU.add)
                last.then_inc(s_read, 1)

            def residual(b, c):
                dve.wait_ge(o_done, NC * b + c + 1)
                if c == 0:
                    dve.wait_ge(xtok_in, 16 * (b + 1))
                nc.vector.tensor_tensor(x_tok[:, c, :], acc[:, (0, 0, 0, 1)[c], :], x_tok[:, c, :],
                                        ALU.add).then_inc(o_read, 1)

            def layer_norm(b, link):
                dve.wait_ge(o_read, NC * (b + 1))
                for c in range(NC):
                    last = nc.vector.bn_stats(bn6[:, c, :], x_tok[:, c, :])
                link(last)
                nc.vector.memset(pad[:, :], 0.0)
                for c in range(NC):
                    last = nc.vector.bn_aggr(ln_mv[:, c, :], bn6[:, c, :])
                link(last)
                nc.vector.tensor_scalar(ln_ve[:, :], ln_mv[:, :, 1], EPS, None, ALU.add).then_inc(lnve_done, 1)
                dve.wait_ge(lnrs_done, b + 1)
                for c in range(NC):
                    last = nc.vector.tensor_scalar(x_tok[:, c, :], x_tok[:, c, :], ln_mv[:, c, 0:1],
                                                   ln_rs[:, c:c + 1], ALU.subtract, ALU.mult)
                last.then_inc(x1_done, 1)

            LINKS_PROJ, LINKS_RET = 2 * NP, NP * (2 + 1 + 2 + 2) + 2

            def part(b, ret, proj, more):
                first = isinstance(b, int) and b < 0
                link = Links(dve, dve_link, 1 if first else 1 + LINKS_PROJ + b * (LINKS_PROJ + LINKS_RET))
                order = pass_order(ret, proj)
                st = lambda p: pass_base(b) + order.index(("ST", p)) + 1
                for p in range(NP):
                    if ret:
                        mask_scores(b, 2 * p)
                        mask_scores(b, 2 * p + 1)
                        if p:
                            pair_variance(b, p - 1, link, st(p - 1))
                    if proj:
                        rotate(b + 1, p)
                    if ret:
                        if p:
                            pair_affine(b, p - 1, link)
                        pair_moments(b, p, link)
                        if p:
                            gated(b, p - 1, link)
                if ret:
                    pair_variance(b, NP - 1, link, st(NP - 1))
                    pair_affine(b, NP - 1, link)
                    gated(b, NP - 1, link)
                if proj:
                    for p in range(NP):
                        finish_gate(b + 1, p, link)
                if more:
                    dve.wait_ge(xs_hi, b + 3)
                    sub(x_l[:, :, :], x_raw[:, :, :], x_h[:, :, :]).then_inc(xs_lo, 1)
                for c, s in ((0, 0), (1, 1), (2, None), (3, 2)):
                    if ret:
                        residual(b, c)
                    if proj and s is not None:
                        add_state(b + 1, s)
                if ret:
                    layer_norm(b, link)
                assert link.n == LINKS_PROJ * proj + LINKS_RET * ret
            run(dve, part)

        @block.gpsimd
        def _(pool):
            pool.wait_ge(init, 1)
            pool.wait_ge(const_in, 16 * 6)

            def rotate(b, c):
                pool.wait_ge(qk_read, NC * b + c + 1)
                nc.gpsimd.tensor_tensor(rot_a[:, :, :, :], rot_a[:, :, :, :], rot_b[:, :, :, :],
                                        ALU.add).then_inc(pool_link, 1)
                pool.wait_ge(pool_link, NC * b + c + 1)
                dc = tab_s[:, c, 4 * ROT:4 * ROT + 2 * NH].rearrange("p (a h) -> p a h", a=2)\
                    .unsqueeze(3).to_broadcast([P, 2, NH, ROT])
                nc.gpsimd.tensor_tensor(qk_tok[:, c, :, :, 0:ROT], rot_a[:, :, :, :], dc, ALU.mult).then_inc(rot_done, 1)

            def rstd(b, p):
                pool.wait_ge(ve_done, NP * b + p + 1)
                nc.gpsimd.tensor_tensor(ab[:, 1:2], ab[:, 0:1], half[:, 0:1], ALU.pow).then_inc(rs_done, 1)

            def part(b, ret, proj, more):
                for p in range(NP):
                    if ret and p:
                        rstd(b, p - 1)
                    if proj:
                        rotate(b + 1, p)
                if ret:
                    rstd(b, NP - 1)
                    pool.wait_ge(lnve_done, b + 1)
                    nc.gpsimd.tensor_tensor(ln_rs[:, :], ln_ve[:, :], half[:, :], ALU.pow).then_inc(lnrs_done, 1)
            run(pool, part)


def ffn_phase(nc, ctxT, ctx_in, mask, qup, sup, bup, aup, bupl, qdn, sdn, bdn, adn, bdnl, consts,
              selup, seldn, x1s, out):
    with ExitStack() as stack:
        def sb(name, shape, dt=F32):
            return stack.enter_context(nc.sbuf_tensor(name, shape, dt))

        wu_h, wu_l = sb("wu_h", [P, NK, FF], F32R), sb("wu_l", [P, NK, FF], F32R)
        wd_h, wd_l = sb("wd_h", [P, NF, D], F32R), sb("wd_l", [P, NF, D], F32R)
        bup_s, bdn_s = sb("bup_s", [P, NF]), sb("bdn_s", [P, D])
        prepare_weights(nc, wu_h, wu_l, wd_h, wd_l, bup_s, bdn_s, qup, sup, bup, aup, bupl, qdn, sdn,
                        bdn, adn, bdnl, selup, seldn)
        ffn_rows(nc, wu_h, wu_l, wd_h, wd_l, bup_s, bdn_s, ctxT, ctx_in, mask, consts, x1s, out)


def prepare_weights(nc, wu_h, wu_l, wd_h, wd_l, bup_s, bdn_s, qup, sup, bup, aup, bupl, qdn, sdn,
                    bdn, adn, bdnl, selup, seldn):
    NQ = 8
    NU = NK * (FF // 512)
    NW = NU + NF
    with ExitStack() as stack:
        def sb(name, shape, dt=F32):
            return stack.enter_context(nc.sbuf_tensor(name, shape, dt))

        def pb(name, shape):
            return stack.enter_context(nc.psum_tensor(name, shape, F32))

        def sem(name):
            return stack.enter_context(nc.semaphore(name))

        q_s = sb("q_s", [P, NQ, 512], I32)
        w_s = sb("w_s", [P, 4, 512])
        su_s, sd_s = sb("su_s", [2 * NK, FF]), sb("sd_s", [2 * NF, D])
        au_s, bu_s = sb("au_s", [R, D]), sb("bu_s", [R, FF])
        ad_s, bd_s = sb("ad_s", [R, FF]), sb("bd_s", [R, D])
        selu_s, seld_s = sb("selu_s", [2 * NK, NK, P]), sb("seld_s", [2 * NF, NF, P])
        pscale = [pb(f"pscale{i}", [P, 512]) for i in range(2)]
        plora = [pb(f"plora{i}", [P, 512]) for i in range(2)]
        small_in, q_in = sem("small_in"), [sem(f"q_in{i}") for i in range(NQ)]
        sl_done, deq_done, w_done, hi_done, lo_done = map(sem, ("sl_done", "deq_done", "w_done", "hi_done", "lo_done"))
        block = stack.enter_context(nc.Block())

        def piece(n):
            if n < NU:
                k, f = divmod(n, FF // 512)
                cols = slice(f * 512, (f + 1) * 512)
                return (qup[k * P:(k + 1) * P, cols], selu_s[:, k, :], su_s[:, cols], au_s[:, k * P:(k + 1) * P],
                        bu_s[:, cols], wu_h[:, k, cols], wu_l[:, k, cols])
            t = n - NU
            return (qdn[t * P:(t + 1) * P, :], seld_s[:, t, :], sd_s[:, :], ad_s[:, t * P:(t + 1) * P],
                    bd_s[:, :], wd_h[:, t, :], wd_l[:, t, :])

        @block.sync
        def _(sp):
            for dst, src in ((su_s[:, :], sup), (au_s[:, :], aup), (bu_s[:, :], bupl), (selu_s[:, :, :], selup),
                             (sd_s[:, :], sdn), (ad_s[:, :], adn), (bd_s[:, :], bdnl), (seld_s[:, :, :], seldn),
                             (bup_s[:, :], bup), (bdn_s[:, :], bdn.to_broadcast([P, D]))):
                sp.dma_start(dst, src).then_inc(small_in, 16)
            for n in range(NW):
                if n >= NQ:
                    sp.wait_ge(deq_done, n - NQ + 1)
                sp.dma_start(q_s[:, n % NQ, :], piece(n)[0]).then_inc(q_in[n % NQ], 16)

        @block.tensor
        def _(pe):
            pe.wait_ge(small_in, 160)
            for n in range(NW):
                _, sel, scale, a, b, _, _ = piece(n)
                if n >= 2:
                    pe.wait_ge(w_done, n - 1)
                nc.tensor.matmul(pscale[n % 2][:, :], sel, scale, start=True, stop=True)
                nc.tensor.matmul(plora[n % 2][:, :], a, b, start=True, stop=True).then_inc(sl_done, 1)

        @block.vector
        def _(dve):
            for n in range(NW):
                dve.wait_ge(q_in[n % NQ], 16 * (n // NQ + 1))
                dve.wait_ge(sl_done, n + 1)
                if n >= 4:
                    dve.wait_ge(lo_done, n - 3)
                w = w_s[:, n % 4, :]
                nc.vector.scalar_tensor_tensor(w, q_s[:, n % NQ, :], -7.5, pscale[n % 2][:, :],
                                               ALU.add, ALU.mult).then_inc(deq_done, 1)
                dve.wait_ge(deq_done, n + 1)
                nc.vector.tensor_tensor(w, w, plora[n % 2][:, :], ALU.add).then_inc(w_done, 1)

        @block.scalar
        def _(act):
            for n in range(NW):
                act.wait_ge(w_done, n + 1)
                nc.scalar.activation(piece(n)[5], w_s[:, n % 4, :], ACT.Copy).then_inc(hi_done, 1)

        @block.gpsimd
        def _(pool):
            for n in range(NW):
                pool.wait_ge(hi_done, n + 1)
                _, _, _, _, _, hi, lo = piece(n)
                nc.gpsimd.tensor_tensor(lo, w_s[:, n % 4, :], hi.bitcast(F32), ALU.subtract).then_inc(lo_done, 1)


def ffn_rows(nc, wu_h, wu_l, wd_h, wd_l, bup_s, bdn_s, ctxT, ctx_in, mask, consts, x1s, out):
    with ExitStack() as stack:
        def sb(name, shape, dt=F32):
            return stack.enter_context(nc.sbuf_tensor(name, shape, dt))

        def pb(name, shape):
            return stack.enter_context(nc.psum_tensor(name, shape, F32))

        def sem(name):
            return stack.enter_context(nc.semaphore(name))

        NHID = 2
        x1 = sb("x1", [P, NC, D])
        x1_T = sb("x1_T", [P, NK, S])
        x2_h, x2_l = sb("x2_h", [P, NK, S], F32R), sb("x2_l", [P, NK, S], F32R)
        x2b = sb("x2b", [P, NC, D])
        hid = sb("hid", [P, 2, S])
        hid_h, hid_l = sb("hid_h", [P, NHID, S], F32R), sb("hid_l", [P, NHID, S], F32R)
        z_out = sb("z_out", [P, 2, D])
        ctx_T, ctx_s = sb("ctx_T", [P, NK, M]), sb("ctx_s", [P, D])
        ctx_h, ctx_l = sb("ctx_h", [P, D], F32R), sb("ctx_l", [P, D], F32R)
        mask_s = sb("mask_s", [P, M], U8)
        keep, bias, valid = sb("keep", [P, M]), sb("bias", [P, M]), sb("valid", [P, 1])
        sm, smax, ssum = sb("sm", [P, NC, M]), sb("smax", [P, NC]), sb("ssum", [P, NC])
        p_Th, p_Tl = sb("p_Th", [P, 2 * P], F32R), sb("p_Tl", [P, 2 * P], F32R)
        ident_s = sb("ident_s", [P, P])
        half2 = sb("half2", [P, NC])
        pad2 = sb("pad2", [P, 1])
        bn6 = sb("bn6b", [P, NC, 6])
        ln_mv, ln_ve, ln_rs = sb("ln_mv2", [P, NC, 2]), sb("ln_ve2", [P, NC]), sb("ln_rs2", [P, NC])
        fn_mv, fn_ve, fn_rs = sb("fn_mv", [P, NC, 2]), sb("fn_ve", [P, NC]), sb("fn_rs", [P, NC])
        pdn = [pb(f"pdn{i}", [P, 512]) for i in range(NC)]
        pup = [pb(f"pup{i}", [P, 512]) for i in range(2)]
        pxa = [pb(f"pxa{i}", [P, 512]) for i in range(2)]

        x1_in, ctx_inn, z_free = sem("x1_in"), sem("ctx_inn"), [sem("z_free0"), sem("z_free1")]
        init = sem("init2")
        t1_done, sc_done, ta_done, rd_done, t2_done, up_done, dn_done = map(
            sem, ("t1_done", "xsc_done", "ta_done", "rd_done", "t2_done", "up_done", "dn_done"))
        t1_read, ctxh_done, ta_hi, exp_done, t2_hi, hid_done = map(
            sem, ("t1_read", "ctxh_done", "ta_hi", "exp_done", "t2_hi", "hid_done"))
        ctxl_done, mask_done, shift_done, prob_done, ta_lo, rd_read, lnve_done, x2_done, t2_lo, hidl_done = map(
            sem, ("ctxl_done", "mask_done", "shift_done", "prob_done", "ta_lo", "rd_read", "xlnve_done", "x2_done",
                  "t2_lo", "hidl_done"))
        pdn_free, fnve_done, z_done = sem("pdn_free"), sem("fnve_done"), sem("z_done")
        lnrs_done, x2b_done, fnrs_done = sem("xlnrs_done"), sem("x2b_done"), sem("fnrs_done")
        dve_link = sem("dve_link2")
        block = stack.enter_context(nc.Block())

        def run(eng, part):
            part(-1, False, True)
            with eng.Fori(0, B - 1) as b:
                part(b, True, True)
            part(B - 1, True, False)

        @block.sync
        def _(sp):
            for n, z in enumerate(z_free):
                cols = slice(n * HD, (n + 1) * HD)
                sp.dma_start(ident_s[:, cols], consts[:, 2 * P + n * HD:2 * P + (n + 1) * HD]).then_inc(z, 16)

            def part(b, ffn, xattn):
                if xattn:
                    if ffn:
                        sp.wait_ge(x2b_done, b + 1)
                    sp.dma_start(x1[:, :, :], x1s[b + 1].rearrange("(c p) n -> p c n", p=P)).then_inc(x1_in, 16)
                    sp.dma_start(ctx_T[:, :, :], ctxT[b + 1].rearrange("(k p) m -> p k m", p=P)).then_inc(ctx_inn, 16)
                    for half in range(2):
                        sp.dma_start(ctx_s[half * M:(half + 1) * M, :], ctx_in[b + 1]).then_inc(ctx_inn, 16)
                    sp.dma_start(mask_s[:, :], mask[b + 1].to_broadcast([P, M])).then_inc(ctx_inn, 16)
                if ffn:
                    for c in range(NC):
                        sp.wait_ge(z_done, NC * b + c + 1)
                        sp.dma_start(out[b, c * P:(c + 1) * P, :], z_out[:, c % 2, :]).then_inc(z_free[c % 2], 16)
            run(sp, part)
            for z in z_free:
                sp.wait_ge(z, 16 * (B * NC // 2 + 1))

        @block.tensor
        def _(pe):
            def split3(dst, lh, ll, rh, rl, first, last):
                nc.tensor.matmul(dst, lh, rh, start=first, stop=False)
                nc.tensor.matmul(dst, ll, rh, start=False, stop=False)
                return nc.tensor.matmul(dst, lh, rl, start=False, stop=last)

            for z in z_free:
                pe.wait_ge(z, 16)

            def transpose_x1(b, k):
                if k == 0:
                    pe.wait_ge(x1_in, 16 * (b + 1))
                if k >= 2:
                    pe.wait_ge(t1_read, NK * b + k - 1)
                for c in range(NC):
                    last = nc.tensor.transpose(pxa[k % 2][:, c * P:(c + 1) * P], x1[:, c, k * P:(k + 1) * P], ident_s[:, :])
                last.then_inc(t1_done, 1)

            def scores(b):
                pe.wait_ge(t1_read, NK * (b + 1))
                pe.wait_ge(ctx_inn, 64 * (b + 1))
                for c in range(NC):
                    for k in range(NK):
                        last = nc.tensor.matmul(pxa[0][:, c * M:(c + 1) * M], x1_T[:, k, c * P:(c + 1) * P],
                                                ctx_T[:, k, :], start=(k == 0), stop=(k == NK - 1))
                last.then_inc(sc_done, 1)

            def transpose_probs(b):
                pe.wait_ge(exp_done, b + 1)
                for a in range(2):
                    last = nc.tensor.transpose(pxa[1][:, a * P:(a + 1) * P],
                                               sm[:, 2 * a:2 * a + 2, :].rearrange("p c m -> p (c m)"), ident_s[:, :])
                last.then_inc(ta_done, 1)

            def read_memory(b, c):
                if c == 0:
                    pe.wait_ge(ta_hi, b + 1)
                    pe.wait_ge(ta_lo, b + 1)
                    pe.wait_ge(ctxl_done, b + 1)
                if c >= 2:
                    pe.wait_ge(rd_read, NC * b + c - 1)
                rows, ts = slice((c % 2) * M, (c % 2 + 1) * M), slice(c // 2 * P, (c // 2 + 1) * P)
                split3(pxa[c % 2][:, :], p_Th[rows, ts], p_Tl[rows, ts], ctx_h[rows, :], ctx_l[rows, :], True, True).then_inc(rd_done, 1)

            def transpose_x2(b, k):
                if k == 0:
                    pe.wait_ge(x2_done, b + 1)
                if k >= 2:
                    pe.wait_ge(t2_hi, NK * b + k - 1)
                    pe.wait_ge(t2_lo, NK * b + k - 1)
                for c in range(NC):
                    last = nc.tensor.transpose(pxa[k % 2][:, c * P:(c + 1) * P], x1[:, c, k * P:(k + 1) * P], ident_s[:, :])
                last.then_inc(t2_done, 1)

            def up(b, f):
                if f == 0:
                    pe.wait_ge(t2_hi, NK * (b + 1))
                    pe.wait_ge(t2_lo, NK * (b + 1))
                if f >= 2:
                    pe.wait_ge(hid_done, NF * b + f - 1)
                fs = slice(f * P, (f + 1) * P)
                for k in range(NK):
                    last = split3(pup[f % 2][:, :], wu_h[:, k, fs], wu_l[:, k, fs], x2_h[:, k, :], x2_l[:, k, :],
                                  k == 0, k == NK - 1)
                last.then_inc(up_done, 1)

            def down(b, f):
                pe.wait_ge(hidl_done, NF * b + f + 1)
                if f == 0:
                    pe.wait_ge(pdn_free, NC * (b + 1))
                for c in range(NC):
                    ts = slice(c * P, (c + 1) * P)
                    last = split3(pdn[c][:, :], hid_h[:, f % NHID, ts], hid_l[:, f % NHID, ts], wd_h[:, f, :],
                                  wd_l[:, f, :], f == 0, f == NF - 1)
                last.then_inc(dn_done, 1)

            def part(b, ffn, xattn):
                def beside(f):
                    if not xattn:
                        return
                    if 4 <= f < 6:
                        transpose_x1(b + 1, 2 * (f - 4))
                        transpose_x1(b + 1, 2 * (f - 4) + 1)
                    if f == 6:
                        scores(b + 1)
                    if f == 8:
                        transpose_probs(b + 1)
                    if 9 <= f < 13:
                        read_memory(b + 1, f - 9)
                for f in range(NF):
                    if ffn:
                        up(b, f)
                    beside(f)
                    if ffn and f:
                        down(b, f - 1)
                if xattn:
                    for k in range(NK):
                        transpose_x2(b + 1, k)
                if ffn:
                    down(b, NF - 1)
            run(pe, part)

        @block.scalar
        def _(act):
            def part(b, ffn, xattn):
                r = b + 1

                def beside(f):
                    if not xattn:
                        return
                    if f == 3:
                        act.wait_ge(ctx_inn, 64 * (r + 1))
                        nc.scalar.activation(ctx_h[:, :], ctx_s[:, :], ACT.Copy).then_inc(ctxh_done, 1)
                    if 4 <= f < 6:
                        for k in (2 * (f - 4), 2 * (f - 4) + 1):
                            act.wait_ge(t1_done, NK * r + k + 1)
                            nc.scalar.activation(x1_T[:, k, :], pxa[k % 2][:, :], ACT.Copy).then_inc(t1_read, 1)
                    if f == 7:
                        act.wait_ge(shift_done, r + 1)
                        nc.scalar.activation(sm[:, :, :], sm[:, :, :], ACT.Exp).then_inc(exp_done, 1)
                    if f == 8:
                        act.wait_ge(ta_done, r + 1)
                        nc.scalar.activation(p_Th[:, :], pxa[1][:, 0:2 * P], ACT.Copy).then_inc(ta_hi, 1)
                for f in range(NF):
                    if ffn:
                        act.wait_ge(up_done, NF * b + f + 1)
                        if f >= 2:
                            act.wait_ge(hidl_done, NF * b + f - 1)
                            act.wait_ge(dn_done, NF * b + f - 1)
                        nc.scalar.activation(hid[:, f % 2, :], pup[f % 2][:, :], ACT.Relu, bias=bup_s[:, f:f + 1])
                        nc.scalar.activation(hid_h[:, f % NHID, :], pup[f % 2][:, :], ACT.Relu,
                                             bias=bup_s[:, f:f + 1]).then_inc(hid_done, 1)
                    beside(f)
                if xattn:
                    for k in range(NK):
                        act.wait_ge(t2_done, NK * r + k + 1)
                        nc.scalar.activation(x2_h[:, k, :], pxa[k % 2][:, :], ACT.Copy).then_inc(t2_hi, 1)
            run(act, part)

        @block.vector
        def _(dve):
            def sub(dst, a, hi):
                return nc.vector.tensor_tensor(dst, a, hi.bitcast(F32), ALU.subtract)

            nc.vector.memset(half2[:, :], -0.5).then_inc(init, 1)
            nc.vector.memset(z_out[:, :, 0:1], 0.0).then_inc(pdn_free, NC)
            LINKS_X, LINKS_F = 6, 2

            def masks(b, link):
                dve.wait_ge(ctx_inn, 64 * (b + 1))
                link(nc.vector.tensor_copy(keep[:, :], mask_s[:, :]))
                nc.vector.tensor_scalar(bias[:, :], keep[:, :], -1.0, NEG, ALU.add, ALU.mult)
                nc.vector.reduce_max(valid[:, :], keep[:, :], AX.X).then_inc(mask_done, 1)
                dve.wait_ge(ctxh_done, b + 1)
                sub(ctx_l[:, :], ctx_s[:, :], ctx_h[:, :]).then_inc(ctxl_done, 1)

            def softmax_shift(b, link):
                dve.wait_ge(sc_done, b + 1)
                dve.wait_ge(mask_done, b + 1)
                kp = keep[:, :].unsqueeze(1).to_broadcast([P, NC, M])
                bs = bias[:, :].unsqueeze(1).to_broadcast([P, NC, M])
                ps = pxa[0][:, 0:NC * M].rearrange("p (c m) -> p c m", c=NC)
                link(nc.vector.scalar_tensor_tensor(sm[:, :, :], ps, float(np.float32(1.0) / np.sqrt(np.float32(D))), kp,
                                                    ALU.mult, ALU.mult))
                link(nc.vector.tensor_tensor(sm[:, :, :], sm[:, :, :], bs, ALU.add))
                link(nc.vector.reduce_max(smax[:, :], sm[:, :, :], AX.X))
                nc.vector.tensor_tensor(sm[:, :, :], sm[:, :, :], smax[:, :].unsqueeze(2).to_broadcast([P, NC, M]),
                                        ALU.subtract).then_inc(shift_done, 1)

            def softmax_sum(b, link):
                dve.wait_ge(exp_done, b + 1)
                nc.vector.reduce_sum(ssum[:, :], sm[:, :, :], AX.X).then_inc(prob_done, 1)
                dve.wait_ge(prob_done, 3 * b + 1)
                nc.vector.reciprocal(ssum[:, :], ssum[:, :]).then_inc(prob_done, 1)
                dve.wait_ge(prob_done, 3 * b + 2)
                nc.vector.tensor_scalar(ssum[:, :], ssum[:, :], valid[:, 0:1], None, ALU.mult).then_inc(prob_done, 1)

            def part(b, ffn, xattn):
                r = b + 1
                first = isinstance(b, int) and b < 0
                link = Links(dve, dve_link, 0 if first else LINKS_X + b * (LINKS_X + LINKS_F))

                def beside(f):
                    if not xattn:
                        return
                    if f == 3:
                        masks(r, link)
                    if f == 6:
                        softmax_shift(r, link)
                    if f == 8:
                        softmax_sum(r, link)
                        dve.wait_ge(ta_hi, r + 1)
                        sub(p_Tl[:, :], pxa[1][:, 0:2 * P], p_Th[:, :]).then_inc(ta_lo, 1)
                    if 9 <= f < 13:
                        c = f - 9
                        dve.wait_ge(rd_done, NC * r + c + 1)
                        if c == 0:
                            dve.wait_ge(prob_done, 3 * (r + 1))
                        nc.vector.scalar_tensor_tensor(x1[:, c, :], pxa[c % 2][:, :], ssum[:, c:c + 1], x1[:, c, :],
                                                       ALU.mult, ALU.add).then_inc(rd_read, 1)
                    if f == 13:
                        dve.wait_ge(rd_read, NC * (r + 1))
                        for c in range(NC):
                            last = nc.vector.bn_stats(bn6[:, c, :], x1[:, c, :])
                        link(last)
                        nc.vector.memset(pad2[:, :], 0.0)
                        for c in range(NC):
                            last = nc.vector.bn_aggr(ln_mv[:, c, :], bn6[:, c, :])
                        link(last)
                        nc.vector.tensor_scalar(ln_ve[:, :], ln_mv[:, :, 1], EPS, None, ALU.add).then_inc(lnve_done, 1)
                    if f == 14:
                        dve.wait_ge(lnrs_done, r + 1)
                        for c in range(NC):
                            last = nc.vector.tensor_scalar(x1[:, c, :], x1[:, c, :], ln_mv[:, c, 0:1],
                                                           ln_rs[:, c:c + 1], ALU.subtract, ALU.mult)
                        last.then_inc(x2_done, 1)
                for f in range(NF):
                    if ffn:
                        dve.wait_ge(hid_done, NF * b + f + 1)
                        if f >= 2:
                            dve.wait_ge(dn_done, NF * b + f - 1)
                        sub(hid_l[:, f % NHID, :], hid[:, f % 2, :], hid_h[:, f % NHID, :]).then_inc(hidl_done, 1)
                    beside(f)
                if xattn:
                    for k in range(NK):
                        dve.wait_ge(t2_hi, NK * r + k + 1)
                        sub(x2_l[:, k, :], pxa[k % 2][:, :], x2_h[:, k, :]).then_inc(t2_lo, 1)
                if ffn:
                    dve.wait_ge(dn_done, NF * (b + 1))
                    dve.wait_ge(x2b_done, b + 1)
                    for c in range(NC):
                        nc.vector.tensor_tensor(x2b[:, c, :], pdn[c][:, :], x2b[:, c, :], ALU.add).then_inc(pdn_free, 1)
                    dve.wait_ge(pdn_free, NC * (b + 2))
                    for c in range(NC):
                        last = nc.vector.bn_stats(bn6[:, c, :], x2b[:, c, :])
                    link(last)
                    nc.vector.memset(pad2[:, :], 0.0)
                    for c in range(NC):
                        last = nc.vector.bn_aggr(fn_mv[:, c, :], bn6[:, c, :])
                    link(last)
                    nc.vector.tensor_scalar(fn_ve[:, :], fn_mv[:, :, 1], EPS, None, ALU.add).then_inc(fnve_done, 1)
                    dve.wait_ge(fnrs_done, b + 1)
                    for c in range(NC):
                        dve.wait_ge(z_free[c % 2], 16 * (2 * b + 1 + c // 2))
                        nc.vector.tensor_scalar(z_out[:, c % 2, :], x2b[:, c, :], fn_mv[:, c, 0:1], fn_rs[:, c:c + 1],
                                                ALU.subtract, ALU.mult).then_inc(z_done, 1)
                assert link.n == LINKS_X * xattn + LINKS_F * ffn
            run(dve, part)

        @block.gpsimd
        def _(pool):
            pool.wait_ge(init, 1)

            def part(b, ffn, xattn):
                if xattn:
                    r = b + 1
                    pool.wait_ge(lnve_done, r + 1)
                    nc.gpsimd.tensor_tensor(ln_rs[:, :], ln_ve[:, :], half2[:, :], ALU.pow).then_inc(lnrs_done, 1)
                if ffn:
                    pool.wait_ge(fnve_done, b + 1)
                    nc.gpsimd.tensor_tensor(fn_rs[:, :], fn_ve[:, :], half2[:, :], ALU.pow).then_inc(fnrs_done, 1)
                if xattn:
                    pool.wait_ge(t2_done, NK * (b + 2))
                    if ffn:
                        pool.wait_ge(z_done, NC * (b + 1))
                    for c in range(NC):
                        last = nc.gpsimd.tensor_tensor(x2b[:, c, :], x1[:, c, :], bdn_s[:, :], ALU.add)
                    last.then_inc(x2b_done, 1)
            run(pool, part)


def kernel(**inputs):
    import numpy as _np
    import concourse.bacc as _bacc
    from concourse import mybir as _mybir
    from concourse.bass_utils import run_bass_kernel_spmd as _run

    a = {k: _np.asarray(v) for k, v in inputs.items()}
    c = _np.ascontiguousarray
    x = a["x"]
    w = a["L0_attn_wqkv"].reshape(NH, 3, HD, D)
    wT = w.transpose(3, 1, 0, 2).reshape(D, 3 * D)
    tab, consts, selup, seldn = tables()
    arrays = {
        "xT": c(x.transpose(0, 2, 1)), "x": c(x),
        "ctxT": c(a["ctx_2048"].transpose(0, 2, 1)), "ctx_in": c(a["ctx_2048"]),
        "mask": c(a["mask_BxS2_bk0"].reshape(B, 1, M)),
        "wqkT": c(wT[:, 0:2 * D]),
        "wvgT": c(_np.concatenate([wT[:, 2 * D:], a["L0_attn_wg"].T], axis=1)),
        "woT": c(a["L0_attn_wo"].T),
        "gnw": c(a["L0_attn_gn_weight"].reshape(NP, 2).T), "gnb": c(a["L0_attn_gn_bias"].reshape(NP, 2).T),
        "qup": c(a["L0_ffn_w_up_q"].T), "sup": c(a["L0_ffn_w_up_scale"].T),
        "bup": c(a["L0_ffn_b_up"].reshape(NF, P).T),
        "aup": c(a["L0_ffn_w_up_lora_a"].T), "bupl": c(a["L0_ffn_w_up_lora_b"]),
        "qdn": c(a["L0_ffn_w_down_q"].T), "sdn": c(a["L0_ffn_w_down_scale"].T),
        "bdn": c(a["L0_ffn_b_down"].reshape(1, D)),
        "adn": c(a["L0_ffn_w_down_lora_a"].T), "bdnl": c(a["L0_ffn_w_down_lora_b"]),
        "tab": tab, "consts": consts, "selup": selup, "seldn": seldn,
    }
    nc = _bacc.Bacc("TRN2", target_bir_lowering=False, num_devices=1)
    args = [nc.dram_tensor(f"in_{k}", v.shape, _mybir.dt.from_np(v.dtype), kind="ExternalInput").ap()
            for k, v in arrays.items()]
    out = nc.dram_tensor("out_0", (B, S, D), F32, kind="ExternalOutput").ap()
    x1s = nc.dram_tensor("x1_scratch", (B, S, D), F32, kind="Internal").ap()
    decoder_kernel(nc, *args, out, x1s)
    r = _run(nc, [{f"in_{k}": v for k, v in arrays.items()}], core_ids=[0])
    return r.results[0]["out_0"]
```

```python
import numpy as np
import concourse.bass as bass
from concourse import mybir
from contextlib import ExitStack

F32 = mybir.dt.float32
F32R = mybir.dt.float32r
I32 = mybir.dt.int32
U8 = mybir.dt.uint8
ALU = mybir.AluOpType
ACT = mybir.ActivationFunctionType
AX = mybir.AxisListType

B, S, D = 8, 512, 512
P = 128
NH, HD, ROT = 8, 64, 32
NC = S // P
NK = D // P
NP = NH // 2
M = 64
FF = 2048
NF = FF // P
QB = 64
R = 16
EPS = 1e-5
NEG = 1e30

PASS_PROJ = [("V", c) for c in range(NC)] + [("G", p) for p in range(NP)]
PASS_BOTH = [("ST", 0), ("ST", 1), ("ST", 2), ("V", 0), ("ST", 3)] + PASS_PROJ[1:]
PASS_RET = [("ST", p) for p in range(NP)]
THEN_BOTH = [("V", 0), ("ST", 3), ("T", 0), ("V", 1), ("T", 1), ("V", 2), ("T", 2), ("V", 3), ("T", 3),
             ("G", 0), ("T", 4), ("G", 1), ("T", 5), ("G", 2), ("T", 6), ("G", 3), ("T", 7)]
THEN_PROJ = [("V", 3), ("T", 0), ("T", 1), ("G", 0), ("T", 2), ("T", 3), ("G", 1), ("T", 4), ("T", 5),
             ("G", 2), ("T", 6), ("T", 7), ("G", 3)]
THEN_RET = [("ST", 3)]


def pass_order(ret, proj):
    return PASS_BOTH if ret and proj else PASS_PROJ if proj else PASS_RET


def then_order(ret, proj):
    return THEN_BOTH if ret and proj else THEN_PROJ if proj else THEN_RET


def pass_base(b):
    return 0 if isinstance(b, int) and b < 0 else b * len(PASS_BOTH) + len(PASS_PROJ)


def tables():
    f = np.float32
    inv = (f(1.0) / (f(10000.0) ** (np.arange(0, ROT, 2, dtype=f) / f(ROT)))).astype(f)
    t = np.arange(S, dtype=f)
    ang = (t[:, None] * inv[None, :]).astype(f)
    ang = np.repeat(ang, 2, axis=-1).astype(np.float64)
    base = ((np.arange(0, ROT, 2, dtype=f) + f(0.4 * ROT)) / f(1.4 * ROT)).astype(np.float64)
    power = ((t - S // 2) / f(512.0)).astype(np.float64)
    sc = base[None, :] ** power[:, None]
    sc = np.concatenate([sc, sc], axis=-1)
    sign = np.tile([-1.0, 1.0], ROT // 2)
    rot = np.zeros((S, 2, 2, ROT))
    for n, s_ in enumerate((sc, 1.0 / sc)):
        rot[:, 0, n] = np.cos(ang) * s_
        rot[:, 1, n] = np.sin(ang) * s_ * sign
    gamma = 1.0 - 2.0 ** (-5.0 - np.arange(NH))
    dist = np.arange(S) - S // 2
    dec = np.stack([gamma[None] ** dist[:, None], gamma[None] ** -dist[:, None]], axis=1)
    tab = np.concatenate([rot.reshape(S, -1), dec.reshape(S, -1)], axis=1)
    tab = tab.reshape(NC, P, -1).transpose(1, 0, 2)
    j, i = np.arange(P)[:, None], np.arange(P)[None, :]
    causal = (j <= i).astype(f)
    heads = np.where((j // HD) == (i // HD), 1.0 / HD, 0.0).astype(f)
    return np.ascontiguousarray(tab.astype(f)), np.concatenate([causal, heads, np.eye(P, dtype=f)], axis=1)


def stacked(a, rows, total):
    out = np.zeros((total, a.shape[1]), a.dtype)
    for r in rows:
        out[r:r + a.shape[0]] = a
    return out


def selector(tiles):
    t, q = np.arange(tiles)[:, None], np.arange(P)[None, :]
    sel = np.zeros((2 * tiles, tiles, P), np.float32)
    sel[2 * t + q // QB, t, q] = 1.0
    return sel.reshape(2 * tiles, tiles * P)


def wait(eng, sem, value):
    if isinstance(value, int) and value <= 0:
        return
    eng.wait_ge(sem, value)


class Links:

    def __init__(self, eng, sem, base):
        self.eng, self.sem, self.base, self.n = eng, sem, base, 0

    def __call__(self, ins):
        ins.then_inc(self.sem, 1)
        self.n += 1
        self.eng.wait_ge(self.sem, self.base + self.n)


def decoder_kernel(nc, xT, x, ctxT, ctx_in, mask, wqkT, wvgT, woT, gnw, gnb, qup, sup, bup, aup, bupl,
                   qdn, sdn, bdn, adn, bdnl, tab, consts, selup, seldn, out, x1s):
    with nc.sbuf_tensor("w1_h", [P, NK, FF], F32R) as w1_h, nc.sbuf_tensor("w1_l", [P, NK, FF], F32R) as w1_l:
        retention_phase(nc, w1_h, w1_l, xT, x, wqkT, wvgT, woT, gnw, gnb, tab, consts, x1s, qup, sup, aup,
                        bupl, selup)
        ffn_rows(nc, w1_h, w1_l, ctxT, ctx_in, mask, bup, qdn, sdn, bdn, adn, bdnl, consts, seldn, x1s, out)


SK, LK = 64, 64 + R
S_AT, L_AT = (0, 32), (0, 32, 64)
PIECES_AT_PAIR, PIECES_AT_NORM, PIECES_AT_OUT = [0, 0, 3, 4], 5, [1, 1, 1, 1]
PIECES_BESIDE = {6: 2, 7: 2, 8: 2, 9: 1, 10: 1, 11: 1, 12: 1, 13: 2, 14: 2, 15: 2}
HEAD = 2


def up_piece(n, qup, w_h, w_l):
    k, f = divmod(n, FF // 512)
    cols = slice(f * 512, (f + 1) * 512)
    return qup[k * P:(k + 1) * P, cols], f * 512, k * P, w_h[:, k, cols], w_l[:, k, cols]


def down_piece(t, qdn, w_h, w_l):
    return qdn[t * P:(t + 1) * P, :], 0, t * P, w_h[:, t, :], w_l[:, t, :]


class Prep:

    def __init__(self, nc, sem, name, pieces, q, w, raw, st, scale, lora, source, piece):
        self.nc, self.pieces, self.q, self.w, self.raw, self.st = nc, pieces, q, w, raw, st
        self.scale, self.lora, self.source, self.piece = scale, lora, source, piece
        self.small_in, self.q_in = sem(f"{name}_small_in"), [sem(f"{name}_q_in{i}") for i in range(len(q))]
        (self.st_hi, self.st_lo, self.spread, self.deq_done, self.w_done, self.hi_done, self.lo_done) = (
            sem(f"{name}_{x}") for x in ("st_hi", "st_lo", "spread", "deq_done", "w_done", "hi_done", "lo_done"))
        self.at = {x: 0 for x in ("pe", "dve", "act", "pool")}

    def next(self, who, count):
        first = self.at[who]
        self.at[who] += count
        assert self.at[who] <= self.pieces
        return range(first, first + count)

    def load_small(self, eng):
        for dst, src in zip(self.raw, self.source):
            rows, cols = src.shape
            eng.dma_start(dst[0:rows, 0:cols], src).then_inc(self.small_in, 16)

    def load(self, eng):
        slots = len(self.q)
        for n in range(self.pieces):
            if n >= slots:
                eng.wait_ge(self.deq_done, n - slots + 1)
            eng.dma_start(self.q[n % slots], self.piece(n)[0]).then_inc(self.q_in[n % slots], 16)

    def split_small(self, act):
        act.wait_ge(self.small_in, 64)
        for dst, src, of in zip(self.st, self.raw, self.source):
            rows, cols = of.shape
            self.nc.scalar.activation(dst[0:rows, 0:cols], src[0:rows, 0:cols], ACT.Copy).then_inc(self.st_hi, 1)

    def split_small_lo(self, pool):
        for n, (at, rows) in enumerate(((S_AT[1], SK - S_AT[1]), (L_AT[2], R), (L_AT[1], R))):
            pool.wait_ge(self.st_hi, n + 1)
            part = (slice(at, at + rows), slice(0, self.source[n].shape[1]))
            self.nc.gpsimd.tensor_tensor(self.st[n][part], self.raw[n][part], self.st[n][part].bitcast(F32),
                                         ALU.subtract).then_inc(self.st_lo, 1)

    def products(self, pe, count):
        for n in self.next("pe", count):
            if n == 0:
                pe.wait_ge(self.st_hi, 4)
                pe.wait_ge(self.st_lo, 3)
            banks = len(self.scale)
            if n >= banks:
                pe.wait_ge(self.w_done, n - banks + 1)
            _, cols, a, _, _ = self.piece(n)
            s_st, b_st, a_st, sel = self.st
            self.nc.tensor.matmul(self.scale[n % banks], sel[0:SK, a:a + P], s_st[0:SK, cols:cols + 512],
                                  start=True, stop=True)
            self.nc.tensor.matmul(self.lora[n % banks], a_st[0:LK, a:a + P], b_st[0:LK, cols:cols + 512],
                                  start=True, stop=True).then_inc(self.spread, 1)

    def dequantise(self, dve, count):
        for n in self.next("dve", count):
            slots, banks = len(self.q), len(self.scale)
            w = self.w[n % len(self.w)]
            dve.wait_ge(self.q_in[n % slots], 16 * (n // slots + 1))
            dve.wait_ge(self.spread, n + 1)
            if n >= len(self.w):
                dve.wait_ge(self.lo_done, n - len(self.w) + 1)
            self.nc.vector.scalar_tensor_tensor(w, self.q[n % slots], -7.5, self.scale[n % banks],
                                                ALU.add, ALU.mult).then_inc(self.deq_done, 1)
            dve.wait_ge(self.deq_done, n + 1)
            self.nc.vector.tensor_tensor(w, w, self.lora[n % banks], ALU.add).then_inc(self.w_done, 1)

    def hi_parts(self, act, count):
        for n in self.next("act", count):
            act.wait_ge(self.w_done, n + 1)
            self.nc.scalar.activation(self.piece(n)[3], self.w[n % len(self.w)], ACT.Copy).then_inc(self.hi_done, 1)

    def lo_parts(self, pool, count):
        for n in self.next("pool", count):
            pool.wait_ge(self.hi_done, n + 1)
            _, _, _, hi, lo = self.piece(n)
            self.nc.gpsimd.tensor_tensor(lo, self.w[n % len(self.w)], hi.bitcast(F32),
                                         ALU.subtract).then_inc(self.lo_done, 1)


def retention_phase(nc, w1_h, w1_l, xT, x, wqkT, wvgT, woT, gnw, gnb, tab, consts, x1s, qup, sup, aup,
                    bupl, selup):
    with ExitStack() as stack:
        def sb(name, shape, dt=F32):
            return stack.enter_context(nc.sbuf_tensor(name, shape, dt))

        def pb(name, shape):
            return stack.enter_context(nc.psum_tensor(name, shape, F32))

        def sem(name):
            return stack.enter_context(nc.semaphore(name))

        wqk_h, wqk_l = w1_h[:, :, 0:2 * D], w1_l[:, :, 0:2 * D]
        wvg_h, wvg_l = w1_h[:, :, 2 * D:4 * D], w1_l[:, :, 2 * D:4 * D]
        wo_h, wo_l = sb("wo_h", [P, NK, D], F32R), sb("wo_l", [P, NK, D], F32R)
        x_raw = sb("x_raw", [P, NK, S])
        x_h, x_l = sb("x_h", [P, NK, S], F32R), sb("x_l", [P, NK, S], F32R)
        x_tok = sb("x_tok", [P, NC, D])
        qk_tok = sb("qk_tok", [P, NC, 2, NH, HD])
        v_tok = sb("v_tok", [P, NC, D])
        q_T, k_T = sb("q_T", [P, NP, S]), sb("k_T", [P, NP, S])
        sc_T = sb("sc_T", [P, 4, NC, P])
        state = sb("state", [P, NC - 1, NP, P])
        gate = sb("gate", [P, NP, S])
        y_h, y_l = sb("y_h", [P, NP, S], F32R), sb("y_l", [P, NP, S], F32R)
        y_t = sb("y_t", [P, 2, S])
        a_st, sel_st = sb("a_st", [LK, D], F32R), sb("sel_st", [SK, NK * P], F32R)
        rot_a, rot_b = sb("rot_a", [P, 2, NH, ROT]), sb("rot_b", [P, 2, NH, ROT])
        tab_s = sb("tab_s", [P, NC, 4 * ROT + 2 * NH])
        cst = sb("cst", [P, 3 * P])
        gn_s = sb("gn_s", [P, 2, NP])
        half = sb("half", [P, NC])
        pad = sb("pad", [P, 1])
        bn6 = sb("bn6", [P, NC, 6])
        mv = sb("mv", [P, 2])
        hm = sb("hm", [P, 2])
        ab = sb("ab", [P, 4])
        ab_b = sb("ab_b", [P, 1])
        ln_mv, ln_ve, ln_rs = sb("ln_mv", [P, NC, 2]), sb("ln_ve", [P, NC]), sb("ln_rs", [P, NC])

        causal, heads, ident = cst[:, 0:P], cst[:, P:2 * P], cst[:, 2 * P:3 * P]
        acc = pb("acc", [P, 2, 512])
        pas = [pb(f"pas{i}", [P, 512]) for i in range(2)]
        psc = [pb(f"psc{i}", [P, NC, P]) for i in range(2)]
        pret = [pb(f"pret{i}", [P, 512]) for i in range(2)]

        wx_in = [sem(f"wx_in{k}") for k in range(NK)]
        wvg_in, wo_in = sem("wvg_in"), sem("wo_in")
        const_in, x_in, xtok_in, x1_out = sem("const_in"), sem("x_in"), sem("xtok_in"), sem("x1_out")
        first_hi, first_lo = sem("first_hi"), sem("first_lo")
        w_hi, w_lo = sem("w_hi"), sem("w_lo")
        xs_hi, xs_lo = sem("xs_hi"), sem("xs_lo")
        init = sem("init")
        qk_done, v_done, g_done, t_done, s_done = map(sem, ("qk_done", "v_done", "g_done", "t_done", "s_done"))
        sc_done, r_done, st_done, o_done = map(sem, ("sc_done", "r_done", "st_done", "o_done"))
        qk_read, rot_done, pas_read, t_read, s_read, sc_read = map(
            sem, ("qk_read", "rot_done", "pas_read", "t_read", "s_read", "sc_read"))
        sq_done, gate_done = sem("sq_done"), sem("gate_done")
        bn_done, ve_done, rs_done, ab_done, aff_done, y_done = map(
            sem, ("bn_done", "ve_done", "rs_done", "ab_done", "aff_done", "y_done"))
        o_read, lnve_done, lnrs_done, x1_done = map(sem, ("o_read", "lnve_done", "lnrs_done", "x1_done"))
        act_link, dve_link, pool_link = sem("act_link"), sem("dve_link"), sem("pool_link")

        raw = qk_tok[:, :, :, :, :].rearrange("p c a h d -> p (c a h d)")
        prep = Prep(nc, sem, "up", NK * (FF // 512),
                    q=[x_raw[:, n, :].bitcast(I32) for n in range(4)], w=[raw[:, n * 512:(n + 1) * 512] for n in range(4)],
                    raw=[raw[:, 0:2048], raw[:, 2048:4096], rot_a[:, :, :, :].rearrange("p a h d -> p (a h d)"),
                         rot_b[:, :, :, :].rearrange("p a h d -> p (a h d)")],
                    st=[x_h[:, :, :].rearrange("p k t -> p (k t)"), x_l[:, :, :].rearrange("p k t -> p (k t)"),
                        a_st[:, :], sel_st[:, :]],
                    scale=[acc[:, 0, :]], lora=[acc[:, 1, :]], source=[sup, bupl, aup, selup],
                    piece=lambda n: up_piece(n, qup, w1_h, w1_l))

        def run(eng, part):
            part(-1, False, True, True)
            with eng.Fori(0, B - 2) as b:
                part(b, True, True, True)
            part(B - 2, True, True, False)
            part(B - 1, True, False, False)

        block = stack.enter_context(nc.Block())

        @block.sync
        def _(sp):
            for k in range(NK):
                rows = slice(k * P, (k + 1) * P)
                sp.dma_start(qk_tok[:, k, :, :, :].rearrange("p a h d -> p (a h d)"), wqkT[rows, :]).then_inc(wx_in[k], 16)
                sp.dma_start(x_raw[:, k, :], xT[0, rows, :]).then_inc(wx_in[k], 16)
            sp.dma_start(tab_s[:, :, :], tab).then_inc(const_in, 16)
            sp.dma_start(cst[:, :], consts).then_inc(const_in, 16)
            for e in range(2):
                for n, g in enumerate((gnw, gnb)):
                    src = g[e:e + 1, :].to_broadcast([HD, NP])
                    sp.dma_start(gn_s[e * HD:(e + 1) * HD, n, :], src).then_inc(const_in, 16)
            sp.dma_start(gate[:, :, :], wvgT.rearrange("(k p) n -> p k n", p=P)[:, :, 0:D]).then_inc(wvg_in, 16)
            sp.dma_start(v_tok[:, :, :], wvgT.rearrange("(k p) n -> p k n", p=P)[:, :, D:2 * D]).then_inc(wvg_in, 16)
            sp.dma_start(sc_T[:, :, :, :].rearrange("p a c q -> p a (c q)"),
                         woT.rearrange("(k p) n -> p k n", p=P)).then_inc(wo_in, 16)

            def part(b, ret, proj, more):
                if more:
                    if ret:
                        sp.wait_ge(xs_hi, b + 1)
                        sp.wait_ge(xs_lo, b + 1)
                    else:
                        sp.wait_ge(first_hi, NK)
                        sp.wait_ge(first_lo, NK)
                    sp.dma_start(x_raw[:, :, :], xT[b + 2].rearrange("(k p) t -> p k t", p=P)).then_inc(x_in, 16)
                if proj and not more:
                    sp.wait_ge(t_done, 2 * NP * B)
                    sp.wait_ge(s_done, (NC - 1) * B)
                    prep.load_small(sp)
                if not proj:
                    prep.load(sp)
                if ret:
                    sp.wait_ge(x1_done, b + 1)
                    sp.dma_start(x1s[b].rearrange("(c p) n -> p c n", p=P), x_tok[:, :, :]).then_inc(x1_out, 16)
                    sp.wait_ge(x1_out, 16 * (b + 1))
                if proj:
                    sp.dma_start(x_tok[:, :, :], x[b + 1].rearrange("(c p) n -> p c n", p=P)).then_inc(xtok_in, 16)
            run(sp, part)

        @block.tensor
        def _(pe):
            def split3(dst, lh, ll, rh, rl, first, last):
                nc.tensor.matmul(dst, lh, rh, start=first, stop=False)
                nc.tensor.matmul(dst, ll, rh, start=False, stop=False)
                return nc.tensor.matmul(dst, lh, rl, start=False, stop=last)

            def project_qk(b, c):
                first = isinstance(b, int) and b == 0 and c == 0
                if c == 0:
                    if not (isinstance(b, int) and b == 0):
                        pe.wait_ge(xs_hi, b)
                        pe.wait_ge(xs_lo, b)
                        pe.wait_ge(s_read, (NC - 1) * b)
                else:
                    pe.wait_ge(qk_read, NC * b + c)
                ts = slice(c * P, (c + 1) * P)
                for n in range(2):
                    for k in range(NK):
                        if first and n == 0:
                            pe.wait_ge(first_hi, k + 1)
                            pe.wait_ge(first_lo, k + 1)
                        cols = slice(n * D, (n + 1) * D)
                        last = split3(acc[:, n, :], x_h[:, k, ts], x_l[:, k, ts], wqk_h[:, k, cols],
                                      wqk_l[:, k, cols], k == 0, k == NK - 1)
                last.then_inc(qk_done, 1)

            def pass_bank(b, ret, proj, item):
                n = pass_order(ret, proj).index(item)
                wait(pe, pas_read, pass_base(b) + n - 1)
                return pas[n % 2]

            def project_v(b, c, bank):
                if isinstance(b, int) and b == 0 and c == 0:
                    pe.wait_ge(w_hi, 1)
                    pe.wait_ge(w_lo, 1)
                ts = slice(c * P, (c + 1) * P)
                for k in range(NK):
                    last = split3(bank[:, :], x_h[:, k, ts], x_l[:, k, ts], wvg_h[:, k, 0:D],
                                  wvg_l[:, k, 0:D], k == 0, k == NK - 1)
                last.then_inc(v_done, 1)

            def project_gate(b, p, bank):
                cols = slice(D + p * P, D + (p + 1) * P)
                for k in range(NK):
                    last = split3(bank[:, :], wvg_h[:, k, cols], wvg_l[:, k, cols], x_h[:, k, :],
                                  x_l[:, k, :], k == 0, k == NK - 1)
                last.then_inc(g_done, 1)

            def transpose_qk(b, t):
                if t == 0:
                    pe.wait_ge(rot_done, NC * (b + 1))
                    pe.wait_ge(qk_read, NC * (b + 1))
                    if isinstance(b, int) and b == 0:
                        pe.wait_ge(const_in, 16 * 6)
                if t >= 2:
                    pe.wait_ge(t_read, 2 * NP * b + t - 1)
                p = t // 2
                for c in range(NC):
                    src = qk_tok[:, c, t % 2, 2 * p:2 * p + 2, :].rearrange("p h d -> p (h d)")
                    last = nc.tensor.transpose(psc[t % 2][:, c, :], src, ident)
                last.then_inc(t_done, 1)

            def chunk_state(b, c, v3):
                if c == 0:
                    pe.wait_ge(pas_read, v3)
                if c == 2:
                    pe.wait_ge(s_read, (NC - 1) * b + 1)
                dst = acc[:, c % 2, :]
                for p in range(NP):
                    cols = slice(p * P, (p + 1) * P)
                    last = nc.tensor.matmul(dst[:, cols],
                                            qk_tok[:, c, 1, 2 * p:2 * p + 2, :].rearrange("p h d -> p (h d)"),
                                            v_tok[:, c, cols], start=True, stop=True)
                last.then_inc(s_done, 1)

            def scores(b, h):
                p, e = h // 2, h % 2
                if h == 0:
                    pe.wait_ge(t_read, 2 * NP * (b + 1))
                if h >= 2:
                    pe.wait_ge(sc_read, NH * b + h - 1)
                rows = slice(e * HD, (e + 1) * HD)
                for c in range(NC):
                    ts = slice(c * P, (c + 1) * P)
                    last = nc.tensor.matmul(psc[e][:, c, :], k_T[rows, p, ts], q_T[rows, p, ts],
                                            start=True, stop=True)
                last.then_inc(sc_done, 1)

            def retention(b, p):
                pe.wait_ge(sc_read, NH * b + 2 * p + 2)
                if p == 0:
                    pe.wait_ge(s_read, (NC - 1) * (b + 1))
                if p >= 2:
                    pe.wait_ge(aff_done, NP * b + p - 1)
                bank = pret[p % 2]
                for c in range(NC):
                    ts = slice(c * P, (c + 1) * P)
                    if c:
                        nc.tensor.matmul(bank[:, ts], state[:, c - 1, p, :], q_T[:, p, ts],
                                         start=True, stop=False, skip_group_check=True)
                    for e in range(2):
                        rows = slice(e * HD, (e + 1) * HD)
                        h = 2 * p + e
                        last = nc.tensor.matmul(bank[rows, ts], v_tok[:, c, h * HD:(h + 1) * HD],
                                                sc_T[:, h % 4, c, :], start=(c == 0), stop=True,
                                                skip_group_check=True)
                last.then_inc(r_done, 1)

            def head_stats(b, p, bank):
                pe.wait_ge(bn_done, NP * b + p + 1)
                nc.tensor.matmul(bank[:, 0:2], heads, mv[:, :], start=True, stop=True).then_inc(st_done, 1)

            def project_out(b, c):
                if c == 0:
                    pe.wait_ge(y_done, NP * (b + 1))
                    pe.wait_ge(w_lo, 2)
                    pe.wait_ge(w_hi, 2)
                if c >= 2:
                    pe.wait_ge(o_read, NC * b + c - 1)
                ts = slice(c * P, (c + 1) * P)
                dst = pret[c % 2]
                for p in range(NP):
                    last = split3(dst[:, :], y_h[:, p, ts], y_l[:, p, ts], wo_h[:, p, :], wo_l[:, p, :],
                                  p == 0, p == NP - 1)
                last.then_inc(o_done, 1)

            def part(b, ret, proj, more):
                order = pass_order(ret, proj)

                def stage(what, n):
                    if what == "T":
                        transpose_qk(b + 1, n)
                        return
                    bank = pass_bank(b, ret, proj, (what, n))
                    if what == "ST":
                        head_stats(b, n, bank)
                    elif what == "V":
                        project_v(b + 1, n, bank)
                    else:
                        project_gate(b + 1, n, bank)

                for p in range(NP):
                    if ret and p:
                        scores(b, 2 * p)
                        scores(b, 2 * p + 1)
                        stage("ST", p - 1)
                    if proj:
                        project_qk(b + 1, p)
                        if not ret and p:
                            stage("V", p - 1)
                    if ret:
                        retention(b, p)
                    if not proj:
                        prep.products(pe, PIECES_AT_PAIR[p])
                for what, n in then_order(ret, proj):
                    stage(what, n)
                if not proj:
                    prep.products(pe, PIECES_AT_NORM)
                for c in range(NC):
                    if ret:
                        project_out(b, c)
                    if proj and c < NC - 1:
                        chunk_state(b + 1, c, pass_base(b) + order.index(("V", 3)) + 1)
                    if not proj:
                        prep.products(pe, PIECES_AT_OUT[c])
                if proj:
                    scores(b + 1, 0)
                    scores(b + 1, 1)
            run(pe, part)

        @block.scalar
        def _(act):
            for k in range(NK):
                act.wait_ge(wx_in[k], 32)
                nc.scalar.activation(wqk_h[:, k, :], qk_tok[:, k, :, :, :].rearrange("p a h d -> p (a h d)"), ACT.Copy)
                nc.scalar.activation(x_h[:, k, :], x_raw[:, k, :], ACT.Copy).then_inc(first_hi, 1)
            act.wait_ge(wvg_in, 32)
            nc.scalar.activation(wvg_h[:, :, 0:D], gate[:, :, :], ACT.Copy)
            nc.scalar.activation(wvg_h[:, :, D:2 * D], v_tok[:, :, :], ACT.Copy).then_inc(w_hi, 1)
            act.wait_ge(wo_in, 16)
            nc.scalar.activation(wo_h[:, :, :], sc_T[:, :, :, :].rearrange("p a c q -> p a (c q)"),
                                 ACT.Copy).then_inc(w_hi, 1)
            act.wait_ge(w_lo, 2)

            def norm_pair(b, p):
                act.wait_ge(ab_done, NP * b + p + 1)
                if p >= 2:
                    act.wait_ge(y_done, NP * b + p - 1)
                nc.scalar.activation(y_t[:, p % 2, :], pret[p % 2][:, :], ACT.Identity, bias=ab_b[:, 0:1],
                                     scale=ab[:, 2:3]).then_inc(aff_done, 1)

            def read_stats(b, p, bank):
                act.wait_ge(st_done, NP * b + p + 1)
                nc.scalar.activation(hm[:, :], bank[:, 0:2], ACT.Copy).then_inc(pas_read, 1)

            def part(b, ret, proj, more):
                order = pass_order(ret, proj)

                def stage(what, i):
                    r = b + 1
                    if what == "T":
                        dst = (q_T, k_T)[i % 2]
                        act.wait_ge(t_done, 2 * NP * r + i + 1)
                        nc.scalar.activation(dst[:, i // 2, :], psc[i % 2][:, :, :], ACT.Copy).then_inc(t_read, 1)
                        return
                    bank = pas[order.index((what, i)) % 2]
                    if what == "ST":
                        read_stats(b, i, bank)
                    elif what == "V":
                        act.wait_ge(v_done, NC * r + i + 1)
                        nc.scalar.activation(v_tok[:, i, :], bank[:, :], ACT.Copy).then_inc(pas_read, 1)
                    else:
                        tmp = sc_T[:, i, :, :].rearrange("p c q -> p (c q)")
                        act.wait_ge(g_done, NP * r + i + 1)
                        if ret:
                            act.wait_ge(y_done, NP * b + i + 1)
                        nc.scalar.activation(tmp, bank[:, :], ACT.Tanh, scale=0.5).then_inc(act_link, 1)
                        nc.scalar.activation(gate[:, i, :], bank[:, :], ACT.Copy).then_inc(pas_read, 1)
                        act.wait_ge(act_link, 2 * NP * r + 2 * i + 1)
                        nc.scalar.activation(tmp, tmp, ACT.Square, bias=1.0, scale=-1.0).then_inc(act_link, 1)
                        act.wait_ge(act_link, 2 * NP * r + 2 * i + 2)
                        nc.scalar.activation(tmp, tmp, ACT.Identity, bias=4.0).then_inc(sq_done, 1)

                if ret:
                    for p in range(NP - 1):
                        stage("ST", p)
                        norm_pair(b, p)
                        if not proj and p == NP - 3:
                            prep.split_small(act)
                        if not proj:
                            prep.hi_parts(act, PIECES_AT_PAIR[p])
                    if not proj:
                        prep.hi_parts(act, PIECES_AT_PAIR[NP - 1])
                elif proj:
                    for c in range(NP - 1):
                        stage("V", c)
                for what, i in then_order(ret, proj):
                    stage(what, i)
                    if ret and (what, i) == (("V", 2) if proj else ("ST", 3)):
                        norm_pair(b, NP - 1)
                if not proj:
                    prep.hi_parts(act, PIECES_AT_NORM + sum(PIECES_AT_OUT))
                if more:
                    act.wait_ge(x_in, 16 * (b + 2))
                    act.wait_ge(g_done, NP * (b + 2))
                    nc.scalar.activation(x_h[:, :, :], x_raw[:, :, :], ACT.Copy).then_inc(xs_hi, 1)
            run(act, part)

        @block.vector
        def _(dve):
            def sub(dst, a, hi):
                return nc.vector.tensor_tensor(dst, a, hi.bitcast(F32), ALU.subtract)

            nc.vector.memset(half[:, :], -0.5).then_inc(init, 1)
            nc.vector.memset(state[:, :, :, :], 0.0).then_inc(dve_link, 1)
            for k in range(NK):
                dve.wait_ge(first_hi, k + 1)
                sub(wqk_l[:, k, :], qk_tok[:, k, :, :, :].rearrange("p a h d -> p (a h d)"), wqk_h[:, k, :])
                sub(x_l[:, k, :], x_raw[:, k, :], x_h[:, k, :]).then_inc(first_lo, 1)
            dve.wait_ge(w_hi, 1)
            sub(wvg_l[:, :, 0:D], gate[:, :, :], wvg_h[:, :, 0:D])
            sub(wvg_l[:, :, D:2 * D], v_tok[:, :, :], wvg_h[:, :, D:2 * D]).then_inc(w_lo, 1)
            dve.wait_ge(w_hi, 2)
            sub(wo_l[:, :, :], sc_T[:, :, :, :].rearrange("p a c q -> p a (c q)"), wo_h[:, :, :]).then_inc(w_lo, 1)
            dve.wait_ge(const_in, 16 * 6)
            dve.wait_ge(dve_link, 1)

            cos, sin = tab_s[:, :, 0:2 * ROT], tab_s[:, :, 2 * ROT:4 * ROT]
            dec = tab_s[:, :, 4 * ROT:4 * ROT + 2 * NH]
            base = [1]

            def mask_scores(b, h):
                dve.wait_ge(sc_done, NH * b + h + 1)
                if h >= 4:
                    dve.wait_ge(r_done, NP * b + (h - 4) // 2 + 1)
                nc.vector.tensor_tensor(sc_T[:, h % 4, :, :], psc[h % 2][:, :, :],
                                        causal.unsqueeze(1).to_broadcast([P, NC, P]), ALU.mult).then_inc(sc_read, 1)

            def rotate(b, c):
                dve.wait_ge(qk_done, NC * b + c + 1)
                wait(dve, rot_done, NC * b + c)
                ps = acc[:, :, :].rearrange("p a (h d) -> p a h d", h=NH)
                cs = cos[:, c, :].rearrange("p (a d) -> p a d", a=2).unsqueeze(2).to_broadcast([P, 2, NH, ROT])
                sn = sin[:, c, :].rearrange("p (a d) -> p a d", a=2).unsqueeze(2).to_broadcast([P, 2, NH, ROT])
                nc.vector.tensor_tensor(rot_a[:, :, :, :], ps[:, :, :, 0:ROT], cs, ALU.mult)
                nc.vector.tensor_tensor(rot_b[:, :, :, 0:ROT:2], ps[:, :, :, 1:ROT:2], sn[:, :, :, 0:ROT:2], ALU.mult)
                nc.vector.tensor_tensor(rot_b[:, :, :, 1:ROT:2], ps[:, :, :, 0:ROT:2], sn[:, :, :, 1:ROT:2], ALU.mult)
                dc = dec[:, c, :].rearrange("p (a h) -> p a h", a=2).unsqueeze(3).to_broadcast([P, 2, NH, HD - ROT])
                nc.vector.tensor_tensor(qk_tok[:, c, :, :, ROT:HD], ps[:, :, :, ROT:HD], dc, ALU.mult).then_inc(qk_read, 1)

            def pair_moments(b, p, link):
                dve.wait_ge(r_done, NP * b + p + 1)
                link(nc.vector.bn_stats(bn6[:, 0, :], pret[p % 2][:, :]))
                nc.vector.memset(pad[:, :], 0.0)
                link(nc.vector.bn_aggr(mv[:, :], bn6[:, 0, :]))
                nc.vector.scalar_tensor_tensor(mv[:, 1:2], mv[:, 0:1], mv[:, 0:1], mv[:, 1:2],
                                               ALU.mult, ALU.add).then_inc(bn_done, 1)

            def pair_variance(b, p, link, st):
                dve.wait_ge(pas_read, st)
                link(nc.vector.scalar_tensor_tensor(ab[:, 0:1], hm[:, 0:1], hm[:, 0:1], hm[:, 1:2],
                                                    ALU.mult, ALU.subtract))
                nc.vector.tensor_scalar(ab[:, 0:1], ab[:, 0:1], -1.0, EPS, ALU.mult, ALU.add).then_inc(ve_done, 1)

            def pair_affine(b, p, link):
                dve.wait_ge(rs_done, NP * b + p + 1)
                link(nc.vector.scalar_tensor_tensor(ab[:, 2:3], ab[:, 1:2], 8.0, gn_s[:, 0, p:p + 1], ALU.mult, ALU.mult))
                link(nc.vector.tensor_tensor(ab[:, 3:4], ab[:, 2:3], hm[:, 0:1], ALU.mult))
                nc.vector.scalar_tensor_tensor(ab_b[:, :], gn_s[:, 1, p:p + 1], 8.0, ab[:, 3:4],
                                               ALU.mult, ALU.subtract).then_inc(ab_done, 1)

            def gated(b, p, link):
                dve.wait_ge(aff_done, NP * b + p + 1)
                if p == 0:
                    dve.wait_ge(gate_done, NP * (b + 1))
                y = y_t[:, p % 2, :]
                link(nc.vector.tensor_tensor(y, y, gate[:, p, :], ALU.mult))
                link(nc.vector.tensor_copy(y_h[:, p, :], y))
                sub(y_l[:, p, :], y, y_h[:, p, :]).then_inc(y_done, 1)

            def finish_gate(b, p, link):
                tmp = sc_T[:, p, :, :].rearrange("p c q -> p (c q)")
                dve.wait_ge(sq_done, NP * b + p + 1)
                link(nc.vector.reciprocal(tmp, tmp))
                nc.vector.scalar_tensor_tensor(gate[:, p, :], tmp, -0.125, gate[:, p, :],
                                               ALU.add, ALU.mult).then_inc(gate_done, 1)

            def add_state(b, c):
                dve.wait_ge(s_done, (NC - 1) * b + c + 1)
                if c:
                    dve.wait_ge(s_read, (NC - 1) * b + c)
                ps = acc[:, c % 2, :].rearrange("p (q n) -> p q n", q=NP)
                for e in range(2):
                    half_ = slice(e * HD, (e + 1) * HD)
                    if c == 0:
                        last = nc.vector.tensor_copy(state[half_, 0, :, half_], ps[half_, :, half_])
                    else:
                        last = nc.vector.tensor_tensor(state[half_, c, :, half_], ps[half_, :, half_],
                                                       state[half_, c - 1, :, half_], ALU.add)
                last.then_inc(s_read, 1)

            def residual(b, c):
                dve.wait_ge(o_done, NC * b + c + 1)
                if c == 0:
                    dve.wait_ge(xtok_in, 16 * (b + 1))
                nc.vector.tensor_tensor(x_tok[:, c, :], pret[c % 2][:, :], x_tok[:, c, :],
                                        ALU.add).then_inc(o_read, 1)

            def layer_norm(b, link):
                dve.wait_ge(o_read, NC * (b + 1))
                for c in range(NC):
                    last = nc.vector.bn_stats(bn6[:, c, :], x_tok[:, c, :])
                link(last)
                nc.vector.memset(pad[:, :], 0.0)
                for c in range(NC):
                    last = nc.vector.bn_aggr(ln_mv[:, c, :], bn6[:, c, :])
                link(last)
                nc.vector.tensor_scalar(ln_ve[:, :], ln_mv[:, :, 1], EPS, None, ALU.add).then_inc(lnve_done, 1)
                dve.wait_ge(lnrs_done, b + 1)
                for c in range(NC):
                    last = nc.vector.tensor_scalar(x_tok[:, c, :], x_tok[:, c, :], ln_mv[:, c, 0:1],
                                                   ln_rs[:, c:c + 1], ALU.subtract, ALU.mult)
                last.then_inc(x1_done, 1)

            LINKS_PROJ, LINKS_RET = NP, NP * (2 + 1 + 2 + 2) + 2

            def part(b, ret, proj, more):
                first = isinstance(b, int) and b < 0
                link = Links(dve, dve_link, 1 if first else 1 + LINKS_PROJ + b * (LINKS_PROJ + LINKS_RET))
                order = pass_order(ret, proj)
                st = lambda p: pass_base(b) + order.index(("ST", p)) + 1
                for p in range(NP):
                    if ret and p:
                        mask_scores(b, 2 * p)
                        mask_scores(b, 2 * p + 1)
                        pair_variance(b, p - 1, link, st(p - 1))
                    if proj:
                        rotate(b + 1, p)
                    if ret:
                        if p:
                            pair_affine(b, p - 1, link)
                        pair_moments(b, p, link)
                        if p:
                            gated(b, p - 1, link)
                    if not proj:
                        prep.dequantise(dve, PIECES_AT_PAIR[p])
                if ret:
                    pair_variance(b, NP - 1, link, st(NP - 1))
                    pair_affine(b, NP - 1, link)
                    gated(b, NP - 1, link)
                if not proj:
                    prep.dequantise(dve, PIECES_AT_NORM)
                for c in range(NC):
                    if proj and c == 0:
                        for p in range(NP - 1):
                            finish_gate(b + 1, p, link)
                    if ret:
                        residual(b, c)
                    if proj and c < NC - 1:
                        add_state(b + 1, c)
                    if proj and c == 1:
                        finish_gate(b + 1, NP - 1, link)
                    if not proj:
                        prep.dequantise(dve, PIECES_AT_OUT[c])
                if proj:
                    mask_scores(b + 1, 0)
                    mask_scores(b + 1, 1)
                if ret:
                    layer_norm(b, link)
                assert link.n == LINKS_PROJ * proj + LINKS_RET * ret
            run(dve, part)

        @block.gpsimd
        def _(pool):
            pool.wait_ge(init, 1)
            pool.wait_ge(const_in, 16 * 6)

            def rotate(b, c):
                pool.wait_ge(qk_read, NC * b + c + 1)
                nc.gpsimd.tensor_tensor(rot_a[:, :, :, :], rot_a[:, :, :, :], rot_b[:, :, :, :],
                                        ALU.add).then_inc(pool_link, 1)
                pool.wait_ge(pool_link, NC * b + c + 1)
                dc = tab_s[:, c, 4 * ROT:4 * ROT + 2 * NH].rearrange("p (a h) -> p a h", a=2)\
                    .unsqueeze(3).to_broadcast([P, 2, NH, ROT])
                nc.gpsimd.tensor_tensor(qk_tok[:, c, :, :, 0:ROT], rot_a[:, :, :, :], dc, ALU.mult).then_inc(rot_done, 1)

            def rstd(b, p):
                pool.wait_ge(ve_done, NP * b + p + 1)
                nc.gpsimd.tensor_tensor(ab[:, 1:2], ab[:, 0:1], half[:, 0:1], ALU.pow).then_inc(rs_done, 1)

            def part(b, ret, proj, more):
                for p in range(NP):
                    if ret and p:
                        rstd(b, p - 1)
                    if proj:
                        rotate(b + 1, p)
                    if not proj and p == NP - 2:
                        prep.split_small_lo(pool)
                    if not proj and p:
                        prep.lo_parts(pool, PIECES_AT_PAIR[p - 1])
                if ret:
                    rstd(b, NP - 1)
                if not proj:
                    prep.lo_parts(pool, PIECES_AT_PAIR[NP - 1] + PIECES_AT_NORM + sum(PIECES_AT_OUT))
                if more:
                    pool.wait_ge(xs_hi, b + 2)
                    nc.gpsimd.tensor_tensor(x_l[:, :, :], x_raw[:, :, :], x_h[:, :, :].bitcast(F32),
                                            ALU.subtract).then_inc(xs_lo, 1)
                if ret:
                    pool.wait_ge(lnve_done, b + 1)
                    nc.gpsimd.tensor_tensor(ln_rs[:, :], ln_ve[:, :], half[:, :], ALU.pow).then_inc(lnrs_done, 1)
            run(pool, part)


def ffn_rows(nc, wu_h, wu_l, ctxT, ctx_in, mask, bup, qdn, sdn, bdn, adn, bdnl, consts, seldn, x1s, out):
    with ExitStack() as stack:
        def sb(name, shape, dt=F32):
            return stack.enter_context(nc.sbuf_tensor(name, shape, dt))

        def pb(name, shape):
            return stack.enter_context(nc.psum_tensor(name, shape, F32))

        def sem(name):
            return stack.enter_context(nc.semaphore(name))

        NHID = 2
        wd_h, wd_l = sb("wd_h", [P, NF, D], F32R), sb("wd_l", [P, NF, D], F32R)
        w_new = sb("w_new", [P, 4, 512])
        bup_s, bdn_s = sb("bup_s", [P, NF]), sb("bdn_s", [P, D])
        x1 = sb("x1", [P, NC, D])
        x1_T = sb("x1_T", [P, NK, S])
        x2_h, x2_l = sb("x2_h", [P, NK, S], F32R), sb("x2_l", [P, NK, S], F32R)
        x2b = sb("x2b", [P, NC, D])
        hid = sb("hid", [P, 2, S])
        hid_h, hid_l = sb("hid_h", [P, NHID, S], F32R), sb("hid_l", [P, NHID, S], F32R)
        z_out = sb("z_out", [P, 2, D])
        ctx_T, ctx_s = sb("ctx_T", [P, NK, M]), sb("ctx_s", [P, D])
        ctx_h, ctx_l = sb("ctx_h", [P, D], F32R), sb("ctx_l", [P, D], F32R)
        mask_s = sb("mask_s", [P, M], U8)
        keep, bias, valid = sb("keep", [P, M]), sb("bias", [P, M]), sb("valid", [P, 1])
        sm, smax, ssum = sb("sm", [P, NC, M]), sb("smax", [P, NC]), sb("ssum", [P, NC])
        p_Th, p_Tl = sb("p_Th", [P, 2 * P], F32R), sb("p_Tl", [P, 2 * P], F32R)
        ident_s = sb("ident_s", [P, P])
        half2 = sb("half2", [P, NC])
        pad2 = sb("pad2", [P, 1])
        bn6 = sb("bn6b", [P, NC, 6])
        ln_mv, ln_ve, ln_rs = sb("ln_mv2", [P, NC, 2]), sb("ln_ve2", [P, NC]), sb("ln_rs2", [P, NC])
        fn_mv, fn_ve, fn_rs = sb("fn_mv", [P, NC, 2]), sb("fn_ve", [P, NC]), sb("fn_rs", [P, NC])
        pdn = [pb(f"pdn{i}", [P, 512]) for i in range(NC)]
        pup = [pb(f"pup{i}", [P, 512]) for i in range(2)]
        pxa = [pb(f"pxa{i}", [P, 512]) for i in range(2)]

        x1_in, ctx_inn, z_free = sem("x1_in"), sem("ctx_inn"), [sem("z_free0"), sem("z_free1")]
        init = sem("init2")
        t1_done, sc_done, ta_done, rd_done, t2_done, up_done, dn_done = map(
            sem, ("t1_done", "xsc_done", "ta_done", "rd_done", "t2_done", "up_done", "dn_done"))
        t1_read, ctxh_done, ta_hi, exp_done, t2_hi, hid_done = map(
            sem, ("t1_read", "ctxh_done", "ta_hi", "exp_done", "t2_hi", "hid_done"))
        ctxl_done, mask_done, shift_done, prob_done, ta_lo, rd_read, lnve_done, x2_done, t2_lo, hidl_done = map(
            sem, ("ctxl_done", "mask_done", "shift_done", "prob_done", "ta_lo", "rd_read", "xlnve_done", "x2_done",
                  "t2_lo", "hidl_done"))
        pdn_free, fnve_done, z_done = sem("pdn_free"), sem("fnve_done"), sem("z_done")
        lnrs_done, x2b_done, fnrs_done = sem("xlnrs_done"), sem("x2b_done"), sem("fnrs_done")
        dve_link, bias_in = sem("dve_link2"), sem("bias_in")

        prep = Prep(nc, sem, "down", NF,
                    q=[t[:, n, :].bitcast(I32) for t in (hid, z_out) for n in range(2)],
                    w=[w_new[:, n, :] for n in range(4)],
                    raw=[x1_T[:, 0, :], x1_T[:, 1, :], x2b[:, :, :].rearrange("p c n -> p (c n)"),
                         w_new[:, :, :].rearrange("p n c -> p (n c)")],
                    st=[hid_h[:, 0, :], hid_h[:, 1, :], x2_l[:, :, :].rearrange("p k t -> p (k t)"),
                        x2_h[:, :, :].rearrange("p k t -> p (k t)")],
                    scale=[pdn[0][:, :], pdn[1][:, :]], lora=[pdn[2][:, :], pdn[3][:, :]],
                    source=[sdn, bdnl, adn, seldn], piece=lambda n: down_piece(n, qdn, wd_h, wd_l))
        block = stack.enter_context(nc.Block())

        def first_row(b):
            return isinstance(b, int) and b == 0

        def run(eng, part):
            part(-1, False, True)
            with eng.Fori(0, B - 1) as b:
                part(b, True, True)
            part(B - 1, True, False)

        @block.sync
        def _(sp):
            for n, z in enumerate(z_free):
                cols = slice(n * HD, (n + 1) * HD)
                sp.dma_start(ident_s[:, cols], consts[:, 2 * P + n * HD:2 * P + (n + 1) * HD]).then_inc(z, 16)

            sp.dma_start(bup_s[:, :], bup).then_inc(bias_in, 16)
            sp.dma_start(bdn_s[:, :], bdn.to_broadcast([P, D])).then_inc(bias_in, 16)
            prep.load_small(sp)

            def part(b, ffn, xattn):
                if xattn:
                    if ffn:
                        sp.wait_ge(x2b_done, b + 1)
                    sp.dma_start(x1[:, :, :], x1s[b + 1].rearrange("(c p) n -> p c n", p=P)).then_inc(x1_in, 16)
                    sp.dma_start(ctx_T[:, :, :], ctxT[b + 1].rearrange("(k p) m -> p k m", p=P)).then_inc(ctx_inn, 16)
                    for half in range(2):
                        sp.dma_start(ctx_s[half * M:(half + 1) * M, :], ctx_in[b + 1]).then_inc(ctx_inn, 16)
                    sp.dma_start(mask_s[:, :], mask[b + 1].to_broadcast([P, M])).then_inc(ctx_inn, 16)
                    if not ffn:
                        prep.load(sp)
                if ffn:
                    for c in range(NC):
                        sp.wait_ge(z_done, NC * b + c + 1)
                        sp.dma_start(out[b, c * P:(c + 1) * P, :], z_out[:, c % 2, :]).then_inc(z_free[c % 2], 16)
            run(sp, part)
            for z in z_free:
                sp.wait_ge(z, 16 * (B * NC // 2 + 1))

        @block.tensor
        def _(pe):
            def split3(dst, lh, ll, rh, rl, first, last):
                nc.tensor.matmul(dst, lh, rh, start=first, stop=False)
                nc.tensor.matmul(dst, ll, rh, start=False, stop=False)
                return nc.tensor.matmul(dst, lh, rl, start=False, stop=last)

            for z in z_free:
                pe.wait_ge(z, 16)

            def transpose_x1(b, k):
                if k == 0:
                    pe.wait_ge(x1_in, 16 * (b + 1))
                if k >= 2:
                    pe.wait_ge(t1_read, NK * b + k - 1)
                for c in range(NC):
                    last = nc.tensor.transpose(pxa[k % 2][:, c * P:(c + 1) * P], x1[:, c, k * P:(k + 1) * P], ident_s[:, :])
                last.then_inc(t1_done, 1)

            def scores(b):
                pe.wait_ge(t1_read, NK * (b + 1))
                pe.wait_ge(ctx_inn, 64 * (b + 1))
                for c in range(NC):
                    for k in range(NK):
                        last = nc.tensor.matmul(pxa[0][:, c * M:(c + 1) * M], x1_T[:, k, c * P:(c + 1) * P],
                                                ctx_T[:, k, :], start=(k == 0), stop=(k == NK - 1))
                last.then_inc(sc_done, 1)

            def transpose_probs(b):
                pe.wait_ge(exp_done, b + 1)
                for a in range(2):
                    last = nc.tensor.transpose(pxa[1][:, a * P:(a + 1) * P],
                                               sm[:, 2 * a:2 * a + 2, :].rearrange("p c m -> p (c m)"), ident_s[:, :])
                last.then_inc(ta_done, 1)

            def read_memory(b, c):
                if c == 0:
                    pe.wait_ge(ta_hi, b + 1)
                    pe.wait_ge(ta_lo, b + 1)
                    pe.wait_ge(ctxl_done, b + 1)
                if c >= 2:
                    pe.wait_ge(rd_read, NC * b + c - 1)
                rows, ts = slice((c % 2) * M, (c % 2 + 1) * M), slice(c // 2 * P, (c // 2 + 1) * P)
                split3(pxa[c % 2][:, :], p_Th[rows, ts], p_Tl[rows, ts], ctx_h[rows, :], ctx_l[rows, :], True, True).then_inc(rd_done, 1)

            def transpose_x2(b, k):
                if k == 0:
                    pe.wait_ge(x2_done, b + 1)
                if k >= 2:
                    pe.wait_ge(t2_hi, NK * b + k - 1)
                    pe.wait_ge(t2_lo, NK * b + k - 1)
                for c in range(NC):
                    last = nc.tensor.transpose(pxa[k % 2][:, c * P:(c + 1) * P], x1[:, c, k * P:(k + 1) * P], ident_s[:, :])
                last.then_inc(t2_done, 1)

            def up(b, f):
                if f == 0:
                    pe.wait_ge(t2_hi, NK * (b + 1))
                    pe.wait_ge(t2_lo, NK * (b + 1))
                if f >= 2 or not first_row(b):
                    pe.wait_ge(hid_done, NF * b + f - 1)
                fs = slice(f * P, (f + 1) * P)
                for k in range(NK):
                    last = split3(pup[f % 2][:, :], wu_h[:, k, fs], wu_l[:, k, fs], x2_h[:, k, :], x2_l[:, k, :],
                                  k == 0, k == NK - 1)
                last.then_inc(up_done, 1)

            def down(b, f):
                pe.wait_ge(hidl_done, NF * b + f + 1)
                if f == 0 and first_row(b):
                    pe.wait_ge(prep.w_done, NF)
                    pe.wait_ge(prep.hi_done, NF)
                    pe.wait_ge(prep.lo_done, NF)
                if f == 0 and not first_row(b):
                    pe.wait_ge(pdn_free, NC * b)
                for c in range(NC):
                    ts = slice(c * P, (c + 1) * P)
                    last = split3(pdn[c][:, :], hid_h[:, f % NHID, ts], hid_l[:, f % NHID, ts], wd_h[:, f, :],
                                  wd_l[:, f, :], f == 0, f == NF - 1)
                last.then_inc(dn_done, 1)

            def part(b, ffn, xattn):
                def beside(f):
                    if not xattn:
                        return
                    if 4 <= f < 6:
                        transpose_x1(b + 1, 2 * (f - 4))
                        transpose_x1(b + 1, 2 * (f - 4) + 1)
                    if f == 6:
                        scores(b + 1)
                    if f == 8:
                        transpose_probs(b + 1)
                    if 9 <= f < 13:
                        read_memory(b + 1, f - 9)
                for f in range(HEAD, NF):
                    if ffn:
                        up(b, f)
                    beside(f)
                    if ffn:
                        down(b, f - 1)
                    else:
                        prep.products(pe, PIECES_BESIDE.get(f, 0))
                if xattn:
                    for k in range(NK):
                        transpose_x2(b + 1, k)
                if ffn:
                    down(b, NF - 1)
                if xattn:
                    for f in range(HEAD):
                        up(b + 1, f)
                        if f:
                            down(b + 1, f - 1)
            run(pe, part)

        @block.scalar
        def _(act):
            prep.split_small(act)
            act.wait_ge(prep.st_lo, 3)
            act.wait_ge(bias_in, 32)

            def relu(b, f):
                act.wait_ge(up_done, NF * b + f + 1)
                if f >= 2 or not first_row(b):
                    act.wait_ge(hidl_done, NF * b + f - 1)
                    act.wait_ge(dn_done, NF * b + f - 1)
                nc.scalar.activation(hid[:, f % 2, :], pup[f % 2][:, :], ACT.Relu, bias=bup_s[:, f:f + 1])
                nc.scalar.activation(hid_h[:, f % NHID, :], pup[f % 2][:, :], ACT.Relu,
                                     bias=bup_s[:, f:f + 1]).then_inc(hid_done, 1)

            def part(b, ffn, xattn):
                r = b + 1

                def beside(f):
                    if not xattn:
                        return
                    if f == 3:
                        act.wait_ge(ctx_inn, 64 * (r + 1))
                        nc.scalar.activation(ctx_h[:, :], ctx_s[:, :], ACT.Copy).then_inc(ctxh_done, 1)
                    if 4 <= f < 6:
                        for k in (2 * (f - 4), 2 * (f - 4) + 1):
                            act.wait_ge(t1_done, NK * r + k + 1)
                            nc.scalar.activation(x1_T[:, k, :], pxa[k % 2][:, :], ACT.Copy).then_inc(t1_read, 1)
                    if f == 7:
                        act.wait_ge(shift_done, r + 1)
                        nc.scalar.activation(sm[:, :, :], sm[:, :, :], ACT.Exp).then_inc(exp_done, 1)
                    if f == 8:
                        act.wait_ge(ta_done, r + 1)
                        nc.scalar.activation(p_Th[:, :], pxa[1][:, 0:2 * P], ACT.Copy).then_inc(ta_hi, 1)
                for f in range(HEAD, NF):
                    if ffn:
                        relu(b, f)
                    beside(f)
                    if not ffn:
                        prep.hi_parts(act, PIECES_BESIDE.get(f, 0))
                if xattn:
                    for k in range(NK):
                        act.wait_ge(t2_done, NK * r + k + 1)
                        nc.scalar.activation(x2_h[:, k, :], pxa[k % 2][:, :], ACT.Copy).then_inc(t2_hi, 1)
                    for f in range(HEAD):
                        relu(r, f)
            run(act, part)

        @block.vector
        def _(dve):
            def sub(dst, a, hi):
                return nc.vector.tensor_tensor(dst, a, hi.bitcast(F32), ALU.subtract)

            nc.vector.memset(half2[:, :], -0.5).then_inc(init, 1)
            LINKS_X, LINKS_F = 6, 2

            def masks(b, link):
                dve.wait_ge(ctx_inn, 64 * (b + 1))
                link(nc.vector.tensor_copy(keep[:, :], mask_s[:, :]))
                nc.vector.tensor_scalar(bias[:, :], keep[:, :], -1.0, NEG, ALU.add, ALU.mult)
                nc.vector.reduce_max(valid[:, :], keep[:, :], AX.X).then_inc(mask_done, 1)
                dve.wait_ge(ctxh_done, b + 1)
                sub(ctx_l[:, :], ctx_s[:, :], ctx_h[:, :]).then_inc(ctxl_done, 1)

            def softmax_shift(b, link):
                dve.wait_ge(sc_done, b + 1)
                dve.wait_ge(mask_done, b + 1)
                kp = keep[:, :].unsqueeze(1).to_broadcast([P, NC, M])
                bs = bias[:, :].unsqueeze(1).to_broadcast([P, NC, M])
                ps = pxa[0][:, 0:NC * M].rearrange("p (c m) -> p c m", c=NC)
                link(nc.vector.scalar_tensor_tensor(sm[:, :, :], ps, float(np.float32(1.0) / np.sqrt(np.float32(D))), kp,
                                                    ALU.mult, ALU.mult))
                link(nc.vector.tensor_tensor(sm[:, :, :], sm[:, :, :], bs, ALU.add))
                link(nc.vector.reduce_max(smax[:, :], sm[:, :, :], AX.X))
                nc.vector.tensor_tensor(sm[:, :, :], sm[:, :, :], smax[:, :].unsqueeze(2).to_broadcast([P, NC, M]),
                                        ALU.subtract).then_inc(shift_done, 1)

            def softmax_sum(b, link):
                dve.wait_ge(exp_done, b + 1)
                nc.vector.reduce_sum(ssum[:, :], sm[:, :, :], AX.X).then_inc(prob_done, 1)
                dve.wait_ge(prob_done, 3 * b + 1)
                nc.vector.reciprocal(ssum[:, :], ssum[:, :]).then_inc(prob_done, 1)
                dve.wait_ge(prob_done, 3 * b + 2)
                nc.vector.tensor_scalar(ssum[:, :], ssum[:, :], valid[:, 0:1], None, ALU.mult).then_inc(prob_done, 1)

            def hid_lo(b, f):
                dve.wait_ge(hid_done, NF * b + f + 1)
                if f >= 2 or not first_row(b):
                    dve.wait_ge(dn_done, NF * b + f - 1)
                sub(hid_l[:, f % NHID, :], hid[:, f % 2, :], hid_h[:, f % NHID, :]).then_inc(hidl_done, 1)

            def part(b, ffn, xattn):
                r = b + 1
                first = isinstance(b, int) and b < 0
                link = Links(dve, dve_link, 0 if first else LINKS_X + b * (LINKS_X + LINKS_F))

                def beside(f):
                    if not xattn:
                        return
                    if f == 3:
                        masks(r, link)
                    if f == 6:
                        softmax_shift(r, link)
                    if f == 8:
                        softmax_sum(r, link)
                        dve.wait_ge(ta_hi, r + 1)
                        sub(p_Tl[:, :], pxa[1][:, 0:2 * P], p_Th[:, :]).then_inc(ta_lo, 1)
                    if 9 <= f < 13:
                        c = f - 9
                        dve.wait_ge(rd_done, NC * r + c + 1)
                        if c == 0:
                            dve.wait_ge(prob_done, 3 * (r + 1))
                        nc.vector.scalar_tensor_tensor(x1[:, c, :], pxa[c % 2][:, :], ssum[:, c:c + 1], x1[:, c, :],
                                                       ALU.mult, ALU.add).then_inc(rd_read, 1)
                    if f == 13:
                        dve.wait_ge(rd_read, NC * (r + 1))
                        for c in range(NC):
                            last = nc.vector.bn_stats(bn6[:, c, :], x1[:, c, :])
                        link(last)
                        nc.vector.memset(pad2[:, :], 0.0)
                        for c in range(NC):
                            last = nc.vector.bn_aggr(ln_mv[:, c, :], bn6[:, c, :])
                        link(last)
                        nc.vector.tensor_scalar(ln_ve[:, :], ln_mv[:, :, 1], EPS, None, ALU.add).then_inc(lnve_done, 1)
                    if f == 14:
                        dve.wait_ge(lnrs_done, r + 1)
                        for c in range(NC):
                            last = nc.vector.tensor_scalar(x1[:, c, :], x1[:, c, :], ln_mv[:, c, 0:1],
                                                           ln_rs[:, c:c + 1], ALU.subtract, ALU.mult)
                        last.then_inc(x2_done, 1)
                for f in range(HEAD, NF):
                    if ffn:
                        hid_lo(b, f)
                    beside(f)
                    if not ffn:
                        prep.dequantise(dve, PIECES_BESIDE.get(f, 0))
                if xattn:
                    for k in range(NK):
                        dve.wait_ge(t2_hi, NK * r + k + 1)
                        sub(x2_l[:, k, :], pxa[k % 2][:, :], x2_h[:, k, :]).then_inc(t2_lo, 1)
                if ffn:
                    dve.wait_ge(dn_done, NF * (b + 1))
                    dve.wait_ge(x2b_done, b + 1)
                    for c in range(NC):
                        nc.vector.tensor_tensor(x2b[:, c, :], pdn[c][:, :], x2b[:, c, :], ALU.add).then_inc(pdn_free, 1)
                if xattn:
                    hid_lo(r, 0)
                if ffn:
                    dve.wait_ge(pdn_free, NC * (b + 1))
                    for c in range(NC):
                        last = nc.vector.bn_stats(bn6[:, c, :], x2b[:, c, :])
                    link(last)
                    nc.vector.memset(pad2[:, :], 0.0)
                    for c in range(NC):
                        last = nc.vector.bn_aggr(fn_mv[:, c, :], bn6[:, c, :])
                    link(last)
                    nc.vector.tensor_scalar(fn_ve[:, :], fn_mv[:, :, 1], EPS, None, ALU.add).then_inc(fnve_done, 1)
                if xattn:
                    hid_lo(r, 1)
                if ffn:
                    dve.wait_ge(fnrs_done, b + 1)
                    for c in range(NC):
                        dve.wait_ge(z_free[c % 2], 16 * (2 * b + 1 + c // 2))
                        nc.vector.tensor_scalar(z_out[:, c % 2, :], x2b[:, c, :], fn_mv[:, c, 0:1], fn_rs[:, c:c + 1],
                                                ALU.subtract, ALU.mult).then_inc(z_done, 1)
                assert link.n == LINKS_X * xattn + LINKS_F * ffn
            run(dve, part)

        @block.gpsimd
        def _(pool):
            prep.split_small_lo(pool)
            pool.wait_ge(init, 1)
            pool.wait_ge(bias_in, 32)

            def part(b, ffn, xattn):
                for f in range(HEAD, NF):
                    if xattn and f == 13:
                        pool.wait_ge(lnve_done, b + 2)
                        nc.gpsimd.tensor_tensor(ln_rs[:, :], ln_ve[:, :], half2[:, :], ALU.pow).then_inc(lnrs_done, 1)
                    if not ffn:
                        prep.lo_parts(pool, PIECES_BESIDE.get(f, 0))
                if ffn:
                    pool.wait_ge(fnve_done, b + 1)
                    nc.gpsimd.tensor_tensor(fn_rs[:, :], fn_ve[:, :], half2[:, :], ALU.pow).then_inc(fnrs_done, 1)
                if xattn:
                    pool.wait_ge(t2_done, NK * (b + 2))
                    if ffn:
                        pool.wait_ge(z_done, NC * (b + 1))
                    for c in range(NC):
                        last = nc.gpsimd.tensor_tensor(x2b[:, c, :], x1[:, c, :], bdn_s[:, :], ALU.add)
                    last.then_inc(x2b_done, 1)
            run(pool, part)


def kernel(**inputs):
    import numpy as _np
    import concourse.bacc as _bacc
    from concourse import mybir as _mybir
    from concourse.bass_utils import run_bass_kernel_spmd as _run

    a = {k: _np.asarray(v) for k, v in inputs.items()}
    c = _np.ascontiguousarray
    x = a["x"]
    w = a["L0_attn_wqkv"].reshape(NH, 3, HD, D)
    wT = w.transpose(3, 1, 0, 2).reshape(D, 3 * D)
    tab, consts = tables()
    arrays = {
        "xT": c(x.transpose(0, 2, 1)), "x": c(x),
        "ctxT": c(a["ctx_2048"].transpose(0, 2, 1)), "ctx_in": c(a["ctx_2048"]),
        "mask": c(a["mask_BxS2_bk0"].reshape(B, 1, M)),
        "wqkT": c(wT[:, 0:2 * D]),
        "wvgT": c(_np.concatenate([wT[:, 2 * D:], a["L0_attn_wg"].T], axis=1)),
        "woT": c(a["L0_attn_wo"].T),
        "gnw": c(a["L0_attn_gn_weight"].reshape(NP, 2).T), "gnb": c(a["L0_attn_gn_bias"].reshape(NP, 2).T),
        "qup": c(a["L0_ffn_w_up_q"].T), "sup": stacked(a["L0_ffn_w_up_scale"].T, S_AT, SK),
        "bup": c(a["L0_ffn_b_up"].reshape(NF, P).T),
        "aup": stacked(a["L0_ffn_w_up_lora_a"].T, L_AT, LK), "bupl": stacked(a["L0_ffn_w_up_lora_b"], L_AT, LK),
        "qdn": c(a["L0_ffn_w_down_q"].T), "sdn": stacked(a["L0_ffn_w_down_scale"].T, S_AT, SK),
        "bdn": c(a["L0_ffn_b_down"].reshape(1, D)),
        "adn": stacked(a["L0_ffn_w_down_lora_a"].T, L_AT, LK), "bdnl": stacked(a["L0_ffn_w_down_lora_b"], L_AT, LK),
        "tab": tab, "consts": consts, "selup": stacked(selector(NK), S_AT, SK), "seldn": stacked(selector(NF), S_AT, SK),
    }
    nc = _bacc.Bacc("TRN2", target_bir_lowering=False, num_devices=1)
    args = [nc.dram_tensor(f"in_{k}", v.shape, _mybir.dt.from_np(v.dtype), kind="ExternalInput").ap()
            for k, v in arrays.items()]
    out = nc.dram_tensor("out_0", (B, S, D), F32, kind="ExternalOutput").ap()
    x1s = nc.dram_tensor("x1_scratch", (B, S, D), F32, kind="Internal").ap()
    decoder_kernel(nc, *args, out, x1s)
    r = _run(nc, [{f"in_{k}": v for k, v in arrays.items()}], core_ids=[0])
    return r.results[0]["out_0"]
```

```python
import numpy as np
import concourse.bass as bass
from concourse import mybir
from contextlib import ExitStack

F32 = mybir.dt.float32
F32R = mybir.dt.float32r
I32 = mybir.dt.int32
U8 = mybir.dt.uint8
ALU = mybir.AluOpType
ACT = mybir.ActivationFunctionType
AX = mybir.AxisListType

B, S, D = 8, 512, 512
P = 128
NH, HD, ROT = 8, 64, 32
NC = S // P
NK = D // P
NP = NH // 2
M = 64
FF = 2048
NF = FF // P
QB = 64
R = 16
EPS = 1e-5
NEG = 1e30

PASS_PROJ = [("G", p) for p in range(NP)] + [("V", c) for c in range(NC)]
PASS_BOTH = [("ST", 0), ("ST", 1), ("ST", 2), ("G", 0), ("V", 0), ("ST", 3), ("G", 1), ("V", 1), ("G", 2), ("V", 2),
             ("G", 3), ("V", 3)]
PASS_RET = [("ST", p) for p in range(NP)]
THEN_BOTH = [("G", 0), ("V", 0), ("ST", 3), ("T", 0), ("T", 1), ("G", 1), ("T", 2), ("V", 1), ("T", 3), ("G", 2),
             ("T", 4), ("V", 2), ("T", 5), ("G", 3), ("T", 6), ("V", 3), ("T", 7)]
THEN_PROJ = [("G", 3), ("V", 0), ("T", 0), ("T", 1), ("V", 1), ("T", 2), ("T", 3), ("V", 2), ("T", 4), ("T", 5),
             ("V", 3), ("T", 6), ("T", 7)]
THEN_RET = [("ST", 3)]


def pass_order(ret, proj):
    return PASS_BOTH if ret and proj else PASS_PROJ if proj else PASS_RET


def then_order(ret, proj):
    return THEN_BOTH if ret and proj else THEN_PROJ if proj else THEN_RET


def pass_base(b):
    return 0 if isinstance(b, int) and b < 0 else b * len(PASS_BOTH) + len(PASS_PROJ)


def tables():
    f = np.float32
    inv = (f(1.0) / (f(10000.0) ** (np.arange(0, ROT, 2, dtype=f) / f(ROT)))).astype(f)
    t = np.arange(S, dtype=f)
    ang = (t[:, None] * inv[None, :]).astype(f)
    ang = np.repeat(ang, 2, axis=-1).astype(np.float64)
    base = ((np.arange(0, ROT, 2, dtype=f) + f(0.4 * ROT)) / f(1.4 * ROT)).astype(np.float64)
    power = ((t - S // 2) / f(512.0)).astype(np.float64)
    sc = base[None, :] ** power[:, None]
    sc = np.concatenate([sc, sc], axis=-1)
    sign = np.tile([-1.0, 1.0], ROT // 2)
    rot = np.zeros((S, 2, 2, ROT))
    for n, s_ in enumerate((sc, 1.0 / sc)):
        rot[:, 0, n] = np.cos(ang) * s_
        rot[:, 1, n] = np.sin(ang) * s_ * sign
    gamma = 1.0 - 2.0 ** (-5.0 - np.arange(NH))
    dist = np.arange(S) - S // 2
    dec = np.stack([gamma[None] ** dist[:, None], gamma[None] ** -dist[:, None]], axis=1)
    tab = np.concatenate([rot.reshape(S, -1), dec.reshape(S, -1)], axis=1)
    tab = tab.reshape(NC, P, -1).transpose(1, 0, 2)
    j, i = np.arange(P)[:, None], np.arange(P)[None, :]
    causal = (j <= i).astype(f)
    heads = np.where((j // HD) == (i // HD), 1.0 / HD, 0.0).astype(f)
    return np.ascontiguousarray(tab.astype(f)), np.concatenate([causal, heads, np.eye(P, dtype=f)], axis=1)


def stacked(a, rows, total):
    out = np.zeros((total, a.shape[1]), a.dtype)
    for r in rows:
        out[r:r + a.shape[0]] = a
    return out


def wait(eng, sem, value):
    if isinstance(value, int) and value <= 0:
        return
    eng.wait_ge(sem, value)


class Links:

    def __init__(self, eng, sem, base):
        self.eng, self.sem, self.base, self.n = eng, sem, base, 0

    def __call__(self, ins):
        ins.then_inc(self.sem, 1)
        self.n += 1
        self.eng.wait_ge(self.sem, self.base + self.n)


def decoder_kernel(nc, xT, x, ctxT, ctx_in, mask, wqkT, wvgT, woT, gnw, gnb, qup, sup, bup, aup, bupl,
                   qdn, sdn, bdn, adn, bdnl, tab, consts, out, x1s):
    with nc.sbuf_tensor("w1_h", [P, NK, FF], F32R) as w1_h, nc.sbuf_tensor("w1_l", [P, NK, FF], F32R) as w1_l, \
            nc.sbuf_tensor("x_tok", [P, NC, D], F32) as x_tok:
        retention_phase(nc, w1_h, w1_l, x_tok, xT, x, wqkT, wvgT, woT, gnw, gnb, tab, consts, x1s, qup, sup, aup,
                        bupl)
        ffn_rows(nc, w1_h, w1_l, x_tok, ctxT, ctx_in, mask, bup, qdn, sdn, bdn, adn, bdnl, consts, x1s, out)


LK = 64 + R
L_AT = (0, 32, 64)
PIECES_BEFORE_PAIR, PIECES_AT_PAIR, PIECES_AT_NORM, PIECES_AT_OUT = [0, 2, 2, 2], [2, 1, 1, 1], 2, [1, 1, 1, 0]
PIECES_BESIDE = {7: 3, 8: 3, 9: 1, 10: 1, 11: 1, 12: 1, 13: 2}
PIECES_AHEAD = 4
HEAD = 2


def up_piece(n, qup, sup, w_h, w_l):
    k, f = divmod(n, FF // 512)
    cols = slice(f * 512, (f + 1) * 512)
    return qup[k * P:(k + 1) * P, cols], sup[2 * k:2 * k + 2, cols], f * 512, k * P, w_h[:, k, cols], w_l[:, k, cols]


def down_piece(t, qdn, sdn, w_h, w_l):
    return qdn[t * P:(t + 1) * P, :], sdn[2 * t:2 * t + 2, :], 0, t * P, w_h[:, t, :], w_l[:, t, :]


class Prep:

    def __init__(self, nc, sem, name, pieces, q, s, w, raw, st, lora, source, piece):
        self.nc, self.pieces, self.q, self.s, self.w, self.raw, self.st = nc, pieces, q, s, w, raw, st
        self.lora, self.source, self.piece = lora, source, piece
        self.small_in, self.q_in = sem(f"{name}_small_in"), [sem(f"{name}_q_in{i}") for i in range(len(q))]
        (self.st_hi, self.st_lo, self.lora_done, self.deq_done, self.w_done, self.hi_done, self.lo_done) = (
            sem(f"{name}_{x}") for x in ("st_hi", "st_lo", "lora_done", "deq_done", "w_done", "hi_done", "lo_done"))
        self.at = {x: 0 for x in ("load", "pe", "dve", "act", "pool")}

    def next(self, who, count):
        first = self.at[who]
        self.at[who] += count
        assert self.at[who] <= self.pieces
        return range(first, first + count)

    def load_small(self, eng):
        for dst, src in zip(self.raw, self.source):
            rows, cols = src.shape
            eng.dma_start(dst[0:rows, 0:cols], src).then_inc(self.small_in, 16)

    def load(self, eng, count):
        slots = len(self.q)
        for n in self.next("load", count):
            if n >= slots:
                eng.wait_ge(self.deq_done, n - slots + 1)
            q, scales = self.piece(n)[0:2]
            eng.dma_start(self.q[n % slots], q).then_inc(self.q_in[n % slots], 16)
            for i in range(P // QB):
                eng.dma_start(self.s[n % slots][i * QB:(i + 1) * QB, :],
                              scales[i:i + 1, :].to_broadcast([QB, 512])).then_inc(self.q_in[n % slots], 16)

    def split_small(self, act):
        act.wait_ge(self.small_in, 32)
        for dst, src, of in zip(self.st, self.raw, self.source):
            rows, cols = of.shape
            self.nc.scalar.activation(dst[0:rows, 0:cols], src[0:rows, 0:cols], ACT.Copy).then_inc(self.st_hi, 1)

    def split_small_lo(self, pool):
        for n, at in enumerate((L_AT[2], L_AT[1])):
            pool.wait_ge(self.st_hi, n + 1)
            part = (slice(at, at + R), slice(0, self.source[n].shape[1]))
            self.nc.gpsimd.tensor_tensor(self.st[n][part], self.raw[n][part], self.st[n][part].bitcast(F32),
                                         ALU.subtract).then_inc(self.st_lo, 1)
            pool.wait_ge(self.st_lo, n + 1)

    def products(self, pe, count):
        for n in self.next("pe", count):
            if n == 0:
                pe.wait_ge(self.st_hi, 2)
                pe.wait_ge(self.st_lo, 2)
            banks = len(self.lora)
            if n >= banks:
                pe.wait_ge(self.w_done, n - banks + 1)
            _, _, cols, a, _, _ = self.piece(n)
            b_st, a_st = self.st
            self.nc.tensor.matmul(self.lora[n % banks], a_st[0:LK, a:a + P], b_st[0:LK, cols:cols + 512],
                                  start=True, stop=True).then_inc(self.lora_done, 1)

    def dequantise(self, dve, count):
        for n in self.next("dve", count):
            slots, banks = len(self.q), len(self.lora)
            if n == 0:
                dve.wait_ge(self.st_hi, 2)
                dve.wait_ge(self.st_lo, 2)
            w = self.w[n % len(self.w)]
            dve.wait_ge(self.q_in[n % slots], 16 * 3 * (n // slots + 1))
            if n >= len(self.w):
                dve.wait_ge(self.lo_done, n - len(self.w) + 1)
            self.nc.vector.scalar_tensor_tensor(w, self.q[n % slots], -7.5, self.s[n % slots],
                                                ALU.add, ALU.mult).then_inc(self.deq_done, 1)
            dve.wait_ge(self.deq_done, n + 1)
            dve.wait_ge(self.lora_done, n + 1)
            self.nc.vector.tensor_tensor(w, w, self.lora[n % banks], ALU.add).then_inc(self.w_done, 1)

    def hi_parts(self, act, count):
        for n in self.next("act", count):
            act.wait_ge(self.w_done, n + 1)
            self.nc.scalar.activation(self.piece(n)[4], self.w[n % len(self.w)], ACT.Copy).then_inc(self.hi_done, 1)

    def lo_parts(self, pool, count):
        for n in self.next("pool", count):
            pool.wait_ge(self.hi_done, n + 1)
            hi, lo = self.piece(n)[4:6]
            self.nc.gpsimd.tensor_tensor(lo, self.w[n % len(self.w)], hi.bitcast(F32),
                                         ALU.subtract).then_inc(self.lo_done, 1)


def retention_phase(nc, w1_h, w1_l, x_tok, xT, x, wqkT, wvgT, woT, gnw, gnb, tab, consts, x1s, qup, sup, aup,
                    bupl):
    with ExitStack() as stack:
        def sb(name, shape, dt=F32):
            return stack.enter_context(nc.sbuf_tensor(name, shape, dt))

        def pb(name, shape):
            return stack.enter_context(nc.psum_tensor(name, shape, F32))

        def sem(name):
            return stack.enter_context(nc.semaphore(name))

        wqk_h, wqk_l = w1_h[:, :, 0:2 * D], w1_l[:, :, 0:2 * D]
        wvg_h, wvg_l = w1_h[:, :, 2 * D:4 * D], w1_l[:, :, 2 * D:4 * D]
        wo_h, wo_l = sb("wo_h", [P, NK, D], F32R), sb("wo_l", [P, NK, D], F32R)
        x_raw = sb("x_raw", [P, NK, S])
        x_h, x_l = sb("x_h", [P, NK, S], F32R), sb("x_l", [P, NK, S], F32R)
        qk_tok = sb("qk_tok", [P, NC, 2, NH, HD])
        v_tok = sb("v_tok", [P, NC, D])
        q_T, k_T = sb("q_T", [P, NP, S]), sb("k_T", [P, NP, S])
        sc_T = sb("sc_T", [P, 4, NC, P])
        state = sb("state", [P, NC - 1, NP, P])
        gate = sb("gate", [P, NP, S])
        y_h, y_l = sb("y_h", [P, NP, S], F32R), sb("y_l", [P, NP, S], F32R)
        y_t = sb("y_t", [P, 2, S])
        a_raw, a_st = sb("a_raw", [LK, D]), sb("a_st", [LK, D], F32R)
        rot_a, rot_b = sb("rot_a", [P, 2, NH, ROT]), sb("rot_b", [P, 2, NH, ROT])
        tab_s = sb("tab_s", [P, NC, 4 * ROT + 2 * NH])
        cst = sb("cst", [P, 3 * P])
        gn_s = sb("gn_s", [P, 2, NP])
        half = sb("half", [P, NC])
        pad = sb("pad", [P, 1])
        bn6 = sb("bn6", [P, NC, 6])
        mv = sb("mv", [P, 2])
        hm = sb("hm", [P, 2])
        ab = sb("ab", [P, 4])
        ab_b = sb("ab_b", [P, 1])
        ln_mv, ln_ve, ln_rs = sb("ln_mv", [P, NC, 2]), sb("ln_ve", [P, NC]), sb("ln_rs", [P, NC])

        causal, heads, ident = cst[:, 0:P], cst[:, P:2 * P], cst[:, 2 * P:3 * P]
        acc = pb("acc", [P, 2, 512])
        pas = [pb(f"pas{i}", [P, 512]) for i in range(2)]
        psc = [pb(f"psc{i}", [P, NC, P]) for i in range(2)]
        pret = [pb(f"pret{i}", [P, 512]) for i in range(2)]

        wx_in = [sem(f"wx_in{k}") for k in range(NK)]
        wv_in, wg_in, wo_in = sem("wv_in"), sem("wg_in"), sem("wo_in")
        const_in, x_in, xtok_in, x1_out = sem("const_in"), sem("x_in"), sem("xtok_in"), sem("x1_out")
        first_hi, first_lo, first_xlo = sem("first_hi"), sem("first_lo"), sem("first_xlo")
        w_hi, w_lo = sem("w_hi"), sem("w_lo")
        xs_hi, xs_lo = sem("xs_hi"), sem("xs_lo")
        init = sem("init")
        qk_done, v_done, g_done, t_done, s_done = map(sem, ("qk_done", "v_done", "g_done", "t_done", "s_done"))
        sc_done, r_done, st_done, o_done = map(sem, ("sc_done", "r_done", "st_done", "o_done"))
        qk_read, rot_done, pas_read, t_read, s_read, sc_read = map(
            sem, ("qk_read", "rot_done", "pas_read", "t_read", "s_read", "sc_read"))
        sq_done, gate_done = sem("sq_done"), sem("gate_done")
        bn_done, ve_done, rs_done, ab_done, aff_done, y_done = map(
            sem, ("bn_done", "ve_done", "rs_done", "ab_done", "aff_done", "y_done"))
        o_read, lnve_done, lnrs_done, x1_done = map(sem, ("o_read", "lnve_done", "lnrs_done", "x1_done"))
        act_link, dve_link, pool_link = sem("act_link"), sem("dve_link"), sem("pool_link")

        raw = qk_tok[:, :, :, :, :].rearrange("p c a h d -> p (c a h d)")
        prep = Prep(nc, sem, "up", NK * (FF // 512),
                    q=[x_raw[:, n, :].bitcast(I32) for n in range(4)],
                    s=[raw[:, 2048 + n * 512:2048 + (n + 1) * 512] for n in range(4)],
                    w=[raw[:, n * 512:(n + 1) * 512] for n in range(4)],
                    raw=[x_raw[:, :, :].rearrange("p k t -> p (k t)"), a_raw[:, :]],
                    st=[x_h[:, :, :].rearrange("p k t -> p (k t)"), a_st[:, :]],
                    lora=[acc[:, n, :] for n in range(2)], source=[bupl, aup],
                    piece=lambda n: up_piece(n, qup, sup, w1_h, w1_l))

        def run(eng, part):
            part(-1, False, True, True)
            with eng.Fori(0, B - 2) as b:
                part(b, True, True, True)
            part(B - 2, True, True, False)
            part(B - 1, True, False, False)

        block = stack.enter_context(nc.Block())

        @block.sync
        def _(sp):
            for k in range(NK):
                rows = slice(k * P, (k + 1) * P)
                sp.dma_start(qk_tok[:, k, :, :, :].rearrange("p a h d -> p (a h d)"), wqkT[rows, :]).then_inc(wx_in[k], 16)
                sp.dma_start(x_raw[:, k, :], xT[0, rows, :]).then_inc(wx_in[k], 16)
            sp.dma_start(tab_s[:, :, :], tab).then_inc(const_in, 16)
            sp.dma_start(cst[:, :], consts).then_inc(const_in, 16)
            for e in range(2):
                for n, g in enumerate((gnw, gnb)):
                    src = g[e:e + 1, :].to_broadcast([HD, NP])
                    sp.dma_start(gn_s[e * HD:(e + 1) * HD, n, :], src).then_inc(const_in, 16)
            wvg = wvgT.rearrange("(k p) n -> p k n", p=P)
            sp.dma_start(gate[:, :, :], wvg[:, :, D:2 * D]).then_inc(wg_in, 16)
            sp.dma_start(sc_T[:, :, :, :].rearrange("p a c q -> p a (c q)"),
                         woT.rearrange("(k p) n -> p k n", p=P)).then_inc(wo_in, 16)
            sp.dma_start(v_tok[:, :, :], wvg[:, :, 0:D]).then_inc(wv_in, 16)

            def part(b, ret, proj, more):
                if more:
                    if ret:
                        sp.wait_ge(xs_hi, NK * (b + 1))
                        sp.wait_ge(xs_lo, NK * (b + 1))
                    else:
                        sp.wait_ge(first_hi, NK)
                        sp.wait_ge(first_xlo, NK)
                    sp.dma_start(x_raw[:, :, :], xT[b + 2].rearrange("(k p) t -> p k t", p=P)).then_inc(x_in, 16)
                if proj and not more:
                    sp.wait_ge(xs_hi, NK * (B - 1))
                    sp.wait_ge(xs_lo, NK * (B - 1))
                    prep.load_small(sp)
                    sp.wait_ge(prep.st_hi, 2)
                    sp.wait_ge(prep.st_lo, 2)
                    sp.wait_ge(t_done, 2 * NP * B)
                    sp.wait_ge(s_done, (NC - 1) * B)
                    prep.load(sp, len(prep.q))
                if not proj:
                    prep.load(sp, prep.pieces - len(prep.q))
                if ret and proj:
                    sp.wait_ge(x1_done, b + 1)
                    sp.dma_start(x1s[b].rearrange("(c p) n -> p c n", p=P), x_tok[:, :, :]).then_inc(x1_out, 16)
                    sp.wait_ge(x1_out, 16 * (b + 1))
                if proj:
                    sp.dma_start(x_tok[:, :, :], x[b + 1].rearrange("(c p) n -> p c n", p=P)).then_inc(xtok_in, 16)
            run(sp, part)

        @block.tensor
        def _(pe):
            def split3(dst, lh, ll, rh, rl, first, last):
                nc.tensor.matmul(dst, lh, rh, start=first, stop=False)
                nc.tensor.matmul(dst, ll, rh, start=False, stop=False)
                return nc.tensor.matmul(dst, lh, rl, start=False, stop=last)

            def project_qk(b, c):
                first = isinstance(b, int) and b == 0 and c == 0
                if c == 0:
                    if not (isinstance(b, int) and b == 0):
                        pe.wait_ge(s_read, (NC - 1) * b)
                else:
                    pe.wait_ge(qk_read, NC * b + c)
                ts = slice(c * P, (c + 1) * P)
                order = [(n, k) for n in range(2) for k in range(NK)]
                for n, k in order if c else sorted(order, key=lambda x: x[1]):
                    if first and n == 0:
                        pe.wait_ge(first_hi, k + 1)
                        pe.wait_ge(first_lo, k + 1)
                        pe.wait_ge(first_xlo, k + 1)
                    elif c == 0 and n == 0:
                        pe.wait_ge(xs_hi, NK * (b - 1) + k + 1)
                        pe.wait_ge(xs_lo, NK * (b - 1) + k + 1)
                    cols = slice(n * D, (n + 1) * D)
                    last = split3(acc[:, n, :], x_h[:, k, ts], x_l[:, k, ts], wqk_h[:, k, cols],
                                  wqk_l[:, k, cols], k == 0, k == NK - 1)
                last.then_inc(qk_done, 1)

            def pass_bank(b, ret, proj, item):
                n = pass_order(ret, proj).index(item)
                wait(pe, pas_read, pass_base(b) + n - 1)
                return pas[n % 2]

            def project_v(b, c, bank):
                if isinstance(b, int) and b == 0 and c == 0:
                    pe.wait_ge(w_hi, 3)
                    pe.wait_ge(w_lo, 3)
                ts = slice(c * P, (c + 1) * P)
                for k in range(NK):
                    last = split3(bank[:, :], x_h[:, k, ts], x_l[:, k, ts], wvg_h[:, k, 0:D],
                                  wvg_l[:, k, 0:D], k == 0, k == NK - 1)
                last.then_inc(v_done, 1)

            def project_gate(b, p, bank):
                if isinstance(b, int) and b == 0 and p == 0:
                    pe.wait_ge(w_hi, 1)
                    pe.wait_ge(w_lo, 1)
                cols = slice(D + p * P, D + (p + 1) * P)
                for k in range(NK):
                    last = split3(bank[:, :], wvg_h[:, k, cols], wvg_l[:, k, cols], x_h[:, k, :],
                                  x_l[:, k, :], k == 0, k == NK - 1)
                last.then_inc(g_done, 1)

            def transpose_qk(b, t):
                if t == 0:
                    pe.wait_ge(rot_done, NC * (b + 1))
                    pe.wait_ge(qk_read, NC * (b + 1))
                    if isinstance(b, int) and b == 0:
                        pe.wait_ge(const_in, 16 * 6)
                if t >= 2:
                    pe.wait_ge(t_read, 2 * NP * b + t - 1)
                p = t // 2
                for c in range(NC):
                    src = qk_tok[:, c, t % 2, 2 * p:2 * p + 2, :].rearrange("p h d -> p (h d)")
                    last = nc.tensor.transpose(psc[t % 2][:, c, :], src, ident)
                last.then_inc(t_done, 1)

            def chunk_state(b, c, v3):
                if c == 0:
                    pe.wait_ge(pas_read, v3)
                if c == 2:
                    pe.wait_ge(s_read, (NC - 1) * b + 1)
                dst = acc[:, c % 2, :]
                for p in range(NP):
                    cols = slice(p * P, (p + 1) * P)
                    last = nc.tensor.matmul(dst[:, cols],
                                            qk_tok[:, c, 1, 2 * p:2 * p + 2, :].rearrange("p h d -> p (h d)"),
                                            v_tok[:, c, cols], start=True, stop=True)
                last.then_inc(s_done, 1)

            def scores(b, p):
                if p == 0:
                    pe.wait_ge(t_read, 2 * NP * (b + 1))
                else:
                    pe.wait_ge(sc_read, NH * b + 2 * p)
                for c in range(NC):
                    ts = slice(c * P, (c + 1) * P)
                    for e in range(2):
                        rows = slice(e * HD, (e + 1) * HD)
                        mm = nc.tensor.matmul(psc[e][:, c, :], k_T[rows, p, ts], q_T[rows, p, ts],
                                              start=True, stop=True)
                        if c == NC - 1:
                            mm.then_inc(sc_done, 1)

            def retention(b, p):
                pe.wait_ge(sc_read, NH * b + 2 * p + 2)
                if p == 0:
                    pe.wait_ge(s_read, (NC - 1) * (b + 1))
                if p >= 2:
                    pe.wait_ge(aff_done, NP * b + p - 1)
                bank = pret[p % 2]
                for c in range(NC):
                    ts = slice(c * P, (c + 1) * P)
                    if c:
                        nc.tensor.matmul(bank[:, ts], state[:, c - 1, p, :], q_T[:, p, ts],
                                         start=True, stop=False, skip_group_check=True)
                    for e in range(2):
                        rows = slice(e * HD, (e + 1) * HD)
                        h = 2 * p + e
                        last = nc.tensor.matmul(bank[rows, ts], v_tok[:, c, h * HD:(h + 1) * HD],
                                                sc_T[:, h % 4, c, :], start=(c == 0), stop=True,
                                                skip_group_check=True)
                last.then_inc(r_done, 1)

            def head_stats(b, p, bank):
                pe.wait_ge(bn_done, NP * b + p + 1)
                nc.tensor.matmul(bank[:, 0:2], heads, mv[:, :], start=True, stop=True).then_inc(st_done, 1)

            def project_out(b, c):
                if c == 0:
                    pe.wait_ge(y_done, NP * b + NP - 1)
                    pe.wait_ge(w_lo, 2)
                    pe.wait_ge(w_hi, 2)
                if c >= 2:
                    pe.wait_ge(o_read, NC * b + c - 1)
                ts = slice(c * P, (c + 1) * P)
                dst = pret[c % 2]
                for p in range(NP):
                    if c == 0 and p == NP - 1:
                        pe.wait_ge(y_done, NP * (b + 1))
                    last = split3(dst[:, :], y_h[:, p, ts], y_l[:, p, ts], wo_h[:, p, :], wo_l[:, p, :],
                                  p == 0, p == NP - 1)
                last.then_inc(o_done, 1)

            def part(b, ret, proj, more):
                order = pass_order(ret, proj)

                def stage(what, n):
                    if what == "T":
                        transpose_qk(b + 1, n)
                        return
                    bank = pass_bank(b, ret, proj, (what, n))
                    if what == "ST":
                        head_stats(b, n, bank)
                    elif what == "V":
                        project_v(b + 1, n, bank)
                    else:
                        project_gate(b + 1, n, bank)

                for p in range(NP):
                    if ret and p:
                        scores(b, p)
                    if proj:
                        project_qk(b + 1, p)
                        if not ret and p:
                            stage("G", p - 1)
                    if not proj:
                        prep.products(pe, PIECES_BEFORE_PAIR[p])
                    if ret and p:
                        stage("ST", p - 1)
                    if ret:
                        retention(b, p)
                    if not proj:
                        prep.products(pe, PIECES_AT_PAIR[p])
                for what, n in then_order(ret, proj):
                    stage(what, n)
                if not proj:
                    prep.products(pe, PIECES_AT_NORM)
                for c in range(NC):
                    if ret:
                        project_out(b, c)
                    if proj and c < NC - 1:
                        chunk_state(b + 1, c, pass_base(b) + order.index(("V", 3)) + 1)
                    if not proj:
                        prep.products(pe, PIECES_AT_OUT[c])
                if proj:
                    scores(b + 1, 0)
            run(pe, part)

        @block.scalar
        def _(act):
            for k in range(NK):
                act.wait_ge(wx_in[k], 32)
                nc.scalar.activation(x_h[:, k, :], x_raw[:, k, :], ACT.Copy)
                nc.scalar.activation(wqk_h[:, k, :], qk_tok[:, k, :, :, :].rearrange("p a h d -> p (a h d)"),
                                     ACT.Copy).then_inc(first_hi, 1)
            act.wait_ge(wg_in, 16)
            nc.scalar.activation(wvg_h[:, :, D:2 * D], gate[:, :, :], ACT.Copy).then_inc(w_hi, 1)
            act.wait_ge(wo_in, 16)
            nc.scalar.activation(wo_h[:, :, :], sc_T[:, :, :, :].rearrange("p a c q -> p a (c q)"),
                                 ACT.Copy).then_inc(w_hi, 1)
            act.wait_ge(wv_in, 16)
            nc.scalar.activation(wvg_h[:, :, 0:D], v_tok[:, :, :], ACT.Copy).then_inc(w_hi, 1)

            def norm_pair(b, p):
                act.wait_ge(ab_done, NP * b + p + 1)
                if p >= 2:
                    act.wait_ge(y_done, NP * b + p - 1)
                nc.scalar.activation(y_t[:, p % 2, :], pret[p % 2][:, :], ACT.Identity, bias=ab_b[:, 0:1],
                                     scale=ab[:, 2:3]).then_inc(aff_done, 1)

            def read_stats(b, p, bank):
                act.wait_ge(st_done, NP * b + p + 1)
                nc.scalar.activation(hm[:, :], bank[:, 0:2], ACT.Copy).then_inc(pas_read, 1)

            def part(b, ret, proj, more):
                order = pass_order(ret, proj)

                def stage(what, i):
                    r = b + 1
                    if what == "T":
                        dst = (q_T, k_T)[i % 2]
                        act.wait_ge(t_done, 2 * NP * r + i + 1)
                        nc.scalar.activation(dst[:, i // 2, :], psc[i % 2][:, :, :], ACT.Copy).then_inc(t_read, 1)
                        return
                    bank = pas[order.index((what, i)) % 2]
                    if what == "ST":
                        read_stats(b, i, bank)
                    elif what == "V":
                        act.wait_ge(v_done, NC * r + i + 1)
                        nc.scalar.activation(v_tok[:, i, :], bank[:, :], ACT.Copy).then_inc(pas_read, 1)
                    else:
                        tmp = sc_T[:, i, :, :].rearrange("p c q -> p (c q)")
                        act.wait_ge(g_done, NP * r + i + 1)
                        if ret:
                            act.wait_ge(y_done, NP * b + i + 1)
                        else:
                            act.wait_ge(w_lo, 2)
                        nc.scalar.activation(tmp, bank[:, :], ACT.Tanh, scale=0.5).then_inc(act_link, 1)
                        nc.scalar.activation(gate[:, i, :], bank[:, :], ACT.Copy).then_inc(pas_read, 1)
                        act.wait_ge(act_link, 2 * NP * r + 2 * i + 1)
                        nc.scalar.activation(tmp, tmp, ACT.Square, bias=1.0, scale=-1.0).then_inc(act_link, 1)
                        act.wait_ge(act_link, 2 * NP * r + 2 * i + 2)
                        nc.scalar.activation(tmp, tmp, ACT.Identity, bias=4.0).then_inc(sq_done, 1)

                if ret:
                    if not proj:
                        prep.hi_parts(act, PIECES_AT_PAIR[0])
                    for p in range(NP - 1):
                        stage("ST", p)
                        if not proj:
                            prep.hi_parts(act, PIECES_BEFORE_PAIR[p + 1])
                        norm_pair(b, p)
                        if not proj:
                            prep.hi_parts(act, PIECES_AT_PAIR[p + 1])
                elif proj:
                    for p in range(NP - 1):
                        stage("G", p)
                for what, i in then_order(ret, proj):
                    stage(what, i)
                    if ret and (what, i) == (("G", 1) if proj else ("ST", 3)):
                        norm_pair(b, NP - 1)
                if not proj:
                    prep.hi_parts(act, PIECES_AT_NORM + sum(PIECES_AT_OUT))
                if more:
                    act.wait_ge(x_in, 16 * (b + 2))
                    act.wait_ge(g_done, NP * (b + 2))
                    for k in range(NK):
                        nc.scalar.activation(x_h[:, k, :], x_raw[:, k, :], ACT.Copy).then_inc(xs_hi, 1)
                elif proj:
                    act.wait_ge(g_done, NP * B)
                    prep.split_small(act)
            run(act, part)

        @block.vector
        def _(dve):
            def sub(dst, a, hi):
                return nc.vector.tensor_tensor(dst, a, hi.bitcast(F32), ALU.subtract)

            nc.vector.memset(half[:, :], -0.5).then_inc(init, 1)
            nc.vector.memset(state[:, :, :, :], 0.0).then_inc(dve_link, 1)
            for k in range(NK):
                dve.wait_ge(first_hi, k + 1)
                sub(wqk_l[:, k, :], qk_tok[:, k, :, :, :].rearrange("p a h d -> p (a h d)"),
                    wqk_h[:, k, :]).then_inc(first_lo, 1)
            dve.wait_ge(const_in, 16 * 6)
            dve.wait_ge(dve_link, 1)

            cos, sin = tab_s[:, :, 0:2 * ROT], tab_s[:, :, 2 * ROT:4 * ROT]
            dec = tab_s[:, :, 4 * ROT:4 * ROT + 2 * NH]
            base = [1]

            def weight_lo(n):
                hi, lo, raw_w = ((wvg_h[:, :, D:2 * D], wvg_l[:, :, D:2 * D], gate[:, :, :]),
                                 (wo_h[:, :, :], wo_l[:, :, :], sc_T[:, :, :, :].rearrange("p a c q -> p a (c q)")),
                                 (wvg_h[:, :, 0:D], wvg_l[:, :, 0:D], v_tok[:, :, :]))[n]
                dve.wait_ge(w_hi, n + 1)
                sub(lo, raw_w, hi).then_inc(w_lo, 1)

            def mask_scores(b, h):
                dve.wait_ge(sc_done, NH * b + h + 1)
                if h >= 4:
                    dve.wait_ge(r_done, NP * b + (h - 4) // 2 + 1)
                nc.vector.tensor_tensor(sc_T[:, h % 4, :, :], psc[h % 2][:, :, :],
                                        causal.unsqueeze(1).to_broadcast([P, NC, P]), ALU.mult).then_inc(sc_read, 1)

            def rotate(b, c):
                dve.wait_ge(qk_done, NC * b + c + 1)
                wait(dve, rot_done, NC * b + c)
                ps = acc[:, :, :].rearrange("p a (h d) -> p a h d", h=NH)
                cs = cos[:, c, :].rearrange("p (a d) -> p a d", a=2).unsqueeze(2).to_broadcast([P, 2, NH, ROT])
                sn = sin[:, c, :].rearrange("p (a d) -> p a d", a=2).unsqueeze(2).to_broadcast([P, 2, NH, ROT])
                nc.vector.tensor_tensor(rot_a[:, :, :, :], ps[:, :, :, 0:ROT], cs, ALU.mult)
                nc.vector.tensor_tensor(rot_b[:, :, :, 0:ROT:2], ps[:, :, :, 1:ROT:2], sn[:, :, :, 0:ROT:2], ALU.mult)
                nc.vector.tensor_tensor(rot_b[:, :, :, 1:ROT:2], ps[:, :, :, 0:ROT:2], sn[:, :, :, 1:ROT:2], ALU.mult)
                dc = dec[:, c, :].rearrange("p (a h) -> p a h", a=2).unsqueeze(3).to_broadcast([P, 2, NH, HD - ROT])
                nc.vector.tensor_tensor(qk_tok[:, c, :, :, ROT:HD], ps[:, :, :, ROT:HD], dc, ALU.mult).then_inc(qk_read, 1)

            def pair_moments(b, p, link):
                dve.wait_ge(r_done, NP * b + p + 1)
                link(nc.vector.bn_stats(bn6[:, 0, :], pret[p % 2][:, :]))
                nc.vector.memset(pad[:, :], 0.0)
                link(nc.vector.bn_aggr(mv[:, :], bn6[:, 0, :]))
                nc.vector.scalar_tensor_tensor(mv[:, 1:2], mv[:, 0:1], mv[:, 0:1], mv[:, 1:2],
                                               ALU.mult, ALU.add).then_inc(bn_done, 1)

            def pair_variance(b, p, link, st):
                dve.wait_ge(pas_read, st)
                link(nc.vector.scalar_tensor_tensor(ab[:, 0:1], hm[:, 0:1], hm[:, 0:1], hm[:, 1:2],
                                                    ALU.mult, ALU.subtract))
                nc.vector.tensor_scalar(ab[:, 0:1], ab[:, 0:1], -1.0, EPS, ALU.mult, ALU.add).then_inc(ve_done, 1)

            def pair_affine(b, p, link):
                dve.wait_ge(rs_done, NP * b + p + 1)
                link(nc.vector.scalar_tensor_tensor(ab[:, 2:3], ab[:, 1:2], 8.0, gn_s[:, 0, p:p + 1], ALU.mult, ALU.mult))
                link(nc.vector.tensor_tensor(ab[:, 3:4], ab[:, 2:3], hm[:, 0:1], ALU.mult))
                nc.vector.scalar_tensor_tensor(ab_b[:, :], gn_s[:, 1, p:p + 1], 8.0, ab[:, 3:4],
                                               ALU.mult, ALU.subtract).then_inc(ab_done, 1)

            def gated(b, p, link):
                dve.wait_ge(aff_done, NP * b + p + 1)
                if p == 0:
                    dve.wait_ge(gate_done, NP * (b + 1))
                y = y_t[:, p % 2, :]
                link(nc.vector.tensor_tensor(y, y, gate[:, p, :], ALU.mult))
                link(nc.vector.tensor_copy(y_h[:, p, :], y))
                sub(y_l[:, p, :], y, y_h[:, p, :]).then_inc(y_done, 1)

            def finish_gate(b, p, link):
                tmp = sc_T[:, p, :, :].rearrange("p c q -> p (c q)")
                dve.wait_ge(sq_done, NP * b + p + 1)
                link(nc.vector.reciprocal(tmp, tmp))
                nc.vector.scalar_tensor_tensor(gate[:, p, :], tmp, -0.125, gate[:, p, :],
                                               ALU.add, ALU.mult).then_inc(gate_done, 1)

            def add_state(b, c):
                dve.wait_ge(s_done, (NC - 1) * b + c + 1)
                if c:
                    dve.wait_ge(s_read, (NC - 1) * b + c)
                ps = acc[:, c % 2, :].rearrange("p (q n) -> p q n", q=NP)
                for e in range(2):
                    half_ = slice(e * HD, (e + 1) * HD)
                    if c == 0:
                        last = nc.vector.tensor_copy(state[half_, 0, :, half_], ps[half_, :, half_])
                    else:
                        last = nc.vector.tensor_tensor(state[half_, c, :, half_], ps[half_, :, half_],
                                                       state[half_, c - 1, :, half_], ALU.add)
                last.then_inc(s_read, 1)

            def residual(b, c):
                dve.wait_ge(o_done, NC * b + c + 1)
                if c == 0:
                    dve.wait_ge(xtok_in, 16 * (b + 1))
                nc.vector.tensor_tensor(x_tok[:, c, :], pret[c % 2][:, :], x_tok[:, c, :],
                                        ALU.add).then_inc(o_read, 1)

            def x_lo(b, k):
                dve.wait_ge(xs_hi, NK * (b - 1) + k + 1)
                sub(x_l[:, k, :], x_raw[:, k, :], x_h[:, k, :]).then_inc(xs_lo, 1)

            def row_stats(b, c):
                dve.wait_ge(o_read, NC * b + c + 1)
                return nc.vector.bn_stats(bn6[:, c, :], x_tok[:, c, :])

            def layer_norm(b, link):
                link(row_stats(b, NC - 1))
                nc.vector.memset(pad[:, :], 0.0)
                for c in range(NC):
                    last = nc.vector.bn_aggr(ln_mv[:, c, :], bn6[:, c, :])
                link(last)
                nc.vector.tensor_scalar(ln_ve[:, :], ln_mv[:, :, 1], EPS, None, ALU.add).then_inc(lnve_done, 1)
                dve.wait_ge(lnrs_done, b + 1)
                for c in range(NC):
                    last = nc.vector.tensor_scalar(x_tok[:, c, :], x_tok[:, c, :], ln_mv[:, c, 0:1],
                                                   ln_rs[:, c:c + 1], ALU.subtract, ALU.mult)
                last.then_inc(x1_done, 1)

            LINKS_PROJ, LINKS_RET = NP, NP * (2 + 1 + 2 + 2) + 2

            def part(b, ret, proj, more):
                first = isinstance(b, int) and b < 0
                link = Links(dve, dve_link, 1 if first else 1 + LINKS_PROJ + b * (LINKS_PROJ + LINKS_RET))
                order = pass_order(ret, proj)
                st = lambda p: pass_base(b) + order.index(("ST", p)) + 1
                for p in range(NP):
                    if ret and p:
                        mask_scores(b, 2 * p)
                        mask_scores(b, 2 * p + 1)
                        pair_variance(b, p - 1, link, st(p - 1))
                    if proj:
                        rotate(b + 1, p)
                        if not ret and p < 3:
                            weight_lo(p)
                        if not ret and p >= 2:
                            finish_gate(b + 1, p - 2, link)
                    if not proj:
                        prep.dequantise(dve, PIECES_BEFORE_PAIR[p])
                    if ret:
                        if p:
                            pair_affine(b, p - 1, link)
                        pair_moments(b, p, link)
                        if p:
                            gated(b, p - 1, link)
                    if not proj:
                        prep.dequantise(dve, PIECES_AT_PAIR[p])
                if ret:
                    pair_variance(b, NP - 1, link, st(NP - 1))
                    pair_affine(b, NP - 1, link)
                    if proj:
                        finish_gate(b + 1, 0, link)
                    gated(b, NP - 1, link)
                if not proj:
                    prep.dequantise(dve, PIECES_AT_NORM)
                if proj:
                    for p in range(1 if ret else 2, NP):
                        finish_gate(b + 1, p, link)
                for c in range(NC):
                    if ret:
                        if c:
                            row_stats(b, c - 1)
                        residual(b, c)
                    if proj and c < NC - 1:
                        add_state(b + 1, c)
                    if more:
                        x_lo(b + 2, c)
                    if not proj:
                        prep.dequantise(dve, PIECES_AT_OUT[c])
                if proj:
                    mask_scores(b + 1, 0)
                    mask_scores(b + 1, 1)
                if ret:
                    layer_norm(b, link)
                assert link.n == LINKS_PROJ * proj + LINKS_RET * ret
            run(dve, part)

        @block.gpsimd
        def _(pool):
            for k in range(NK):
                pool.wait_ge(first_hi, k + 1)
                nc.gpsimd.tensor_tensor(x_l[:, k, :], x_raw[:, k, :], x_h[:, k, :].bitcast(F32),
                                        ALU.subtract).then_inc(first_xlo, 1)
            pool.wait_ge(init, 1)
            pool.wait_ge(const_in, 16 * 6)

            def rotate(b, c):
                pool.wait_ge(qk_read, NC * b + c + 1)
                nc.gpsimd.tensor_tensor(rot_a[:, :, :, :], rot_a[:, :, :, :], rot_b[:, :, :, :],
                                        ALU.add).then_inc(pool_link, 1)
                pool.wait_ge(pool_link, NC * b + c + 1)
                dc = tab_s[:, c, 4 * ROT:4 * ROT + 2 * NH].rearrange("p (a h) -> p a h", a=2)\
                    .unsqueeze(3).to_broadcast([P, 2, NH, ROT])
                nc.gpsimd.tensor_tensor(qk_tok[:, c, :, :, 0:ROT], rot_a[:, :, :, :], dc, ALU.mult).then_inc(rot_done, 1)

            def rstd(b, p):
                pool.wait_ge(ve_done, NP * b + p + 1)
                nc.gpsimd.tensor_tensor(ab[:, 1:2], ab[:, 0:1], half[:, 0:1], ALU.pow).then_inc(rs_done, 1)

            def part(b, ret, proj, more):
                for p in range(NP):
                    if ret and p:
                        rstd(b, p - 1)
                    if proj:
                        rotate(b + 1, p)
                    else:
                        prep.lo_parts(pool, PIECES_BEFORE_PAIR[p] + (PIECES_AT_PAIR[p] if p < NP - 1 else 0))
                if ret:
                    rstd(b, NP - 1)
                if not proj:
                    prep.lo_parts(pool, PIECES_AT_PAIR[NP - 1] + PIECES_AT_NORM + sum(PIECES_AT_OUT))
                if proj and not more:
                    prep.split_small_lo(pool)
                if ret:
                    pool.wait_ge(lnve_done, b + 1)
                    nc.gpsimd.tensor_tensor(ln_rs[:, :], ln_ve[:, :], half[:, :], ALU.pow).then_inc(lnrs_done, 1)
            run(pool, part)


def ffn_rows(nc, wu_h, wu_l, x1, ctxT, ctx_in, mask, bup, qdn, sdn, bdn, adn, bdnl, consts, x1s, out):
    with ExitStack() as stack:
        def sb(name, shape, dt=F32):
            return stack.enter_context(nc.sbuf_tensor(name, shape, dt))

        def pb(name, shape):
            return stack.enter_context(nc.psum_tensor(name, shape, F32))

        def sem(name):
            return stack.enter_context(nc.semaphore(name))

        NHID = 2
        wd_h, wd_l = sb("wd_h", [P, NF, D], F32R), sb("wd_l", [P, NF, D], F32R)
        w_new = sb("w_new", [P, 4, 512])
        bup_s, bdn_s = sb("bup_s", [P, NF]), sb("bdn_s", [P, D])
        x1_T = sb("x1_T", [P, NK, S])
        x2_h, x2_l = sb("x2_h", [P, NK, S], F32R), sb("x2_l", [P, NK, S], F32R)
        x2b = sb("x2b", [P, NC, D])
        hid = sb("hid", [P, 2, S])
        hid_h, hid_l = sb("hid_h", [P, NHID, S], F32R), sb("hid_l", [P, NHID, S], F32R)
        z_out = sb("z_out", [P, 2, D])
        ctx_T, ctx_s = sb("ctx_T", [P, NK, M]), sb("ctx_s", [P, D])
        ctx_h, ctx_l = sb("ctx_h", [P, D], F32R), sb("ctx_l", [P, D], F32R)
        mask_s = sb("mask_s", [P, M], U8)
        keep, bias, valid = sb("keep", [P, M]), sb("bias", [P, M]), sb("valid", [P, 1])
        sm, smax, ssum = sb("sm", [P, NC, M]), sb("smax", [P, NC]), sb("ssum", [P, NC])
        p_Th, p_Tl = sb("p_Th", [P, 2 * P], F32R), sb("p_Tl", [P, 2 * P], F32R)
        ident_s = sb("ident_s", [P, P])
        half2 = sb("half2", [P, NC])
        pad2 = sb("pad2", [P, 1])
        bn6 = sb("bn6b", [P, NC, 6])
        ln_mv, ln_ve, ln_rs = sb("ln_mv2", [P, NC, 2]), sb("ln_ve2", [P, NC]), sb("ln_rs2", [P, NC])
        fn_mv, fn_ve, fn_rs = sb("fn_mv", [P, NC, 2]), sb("fn_ve", [P, NC]), sb("fn_rs", [P, NC])
        pdn = [pb(f"pdn{i}", [P, 512]) for i in range(NC)]
        pup = [pb(f"pup{i}", [P, 512]) for i in range(2)]
        pxa = [pb(f"pxa{i}", [P, 512]) for i in range(2)]

        x1_in, ctx_inn, z_free = sem("x1_in"), sem("ctx_inn"), [sem("z_free0"), sem("z_free1")]
        init = sem("init2")
        t1_done, sc_done, ta_done, rd_done, t2_done, up_done, dn_done = map(
            sem, ("t1_done", "xsc_done", "ta_done", "rd_done", "t2_done", "up_done", "dn_done"))
        t1_read, ctxh_done, ta_hi, exp_done, t2_hi, hid_done = map(
            sem, ("t1_read", "ctxh_done", "ta_hi", "exp_done", "t2_hi", "hid_done"))
        ctxl_done, mask_done, shift_done, prob_done, ta_lo, rd_read, lnve_done, x2_done, t2_lo, hidl_done = map(
            sem, ("ctxl_done", "mask_done", "shift_done", "prob_done", "ta_lo", "rd_read", "xlnve_done", "x2_done",
                  "t2_lo", "hidl_done"))
        pdn_free, fnve_done, z_done = sem("pdn_free"), sem("fnve_done"), sem("z_done")
        lnrs_done, x2b_done, fnrs_done = sem("xlnrs_done"), sem("x2b_done"), sem("fnrs_done")
        dve_link, bias_in, dn_chunk = sem("dve_link2"), sem("bias_in"), sem("dn_chunk")

        prep = Prep(nc, sem, "down", NF,
                    q=[x2b[:, n, :].bitcast(I32) for n in range(4)],
                    s=[t[:, n, :] for t in (hid, z_out) for n in range(2)],
                    w=[w_new[:, n, :] for n in range(4)],
                    raw=[bdn_s[:, :], w_new[:, :, :].rearrange("p n c -> p (n c)")],
                    st=[hid_h[:, 0, :], x2_l[:, :, :].rearrange("p k t -> p (k t)")],
                    lora=[t[:, :] for t in pdn], source=[bdnl, adn],
                    piece=lambda n: down_piece(n, qdn, sdn, wd_h, wd_l))
        block = stack.enter_context(nc.Block())

        def first_row(b):
            return isinstance(b, int) and b == 0

        def z_slot(xattn, c):
            return z_out[:, c % 2, :] if xattn or c < 2 else x1[:, c, :]

        def run(eng, part):
            part(-1, False, True)
            with eng.Fori(0, B - 1) as b:
                part(b, True, True)
            part(B - 1, True, False)

        @block.sync
        def _(sp):
            for n, z in enumerate(z_free):
                cols = slice(n * HD, (n + 1) * HD)
                sp.dma_start(ident_s[:, cols], consts[:, 2 * P + n * HD:2 * P + (n + 1) * HD]).then_inc(z, 16)

            def part(b, ffn, xattn):
                if xattn:
                    if ffn:
                        sp.wait_ge(rd_done, NC * (b + 1))
                    if not ffn:
                        prep.load_small(sp)
                    sp.dma_start(ctx_T[:, :, :], ctxT[b + 1].rearrange("(k p) m -> p k m", p=P)).then_inc(ctx_inn, 16)
                    for half in range(2):
                        sp.dma_start(ctx_s[half * M:(half + 1) * M, :], ctx_in[b + 1]).then_inc(ctx_inn, 16)
                    sp.dma_start(mask_s[:, :], mask[b + 1].to_broadcast([P, M])).then_inc(ctx_inn, 16)
                    if ffn:
                        sp.wait_ge(x2b_done, b + 1)
                        sp.dma_start(x1[:, :, :], x1s[b].rearrange("(c p) n -> p c n", p=P)).then_inc(x1_in, 16)
                    else:
                        prep.load(sp, NF)
                        sp.dma_start(bup_s[:, :], bup).then_inc(bias_in, 16)
                        sp.wait_ge(prep.st_hi, 2)
                        sp.wait_ge(prep.st_lo, 2)
                        sp.dma_start(bdn_s[:, :], bdn.to_broadcast([P, D])).then_inc(bias_in, 16)
                if ffn:
                    for c in range(NC):
                        sp.wait_ge(z_done, NC * b + c + 1)
                        sp.dma_start(out[b, c * P:(c + 1) * P, :], z_slot(xattn, c)).then_inc(z_free[c % 2], 16)
            run(sp, part)
            for z in z_free:
                sp.wait_ge(z, 16 * (B * NC // 2 + 1))

        @block.tensor
        def _(pe):
            def split3(dst, lh, ll, rh, rl, first, last):
                nc.tensor.matmul(dst, lh, rh, start=first, stop=False)
                nc.tensor.matmul(dst, ll, rh, start=False, stop=False)
                return nc.tensor.matmul(dst, lh, rl, start=False, stop=last)

            for z in z_free:
                pe.wait_ge(z, 16)

            def transpose_x1(b, k):
                if k == 0 and not first_row(b):
                    pe.wait_ge(x1_in, 16 * b)
                if k >= 2:
                    pe.wait_ge(t1_read, NK * b + k - 1)
                for c in range(NC):
                    last = nc.tensor.transpose(pxa[k % 2][:, c * P:(c + 1) * P], x1[:, c, k * P:(k + 1) * P], ident_s[:, :])
                last.then_inc(t1_done, 1)

            def scores(b):
                pe.wait_ge(t1_read, NK * (b + 1))
                pe.wait_ge(ctx_inn, 64 * (b + 1))
                for c in range(NC):
                    for k in range(NK):
                        last = nc.tensor.matmul(pxa[0][:, c * M:(c + 1) * M], x1_T[:, k, c * P:(c + 1) * P],
                                                ctx_T[:, k, :], start=(k == 0), stop=(k == NK - 1))
                last.then_inc(sc_done, 1)

            def transpose_probs(b):
                pe.wait_ge(exp_done, b + 1)
                for a in range(2):
                    last = nc.tensor.transpose(pxa[1][:, a * P:(a + 1) * P],
                                               sm[:, 2 * a:2 * a + 2, :].rearrange("p c m -> p (c m)"), ident_s[:, :])
                last.then_inc(ta_done, 1)

            def read_memory(b, c):
                if c == 0:
                    pe.wait_ge(ta_hi, b + 1)
                    pe.wait_ge(ta_lo, b + 1)
                    pe.wait_ge(ctxl_done, b + 1)
                if c >= 2:
                    pe.wait_ge(rd_read, NC * b + c - 1)
                rows, ts = slice((c % 2) * M, (c % 2 + 1) * M), slice(c // 2 * P, (c // 2 + 1) * P)
                split3(pxa[c % 2][:, :], p_Th[rows, ts], p_Tl[rows, ts], ctx_h[rows, :], ctx_l[rows, :], True, True).then_inc(rd_done, 1)

            def transpose_x2(b, k):
                if k == 0:
                    pe.wait_ge(x2_done, b + 1)
                if k >= 2:
                    pe.wait_ge(t2_hi, NK * b + k - 1)
                    pe.wait_ge(t2_lo, NK * b + k - 1)
                for c in range(NC):
                    last = nc.tensor.transpose(pxa[k % 2][:, c * P:(c + 1) * P], x1[:, c, k * P:(k + 1) * P], ident_s[:, :])
                last.then_inc(t2_done, 1)

            def up(b, f):
                if f >= 2 or not first_row(b):
                    pe.wait_ge(hid_done, NF * b + f - 1)
                fs = slice(f * P, (f + 1) * P)
                for k in range(NK):
                    if f == 0:
                        pe.wait_ge(t2_hi, NK * b + k + 1)
                        pe.wait_ge(t2_lo, NK * b + k + 1)
                    last = split3(pup[f % 2][:, :], wu_h[:, k, fs], wu_l[:, k, fs], x2_h[:, k, :], x2_l[:, k, :],
                                  k == 0, k == NK - 1)
                last.then_inc(up_done, 1)

            def down(b, f, chunks=range(NC)):
                pe.wait_ge(hidl_done, NF * b + f + 1)
                if f == 0 and first_row(b):
                    pe.wait_ge(prep.w_done, NF)
                    pe.wait_ge(prep.hi_done, 1)
                    pe.wait_ge(prep.lo_done, 1)
                if f == 1:
                    pe.wait_ge(prep.hi_done, NF)
                    pe.wait_ge(prep.lo_done, NF)
                if f == 0 and not first_row(b):
                    pe.wait_ge(pdn_free, NC * b)
                for c in chunks:
                    ts = slice(c * P, (c + 1) * P)
                    last = split3(pdn[c][:, :], hid_h[:, f % NHID, ts], hid_l[:, f % NHID, ts], wd_h[:, f, :],
                                  wd_l[:, f, :], f == 0, f == NF - 1)
                    if f == NF - 1 and c < NC - 1:
                        last.then_inc(dn_chunk, 1)
                if c == NC - 1:
                    last.then_inc(dn_done, 1)

            def part(b, ffn, xattn):
                def beside(f):
                    if not xattn:
                        return
                    if 5 <= f < 7:
                        transpose_x1(b + 1, 2 * (f - 5))
                        transpose_x1(b + 1, 2 * (f - 5) + 1)
                    if f == 7:
                        scores(b + 1)
                    if f == 8:
                        transpose_probs(b + 1)
                    if 9 <= f < 13:
                        read_memory(b + 1, f - 9)
                for f in range(HEAD, NF):
                    if ffn:
                        up(b, f)
                    beside(f)
                    if ffn:
                        down(b, f - 1)
                    else:
                        prep.products(pe, PIECES_BESIDE.get(f, 0))
                if not ffn:
                    prep.products(pe, PIECES_AHEAD)
                for k in range(NK):
                    if xattn:
                        transpose_x2(b + 1, k)
                    if ffn and k:
                        down(b, NF - 1, ([0, 1], [2], [3])[k - 1])
                if xattn:
                    for f in range(HEAD):
                        up(b + 1, f)
                        if f:
                            down(b + 1, f - 1)
            run(pe, part)

        @block.scalar
        def _(act):
            def relu(b, f):
                if f == 0 and first_row(b):
                    act.wait_ge(bias_in, 32)
                act.wait_ge(up_done, NF * b + f + 1)
                if f >= 2 or not first_row(b):
                    act.wait_ge(hidl_done, NF * b + f - 1)
                    act.wait_ge(dn_done, NF * b + f - 1)
                nc.scalar.activation(hid[:, f % 2, :], pup[f % 2][:, :], ACT.Relu, bias=bup_s[:, f:f + 1])
                nc.scalar.activation(hid_h[:, f % NHID, :], pup[f % 2][:, :], ACT.Relu,
                                     bias=bup_s[:, f:f + 1]).then_inc(hid_done, 1)

            def part(b, ffn, xattn):
                r = b + 1

                def beside(f):
                    if not xattn:
                        return
                    if f == 5:
                        act.wait_ge(ctx_inn, 64 * (r + 1))
                        nc.scalar.activation(ctx_h[:, :], ctx_s[:, :], ACT.Copy).then_inc(ctxh_done, 1)
                        if not ffn:
                            prep.split_small(act)
                    if f == 7:
                        act.wait_ge(shift_done, r + 1)
                        nc.scalar.activation(sm[:, :, :], sm[:, :, :], ACT.Exp).then_inc(exp_done, 1)
                    if f == 8:
                        act.wait_ge(ta_done, r + 1)
                        nc.scalar.activation(p_Th[:, :], pxa[1][:, 0:2 * P], ACT.Copy).then_inc(ta_hi, 1)
                for f in range(HEAD, NF):
                    if ffn:
                        relu(b, f)
                    beside(f)
                    if not ffn:
                        prep.hi_parts(act, PIECES_BESIDE.get(f, 0))
                if xattn:
                    for k in range(NK):
                        act.wait_ge(t2_done, NK * r + k + 1)
                        nc.scalar.activation(x2_h[:, k, :], pxa[k % 2][:, :], ACT.Copy).then_inc(t2_hi, 1)
                    for f in range(HEAD):
                        if not ffn:
                            prep.hi_parts(act, PIECES_AHEAD // HEAD)
                        relu(r, f)
            run(act, part)

        @block.vector
        def _(dve):
            def sub(dst, a, hi):
                return nc.vector.tensor_tensor(dst, a, hi.bitcast(F32), ALU.subtract)

            nc.vector.memset(half2[:, :], -0.5).then_inc(init, 1)
            LINKS_X, LINKS_F = 6, 2

            def masks(b, link):
                dve.wait_ge(ctx_inn, 64 * (b + 1))
                link(nc.vector.tensor_copy(keep[:, :], mask_s[:, :]))
                nc.vector.tensor_scalar(bias[:, :], keep[:, :], -1.0, NEG, ALU.add, ALU.mult)
                nc.vector.reduce_max(valid[:, :], keep[:, :], AX.X).then_inc(mask_done, 1)
                dve.wait_ge(ctxh_done, b + 1)
                sub(ctx_l[:, :], ctx_s[:, :], ctx_h[:, :]).then_inc(ctxl_done, 1)

            def softmax_shift(b, link):
                dve.wait_ge(sc_done, b + 1)
                dve.wait_ge(mask_done, b + 1)
                kp = keep[:, :].unsqueeze(1).to_broadcast([P, NC, M])
                bs = bias[:, :].unsqueeze(1).to_broadcast([P, NC, M])
                ps = pxa[0][:, 0:NC * M].rearrange("p (c m) -> p c m", c=NC)
                link(nc.vector.scalar_tensor_tensor(sm[:, :, :], ps, float(np.float32(1.0) / np.sqrt(np.float32(D))), kp,
                                                    ALU.mult, ALU.mult))
                link(nc.vector.tensor_tensor(sm[:, :, :], sm[:, :, :], bs, ALU.add))
                link(nc.vector.reduce_max(smax[:, :], sm[:, :, :], AX.X))
                nc.vector.tensor_tensor(sm[:, :, :], sm[:, :, :], smax[:, :].unsqueeze(2).to_broadcast([P, NC, M]),
                                        ALU.subtract).then_inc(shift_done, 1)

            def softmax_sum(b, link):
                dve.wait_ge(exp_done, b + 1)
                nc.vector.reduce_sum(ssum[:, :], sm[:, :, :], AX.X).then_inc(prob_done, 1)
                dve.wait_ge(prob_done, 3 * b + 1)
                nc.vector.reciprocal(ssum[:, :], ssum[:, :]).then_inc(prob_done, 1)
                dve.wait_ge(prob_done, 3 * b + 2)
                nc.vector.tensor_scalar(ssum[:, :], ssum[:, :], valid[:, 0:1], None, ALU.mult).then_inc(prob_done, 1)

            def sum_stats(b, c):
                dve.wait_ge(pdn_free, NC * b + c + 1)
                return nc.vector.bn_stats(bn6[:, c, :], x2b[:, c, :])

            def hid_lo(b, f):
                dve.wait_ge(hid_done, NF * b + f + 1)
                if f >= 2 or not first_row(b):
                    dve.wait_ge(dn_done, NF * b + f - 1)
                sub(hid_l[:, f % NHID, :], hid[:, f % 2, :], hid_h[:, f % NHID, :]).then_inc(hidl_done, 1)

            def part(b, ffn, xattn):
                r = b + 1
                first = isinstance(b, int) and b < 0
                link = Links(dve, dve_link, 0 if first else LINKS_X + b * (LINKS_X + LINKS_F))

                def beside(f):
                    if not xattn:
                        return
                    if 5 <= f < 7:
                        for k in (2 * (f - 5), 2 * (f - 5) + 1):
                            dve.wait_ge(t1_done, NK * r + k + 1)
                            nc.vector.tensor_copy(x1_T[:, k, :], pxa[k % 2][:, :]).then_inc(t1_read, 1)
                    if f == 6:
                        masks(r, link)
                    if f == 7:
                        softmax_shift(r, link)
                    if f == 8:
                        softmax_sum(r, link)
                        dve.wait_ge(ta_hi, r + 1)
                        sub(p_Tl[:, :], pxa[1][:, 0:2 * P], p_Th[:, :]).then_inc(ta_lo, 1)
                    if 9 <= f < 13:
                        c = f - 9
                        dve.wait_ge(rd_done, NC * r + c + 1)
                        if c == 0:
                            dve.wait_ge(prob_done, 3 * (r + 1))
                        nc.vector.scalar_tensor_tensor(x1[:, c, :], pxa[c % 2][:, :], ssum[:, c:c + 1], x1[:, c, :],
                                                       ALU.mult, ALU.add).then_inc(rd_read, 1)
                    if f == 13:
                        dve.wait_ge(rd_read, NC * (r + 1))
                        for c in range(NC):
                            last = nc.vector.bn_stats(bn6[:, c, :], x1[:, c, :])
                        link(last)
                        nc.vector.memset(pad2[:, :], 0.0)
                        for c in range(NC):
                            last = nc.vector.bn_aggr(ln_mv[:, c, :], bn6[:, c, :])
                        link(last)
                        nc.vector.tensor_scalar(ln_ve[:, :], ln_mv[:, :, 1], EPS, None, ALU.add).then_inc(lnve_done, 1)
                    if f == 14:
                        dve.wait_ge(lnrs_done, r + 1)
                        for c in range(NC):
                            last = nc.vector.tensor_scalar(x1[:, c, :], x1[:, c, :], ln_mv[:, c, 0:1],
                                                           ln_rs[:, c:c + 1], ALU.subtract, ALU.mult)
                        last.then_inc(x2_done, 1)
                for f in range(HEAD, NF):
                    if ffn:
                        hid_lo(b, f)
                    beside(f)
                    if not ffn:
                        prep.dequantise(dve, PIECES_BESIDE.get(f, 0))
                if xattn:
                    for k in range(NK):
                        if not ffn and k % 2 == 0:
                            prep.dequantise(dve, 1)
                        dve.wait_ge(t2_hi, NK * r + k + 1)
                        sub(x2_l[:, k, :], pxa[k % 2][:, :], x2_h[:, k, :]).then_inc(t2_lo, 1)
                if ffn:
                    dve.wait_ge(x2b_done, b + 1)
                    for c in range(NC):
                        if c < NC - 1:
                            dve.wait_ge(dn_chunk, (NC - 1) * b + c + 1)
                        else:
                            dve.wait_ge(dn_done, NF * (b + 1))
                        nc.vector.tensor_tensor(x2b[:, c, :], pdn[c][:, :], x2b[:, c, :], ALU.add).then_inc(pdn_free, 1)
                        if not xattn:
                            last = sum_stats(b, c)
                if not ffn:
                    prep.dequantise(dve, PIECES_AHEAD - 2)
                if xattn:
                    hid_lo(r, 0)
                if ffn:
                    if xattn:
                        for c in range(NC):
                            last = sum_stats(b, c)
                    link(last)
                    nc.vector.memset(pad2[:, :], 0.0)
                    for c in range(NC):
                        last = nc.vector.bn_aggr(fn_mv[:, c, :], bn6[:, c, :])
                    link(last)
                    nc.vector.tensor_scalar(fn_ve[:, :], fn_mv[:, :, 1], EPS, None, ALU.add).then_inc(fnve_done, 1)
                if xattn:
                    hid_lo(r, 1)
                if ffn:
                    dve.wait_ge(fnrs_done, b + 1)
                    for c in range(NC):
                        if xattn or c < 2:
                            dve.wait_ge(z_free[c % 2], 16 * (2 * b + 1 + c // 2))
                        nc.vector.tensor_scalar(z_slot(xattn, c), x2b[:, c, :], fn_mv[:, c, 0:1], fn_rs[:, c:c + 1],
                                                ALU.subtract, ALU.mult).then_inc(z_done, 1)
                assert link.n == LINKS_X * xattn + LINKS_F * ffn
            run(dve, part)

        @block.gpsimd
        def _(pool):
            prep.split_small_lo(pool)
            pool.wait_ge(init, 1)

            def part(b, ffn, xattn):
                for f in range(HEAD, NF):
                    if xattn and f == 13:
                        pool.wait_ge(lnve_done, b + 2)
                        nc.gpsimd.tensor_tensor(ln_rs[:, :], ln_ve[:, :], half2[:, :], ALU.pow).then_inc(lnrs_done, 1)
                    if not ffn:
                        prep.lo_parts(pool, PIECES_BESIDE.get(f, 0))
                if ffn:
                    pool.wait_ge(fnve_done, b + 1)
                    nc.gpsimd.tensor_tensor(fn_rs[:, :], fn_ve[:, :], half2[:, :], ALU.pow).then_inc(fnrs_done, 1)
                if xattn:
                    pool.wait_ge(t2_done, NK * (b + 2))
                    if ffn:
                        pool.wait_ge(z_done, NC * (b + 1))
                    if not ffn:
                        prep.lo_parts(pool, PIECES_AHEAD)
                        pool.wait_ge(bias_in, 32)
                    for c in range(NC):
                        last = nc.gpsimd.tensor_tensor(x2b[:, c, :], x1[:, c, :], bdn_s[:, :], ALU.add)
                    last.then_inc(x2b_done, 1)
            run(pool, part)


def kernel(**inputs):
    import numpy as _np
    import concourse.bacc as _bacc
    from concourse import mybir as _mybir
    from concourse.bass_utils import run_bass_kernel_spmd as _run

    a = {k: _np.asarray(v) for k, v in inputs.items()}
    c = _np.ascontiguousarray
    x = _np.concatenate([a["x"][1:], a["x"][:1]])
    w = a["L0_attn_wqkv"].reshape(NH, 3, HD, D)
    wT = w.transpose(3, 1, 0, 2).reshape(D, 3 * D)
    tab, consts = tables()
    arrays = {
        "xT": c(x.transpose(0, 2, 1)), "x": c(x),
        "ctxT": c(a["ctx_2048"].transpose(0, 2, 1)), "ctx_in": c(a["ctx_2048"]),
        "mask": c(a["mask_BxS2_bk0"].reshape(B, 1, M)),
        "wqkT": c(wT[:, 0:2 * D]),
        "wvgT": c(_np.concatenate([wT[:, 2 * D:], a["L0_attn_wg"].T], axis=1)),
        "woT": c(a["L0_attn_wo"].T),
        "gnw": c(a["L0_attn_gn_weight"].reshape(NP, 2).T), "gnb": c(a["L0_attn_gn_bias"].reshape(NP, 2).T),
        "qup": c(a["L0_ffn_w_up_q"].T), "sup": c(a["L0_ffn_w_up_scale"].T),
        "bup": c(a["L0_ffn_b_up"].reshape(NF, P).T),
        "aup": stacked(a["L0_ffn_w_up_lora_a"].T, L_AT, LK), "bupl": stacked(a["L0_ffn_w_up_lora_b"], L_AT, LK),
        "qdn": c(a["L0_ffn_w_down_q"].T), "sdn": c(a["L0_ffn_w_down_scale"].T),
        "bdn": c(a["L0_ffn_b_down"].reshape(1, D)),
        "adn": stacked(a["L0_ffn_w_down_lora_a"].T, L_AT, LK), "bdnl": stacked(a["L0_ffn_w_down_lora_b"], L_AT, LK),
        "tab": tab, "consts": consts,
    }
    nc = _bacc.Bacc("TRN2", target_bir_lowering=False, num_devices=1)
    args = [nc.dram_tensor(f"in_{k}", v.shape, _mybir.dt.from_np(v.dtype), kind="ExternalInput").ap()
            for k, v in arrays.items()]
    out = nc.dram_tensor("out_0", (B, S, D), F32, kind="ExternalOutput").ap()
    x1s = nc.dram_tensor("x1_scratch", (B, S, D), F32, kind="Internal").ap()
    decoder_kernel(nc, *args, out, x1s)
    r = _run(nc, [{f"in_{k}": v for k, v in arrays.items()}], core_ids=[0])
    return r.results[0]["out_0"]
```
